# Optimizing a Trainium2 kernel written in Bass

```python
import numpy as np
import jax
import jax.numpy as jnp

def _softmax(x, axis=-1):
    return jax.nn.softmax(x, axis=axis)

def _gelu(x):
    return jax.nn.gelu(x, approximate=True)

def _silu(x):
    return jax.nn.silu(x)

def _sigmoid(x):
    return jax.nn.sigmoid(x)

def _layernorm(x, axis=-1, eps=1e-05):
    m = jnp.mean(x, axis=axis, keepdims=True)
    v = jnp.var(x, axis=axis, keepdims=True)
    return (x - m) / jnp.sqrt(v + eps)

def _scatter_add(tgt, idx, src, axis=0):
    return tgt.at[idx].add(src)

def _segment_sum(src, seg, n):
    return jax.ops.segment_sum(src, seg, n)
kernel_name = 'mk_gps_d1_gnn_r8_79001e'

def setup_inputs(seed: int=0):
    np.random.seed(seed)
    _w = jnp.asarray

    def _rec_inputs():
        import jax
        import jax.numpy as jnp
        _gk = jax.random.key(seed)
        x = -0.0003713 + 1 * jax.random.normal(jax.random.fold_in(_gk, 1), (6250, 256), jnp.float32)
        _s = jax.random.randint(jax.random.fold_in(_gk, 2), (100000,), 0, 6250, jnp.int32)
        _d = jax.random.randint(jax.random.fold_in(_gk, 3), (100000,), 0, 6250, jnp.int32)
        _loop = jnp.arange(6250, dtype=jnp.int32)
        src = jnp.concatenate([_s, _d, _loop])
        dst = jnp.concatenate([_d, _s, _loop])
        _o = jnp.argsort(dst, stable=True)
        src = src[_o]
        dst = dst[_o]
        return (x, src, dst)
    x, src, dst = _rec_inputs()

    def _L0_gnn_setup():
        import jax, jax.numpy as jnp
        import numpy as np
        N_NODES = 6250
        N_EDGES = 200000
        IN_DIM, OUT_DIM, N_HEADS = (256, 64, 4)
        EPS = 1e-12
        key = jax.random.key(seed)
        k1, k2, k3, k4, k5 = jax.random.split(key, 5)
        h = jax.random.normal(k1, (N_NODES, IN_DIM), dtype=jnp.float32)
        edge_index = jax.random.randint(k2, (2, N_EDGES), 0, N_NODES, dtype=jnp.int32)
        W = jax.random.normal(k3, (IN_DIM, OUT_DIM), dtype=jnp.float32) * 0.05
        Wl = jax.random.normal(k4, (N_HEADS, OUT_DIM), dtype=jnp.float32) * 0.05
        Wr = jax.random.normal(k5, (N_HEADS, OUT_DIM), dtype=jnp.float32) * 0.05
        b = jnp.zeros((OUT_DIM,), dtype=jnp.float32)
        return {'h': h, 'W': W, 'Wl': Wl, 'Wr': Wr, 'b': b, 'edge_index': edge_index}
    _L0_gnn_all = _L0_gnn_setup()
    _L0_gnn_in = {k: v for k, v in _L0_gnn_all.items() if k in ('W', 'Wl', 'Wr', 'b')}
    del _L0_gnn_all

    def _L0_mix_setup():
        import jax, jax.numpy as jnp
        import numpy as np
        DIM = 256
        HEADS = 4
        DIM_HEAD = 32
        NUM_MEM = 4
        HIDDEN = HEADS * DIM_HEAD
        SCALE = DIM_HEAD ** (-0.5)

        def rmsnorm(x, g):
            n = jnp.linalg.norm(x, axis=-1, keepdims=True)
            return x / jnp.maximum(n, 1e-12) * g * x.shape[-1] ** 0.5
        key = jax.random.key(seed)
        ks = jax.random.split(key, 8)
        B, N = (4, 2048)
        return {'x': jax.random.normal(ks[0], (B, N, DIM), jnp.float32), 't': jax.random.normal(ks[1], (B,), jnp.float32), 'w_qkv': jax.random.normal(ks[2], (DIM, 3 * HIDDEN), jnp.float32) * 0.02, 'mem_kv': jax.random.normal(ks[3], (2, HEADS, DIM_HEAD, NUM_MEM), jnp.float32), 'w_out': jax.random.normal(ks[4], (HIDDEN, DIM), jnp.float32) * 0.02, 'b_out': jnp.zeros((DIM,), jnp.float32), 'g_out': jnp.ones((DIM,), jnp.float32), 'g_pre': jnp.ones((DIM,), jnp.float32)}
    _L0_mix_all = _L0_mix_setup()
    _L0_mix_in = {k: v for k, v in _L0_mix_all.items() if k in ('t', 'w_qkv', 'mem_kv', 'w_out', 'b_out', 'g_out', 'g_pre')}
    del _L0_mix_all

    def _L0_ffn_setup():
        import jax, jax.numpy as jnp
        import numpy as np
        NUM_EXPERTS = 8
        TOP_K = 2
        B, S, D = (8, 1024, 256)

        def _moe(tokens, router_w, w1, b1, w2, b2):
            N = tokens.shape[0]
            E = router_w.shape[0]
            logits = tokens.astype(jnp.float32) @ router_w.astype(jnp.float32).T
            probs = jax.nn.softmax(logits, axis=-1)
            rw, re = jax.lax.top_k(probs, TOP_K)
            if TOP_K > 1:
                rw = rw / jnp.maximum(rw.sum(-1, keepdims=True), 1e-12)
            rw = rw.astype(tokens.dtype)
            combine = jnp.zeros((N, E), tokens.dtype).at[jnp.arange(N)[:, None], re].set(rw)
            out = tokens
            for e in range(E):
                h = jax.nn.gelu(tokens @ w1[e] + b1[e], approximate=False)
                y = h @ w2[e] + b2[e]
                out = out + combine[:, e:e + 1] * y
            return out
        key = jax.random.key(seed)
        ks = jax.random.split(key, 4)
        scale = 1.0 / np.sqrt(D).astype(np.float32)
        return {'input_embeddings': jax.random.normal(ks[0], (B, S, D), jnp.float32), 'router_w': jax.random.normal(ks[1], (NUM_EXPERTS, D), jnp.float32) * scale, 'w1': jax.random.normal(ks[2], (NUM_EXPERTS, D, D), jnp.float32) * scale, 'b1': jnp.zeros((NUM_EXPERTS, D), jnp.float32), 'w2': jax.random.normal(ks[3], (NUM_EXPERTS, D, D), jnp.float32) * scale, 'b2': jnp.zeros((NUM_EXPERTS, D), jnp.float32)}
    _L0_ffn_all = _L0_ffn_setup()
    _L0_ffn_in = {k: v for k, v in _L0_ffn_all.items() if k in ('router_w', 'w1', 'b1', 'w2', 'b2')}
    del _L0_ffn_all
    return {'x': x, 'src': src, 'dst': dst, 'L0_gnn_W': _L0_gnn_in['W'], 'L0_gnn_Wl': _L0_gnn_in['Wl'], 'L0_gnn_Wr': _L0_gnn_in['Wr'], 'L0_gnn_b': _L0_gnn_in['b'], 'L0_mix_t': _L0_mix_in['t'], 'L0_mix_w_qkv': _L0_mix_in['w_qkv'], 'L0_mix_mem_kv': _L0_mix_in['mem_kv'], 'L0_mix_w_out': _L0_mix_in['w_out'], 'L0_mix_b_out': _L0_mix_in['b_out'], 'L0_mix_g_out': _L0_mix_in['g_out'], 'L0_mix_g_pre': _L0_mix_in['g_pre'], 'L0_ffn_router_w': _L0_ffn_in['router_w'], 'L0_ffn_w1': _L0_ffn_in['w1'], 'L0_ffn_b1': _L0_ffn_in['b1'], 'L0_ffn_w2': _L0_ffn_in['w2'], 'L0_ffn_b2': _L0_ffn_in['b2']}

def reference(x, src, dst, L0_gnn_W, L0_gnn_Wl, L0_gnn_Wr, L0_gnn_b, L0_mix_t, L0_mix_w_qkv, L0_mix_mem_kv, L0_mix_w_out, L0_mix_b_out, L0_mix_g_out, L0_mix_g_pre, L0_ffn_router_w, L0_ffn_w1, L0_ffn_b1, L0_ffn_w2, L0_ffn_b2):
    import jax
    import jax.numpy as jnp

    def _L0_gnn_ref(h, W, Wl, Wr, b, edge_index):
        import jax, jax.numpy as jnp
        import numpy as np
        N_NODES = 6250
        N_EDGES = 200000
        IN_DIM, OUT_DIM, N_HEADS = (256, 64, 4)
        EPS = 1e-12
        N = h.shape[0]
        H = Wl.shape[0]
        x = h @ W
        el = x @ Wl.T
        er = x @ Wr.T
        src, dst = (edge_index[0], edge_index[1])
        e = el[src] + er[dst]
        e = jnp.exp(jax.nn.leaky_relu(e, negative_slope=0.2))
        rowsum = jax.ops.segment_sum(e, src, num_segments=N)
        w = e / jnp.maximum(rowsum, EPS)[src]
        heads = [jax.ops.segment_sum(w[:, hd:hd + 1] * x[dst], src, num_segments=N) for hd in range(H)]
        out = jnp.stack(heads, axis=1)
        out = jax.nn.elu(out + b)
        return out.reshape(N, H * x.shape[1])

    def _L0_mix_ref(x, t, w_qkv, mem_kv, w_out, b_out, g_out, g_pre):
        import jax, jax.numpy as jnp
        import numpy as np
        DIM = 256
        HEADS = 4
        DIM_HEAD = 32
        NUM_MEM = 4
        HIDDEN = HEADS * DIM_HEAD
        SCALE = DIM_HEAD ** (-0.5)

        def rmsnorm(x, g):
            n = jnp.linalg.norm(x, axis=-1, keepdims=True)
            return x / jnp.maximum(n, 1e-12) * g * x.shape[-1] ** 0.5
        b, n, c = x.shape
        xn = rmsnorm(x, g_pre)
        qkv = xn @ w_qkv
        q, k, v = jnp.split(qkv, 3, axis=-1)

        def to_heads(z):
            return z.reshape(b, n, HEADS, DIM_HEAD).transpose(0, 2, 3, 1)
        q, k, v = map(to_heads, (q, k, v))
        mk = jnp.broadcast_to(mem_kv[0], (b, HEADS, DIM_HEAD, NUM_MEM))
        mv = jnp.broadcast_to(mem_kv[1], (b, HEADS, DIM_HEAD, NUM_MEM))
        k = jnp.concatenate([mk, k], axis=-1)
        v = jnp.concatenate([mv, v], axis=-1)
        q = jax.nn.softmax(q, axis=-2) * SCALE
        k = jax.nn.softmax(k, axis=-1)
        context = jnp.einsum('bhdn,bhen->bhde', k, v)
        out = jnp.einsum('bhde,bhdn->bhen', context, q)
        out = out.transpose(0, 3, 1, 2).reshape(b, n, HIDDEN)
        out = rmsnorm(out @ w_out + b_out, g_out)
        return out + x

    def _L0_ffn_ref(input_embeddings, router_w, w1, b1, w2, b2):
        import jax, jax.numpy as jnp
        import numpy as np
        NUM_EXPERTS = 8
        TOP_K = 2
        B, S, D = (8, 1024, 256)

        def _moe(tokens, router_w, w1, b1, w2, b2):
            N = tokens.shape[0]
            E = router_w.shape[0]
            logits = tokens.astype(jnp.float32) @ router_w.astype(jnp.float32).T
            probs = jax.nn.softmax(logits, axis=-1)
            rw, re = jax.lax.top_k(probs, TOP_K)
            if TOP_K > 1:
                rw = rw / jnp.maximum(rw.sum(-1, keepdims=True), 1e-12)
            rw = rw.astype(tokens.dtype)
            combine = jnp.zeros((N, E), tokens.dtype).at[jnp.arange(N)[:, None], re].set(rw)
            out = tokens
            for e in range(E):
                h = jax.nn.gelu(tokens @ w1[e] + b1[e], approximate=False)
                y = h @ w2[e] + b2[e]
                out = out + combine[:, e:e + 1] * y
            return out
        b, s, d = input_embeddings.shape
        tokens = input_embeddings.reshape(b * s, d)
        return _moe(tokens, router_w, w1, b1, w2, b2).reshape(b, s, d)
    edge_index = jnp.stack([src, dst])
    xn = _layernorm(x, axis=-1)
    x = x + _L0_gnn_ref(xn, L0_gnn_W, L0_gnn_Wl, L0_gnn_Wr, L0_gnn_b, edge_index) + _L0_mix_ref(xn[None], L0_mix_t, L0_mix_w_qkv, L0_mix_mem_kv, L0_mix_w_out, L0_mix_b_out, L0_mix_g_out, L0_mix_g_pre)[0]
    x = x + _L0_ffn_ref(_layernorm(x, axis=-1)[None], L0_ffn_router_w, L0_ffn_w1, L0_ffn_b1, L0_ffn_w2, L0_ffn_b2)[0]
    return x

_drawn_inputs = setup_inputs


def setup_inputs(seed=0):
    import zlib

    import numpy as np

    out = dict(_drawn_inputs(seed))
    spreads = {'L0_gnn_b': (0.0, 0.1),
     'L0_mix_b_out': (0.0, 0.1),
     'L0_mix_g_out': (1.0, 0.2),
     'L0_mix_g_pre': (1.0, 0.6),
     'L0_ffn_b1': (0.0, 0.523),
     'L0_ffn_b2': (0.0, 0.354)}
    factors = {'L0_gnn_Wl': 5.714, 'L0_mix_w_qkv': 8.0, 'L0_mix_mem_kv': 8.0, 'L0_mix_w_out': 8.0}
    for name, (base, spread) in spreads.items():
        noise = np.random.default_rng([zlib.crc32(name.encode()), seed]).standard_normal(out[name].shape)
        drawn = base * np.exp(spread * noise) if base else spread * noise
        out[name] = jnp.asarray(drawn.astype(out[name].dtype))
    for name, factor in factors.items():
        out[name] = (out[name] * factor).astype(out[name].dtype)
    return out
```

```python
import concourse.bass as bass
from concourse import mybir
from contextlib import ExitStack

ALU = mybir.AluOpType
ACT = mybir.ActivationFunctionType
AX = mybir.AxisListType
F32 = mybir.dt.float32
I32 = mybir.dt.int32
U32 = mybir.dt.uint32

P = 128
LN_EPS = 1e-5
TINY = 1e-12

ROW_BITS = 7
NODE_BITS = 13
PAD_NODE = (1 << NODE_BITS) - 1
KEY_BASE = 0x20000000


def make_plan(levels):
    plan = []
    for k in range(1, ROW_BITS + 1):
        plan += [("plain", "A", k, j) for j in range(k - 1, -1, -1)]
    for k in range(ROW_BITS + 1, levels + 1):
        plan.append(("enter", "B", k, k - 1))
        plan += [("plain", "B", k, j) for j in range(k - 2, ROW_BITS - 1, -1)]
        plan.append(("enter", "A", k, ROW_BITS - 1))
        plan += [("plain", "A", k, j) for j in range(ROW_BITS - 2, -1, -1)]
    return plan


def inner(x, w, part):
    v = x[:, part[0]:part[1], :].rearrange("p t (g b l) -> p (t g) b l", b=2, l=w)
    return v[:, :, 0, :], v[:, :, 1, :]


def directed(x, w, a, d, part):
    v = x[:, part[0]:part[1], :].rearrange("p t (g d a b l) -> p (t g) d a b l", d=2, a=a, b=2, l=w)
    return v[:, :, d, :, 0, :], v[:, :, d, :, 1, :]


def outer(x, u, nb):
    n = nb // (2 * u) * (2 * u)
    pairs = []
    if n:
        v = x[:, 0:n, :].rearrange("p (q b u) m -> p q b (u m)", b=2, u=u)
        pairs.append((v[:, :, 0, :], v[:, :, 1, :]))
    left = nb - n - u
    if left > 0:
        pairs.append((x[:, n:n + left, :], x[:, n + u:nb, :]))
        return pairs, (n + left, n + u)
    return pairs, (n, nb)


def enter_pairs(k, part, nb):
    top = ROW_BITS * 2
    if k < top:
        return [(lambda x, d=d: directed(x, 1 << (k - ROW_BITS - 1), 1, d, part), 2 * d - 1) for d in range(2)], None
    if k == top:
        last = nb - 1
        end = min(part[1], last)
        res = []
        for d in range(2):
            first = part[0] + (part[0] + d) % 2
            res.append((lambda x, s=first: tuple(x[:, s:end:2, c * 64:c * 64 + 64] for c in range(2)), 2 * d - 1))
        if part[1] == nb:
            res.append((lambda x: tuple(x[:, last:nb, c * 64:c * 64 + 64] for c in range(2)), 1))
        return res, None
    if k == top + 1:
        def pick(x, d):
            v = x[:, 0:12, :].rearrange("p (q d b) m -> p q d b m", d=2, b=2)
            return v[:, :, d, 0, :], v[:, :, d, 1, :]
        return [(lambda x, d=d: pick(x, d), 2 * d - 1) for d in range(2)], (12, 13, 1)
    if k == top + 2:
        return [(lambda x, q=q: (x[:, 4 * q:4 * q + 2, :], x[:, 4 * q + 2:4 * q + 4, :]), 1 if q == 1 else -1)
                for q in range(3)], (12, 13, 1)
    if k == top + 3:
        return [(lambda x: (x[:, 0:4, :], x[:, 4:8, :]), -1), (lambda x: (x[:, 8:9, :], x[:, 12:13, :]), 1)], (9, 12, -1)
    return [(lambda x: (x[:, 0:5, :], x[:, 8:13, :]), 1)], (5, 8, -1)


def run(eng, n, unroll, head, body):
    end = head + (n - head) // unroll * unroll
    for i in range(head):
        body(i, i % unroll)
    if end > head:
        with eng.Fori(0, (end - head) // unroll) as turn:
            for u in range(unroll):
                body(turn * unroll + (head + u), (head + u) % unroll)
    for i in range(end, n):
        body(i, i % unroll)


def after(eng, sem, i, lag, per=1):
    if isinstance(i, int) and i < lag:
        return
    eng.wait_ge(sem, (i - lag + 1) * per)


def bcast(ap, axis, n):
    v = ap.unsqueeze(axis)
    shape = list(v.shape)
    shape[axis] = n
    return v.broadcast_to(shape)


def gps_layer(nc, x, src, dst, W, Wl, Wr, gnn_b, w_qkv, mem_kv, w_out, b_out, g_out, g_pre,
              router_w, w1, b1, w2, b2, out):
    N, D = x.shape
    E = src.shape[0]
    HD, C = Wl.shape
    _, MH, MD, MEM = mem_kv.shape
    HID = MH * MD
    NE, _, F = w1.shape
    T = -(-N // P)
    TAIL = N - (T - 1) * P
    SCALE = float(MD) ** -0.5
    KC = D // P
    TS = 7
    NS = T // TS
    HALFT = TS * P // 2
    assert T == TS * NS and HID == P and D == HD * C and F == D

    BLK = P * P
    NB = -(-E // BLK)
    LEVELS = (NB * BLK - 1).bit_length()
    assert NB == 13 and LEVELS == 18 and N <= PAD_NODE
    FULL = (NB - 1) * BLK
    ROWS = (E - FULL) // P
    REST = E - FULL - ROWS * P
    HALVES = ((0, 8), (8, NB))

    GT = 4
    GE = GT * P
    RING = 4
    NG = -(-((E + T * (GE - 1)) // GE) // RING) * RING
    GW = C + HD
    RW = D + HD
    assert NG % RING == 0 and (NB * BLK - E) >= GE

    plan = make_plan(LEVELS)
    enters = [(n, s) for n, s in enumerate(plan) if s[0] == "enter"]

    table_d = nc.dram_tensor("gather_table", (T * P, GW), F32).ap()
    sorted_d = nc.dram_tensor("sorted_edges", (NB * BLK * 2,), F32).ap()
    groups_d = nc.dram_tensor("group_table", (P * GT, 2), I32).ap()
    bases_d = nc.dram_tensor("group_bases", (P * GT,), F32).ap()

    with ExitStack() as ctx:
        def sb(name, shape, dt=F32):
            return ctx.enter_context(nc.sbuf_tensor(name, shape, dt))

        def sem(name):
            return ctx.enter_context(nc.semaphore(name))

        ps = ctx.enter_context(nc.psum_tensor("ps", [P, 8, 512], F32))

        ident = sb("ident", [P, P])
        ones = sb("ones", [P, P])
        lane = sb("lane", [P, P])
        lane_i = sb("lane_i", [P, P], I32)
        row_i = sb("row_i", [P, 1], I32)
        rowf = sb("rowf", [P, 1])
        sign7 = sb("sign7", [P, 1])
        eps_t = sb("eps_t", [P, 1])
        base = sb("base", [P, T, D])
        mv = sb("mv", [P, T, 2])
        rstd = sb("rstd", [P, T])
        nmr = sb("nmr", [P, T])
        rsc = sb("rsc", [P, T])
        tmpT = sb("tmpT", [P, T])
        el_all = sb("el_all", [P, T, HD + 1])
        big = sb("big", [P, T * RW])
        kv = big[:, 0:T * 2 * HID].rearrange("p (t c) -> p t c", t=T)
        att = big[:, 0:T * D].rearrange("p (t c) -> p t c", t=T)
        acc = big[:, :].rearrange("p (t c) -> p t c", t=T)

        n_sort = NB * P
        A_Q, A_TB = 0, T * HID
        A_E = A_TB + T * GW
        A_K = A_E + 2 * n_sort
        A_END1 = A_K + 3 * n_sort
        A_W1, A_W2 = 0, NE * KC * F
        A_Y = A_W2 + NE * KC * D
        A_H = A_Y + 2 * KC * TS * P
        A_X = A_H + 2 * KC * TS * P
        A_END2 = A_X + 2 * TS * D
        A_G = A_Y
        assert A_G + RING * GT * GW + 2 * GT * (2 * P + RW) <= A_END2
        arena = sb("arena", [P, max(A_END1, A_END2)])
        q_all = arena[:, A_Q:A_TB].rearrange("p (t c) -> p t c", t=T)
        tb = arena[:, A_TB:A_E].rearrange("p (t c) -> p t c", t=T)
        src_i = arena[:, A_E:A_E + n_sort].bitcast(I32).rearrange("p (t l) -> p t l", t=NB)
        dst_i = arena[:, A_E + n_sort:A_K].bitcast(I32).rearrange("p (t l) -> p t l", t=NB)
        pair = arena[:, A_E:A_K].rearrange("p (t l c) -> p t l c", t=NB, c=2)
        keys = [arena[:, A_K + i * n_sort:A_K + (i + 1) * n_sort].rearrange("p (t l) -> p t l", t=NB) for i in range(2)]
        right = arena[:, A_K + 2 * n_sort:A_END1].rearrange("p (t l) -> p t l", t=NB)
        w1_s = arena[:, A_W1:A_W2].rearrange("p (e k f) -> p e k f", e=NE, k=KC)
        w2_s = arena[:, A_W2:A_Y].rearrange("p (e k f) -> p e k f", e=NE, k=KC)
        yT = [arena[:, A_Y + i * KC * TS * P:A_Y + (i + 1) * KC * TS * P].rearrange("p (k n) -> p k n", k=KC) for i in range(2)]
        hT = [arena[:, A_H + i * KC * TS * P:A_H + (i + 1) * KC * TS * P].rearrange("p (k n) -> p k n", k=KC) for i in range(2)]
        low = arena[:, A_X:A_X + TS * D].rearrange("p (t c) -> p t c", t=TS)
        mid = arena[:, A_X + TS * D:A_END2].rearrange("p (t c) -> p t c", t=TS)

        spare = arena[:, A_END1:A_END2]
        stats = spare[:, 0:T * 6].rearrange("p (t s) -> p t s", t=T)
        wT = spare[0:C, T * 6:T * 6 + KC * P].rearrange("p (k n) -> p k n", k=KC)
        b1_r = spare[0:NE * KC, T * 6 + KC * P:T * 6 + (KC + 1) * P]
        gpre_r = spare[0:KC, T * 6 + (KC + 1) * P:T * 6 + (KC + 2) * P]

        wcat = sb("wcat", [P, KC, GW + HD + 3 * HID])
        CQ = GW + HD
        wlr = sb("wlr", [2 * HD, C])
        wlrT = sb("wlrT", [C, 2 * HD])
        gpre_t = sb("gpre_t", [P, KC])
        wout_s = sb("wout_s", [P, D])
        rows_b = sb("rows_b", [P, 2, D])
        gnnb_t = sb("gnnb_t", [P, C])
        mk_t = sb("mk_t", [P, 2, MEM])
        rw_s = sb("rw_s", [NE, D])
        rwT = sb("rwT", [P, KC, NE])
        b1_t = sb("b1_t", [P, NE, KC])
        b2_s = sb("b2_s", [NE, D])

        xn = [sb(f"xn{i}", [P, D]) for i in range(2)]
        xnT = [sb(f"xnT{i}", [P, KC, P]) for i in range(2)]
        kmx = sb("kmx", [P, 4])
        kmaxp = sb("kmaxp", [P, P])
        kdiag, kmaxb = xn[1][:, 0:P], xn[1][:, P:2 * P]
        mexp = sb("mexp", [P, MEM])
        memT = sb("memT", [MEM, 2, P])
        ctxm = sb("ctxm", [P, P])
        mixw = sb("mixw", [P, D])
        qst = sb("qst", [P, 2, T * MH])
        qT = xnT[0][:, 0, :], xnT[1][:, 0, :]
        sq = xn[0]
        ss = sb("ss", [P, T])
        cnt = sb("cnt", [P, T])
        starts = sb("starts", [P, T + 1])
        gtab = sb("gtab", [P, 4, T])
        gsel = sb("gsel", [P, GT, T])
        gidx = sb("gidx", [P, GT])
        gsum = sb("gsum", [P, 4, GT])
        gout = sb("gout", [P, GT, 2], I32)
        nthr = sb("nthr", [P, T])
        trow = sb("trow", [1, P * GT * 2], I32)
        bases = sb("bases", [P, P * GT])
        kd = [sb(f"kd{i}", [P, GT, 2]) for i in range(RING)]

        def ring(start, n, width):
            return [arena[:, start + i * GT * width:start + (i + 1) * GT * width].rearrange("p (c w) -> p c w", c=GT) for i in range(n)]
        gat = ring(A_G, RING, GW)
        hot = ring(A_G + RING * GT * GW, 2, P)
        hotT = ring(A_G + RING * GT * GW + 2 * GT * P, 2, P)
        wx = ring(A_G + RING * GT * GW + 4 * GT * P, 2, RW)
        loc = [sb(f"loc{i}", [P, GT]) for i in range(2)]
        zed = [sb(f"zed{i}", [P, 3, GT * HD]) for i in range(2)]
        den = sb("den", [P, 2, TS * HD])
        st2 = sb("st2", [P, TS, 6])
        mv2 = sb("mv2", [P, TS, 2])
        ln2 = sb("ln2", [P, 3, TS])
        rt = sb("rt", [P, 6, TS * NE])
        top = sb("top", [P, TS, 8])
        topi = sb("topi", [P, TS, 8], U32)
        topf = sb("topf", [P, TS, 8])
        rs = sb("rs", [P, 4, TS])
        comb = [sb(f"comb{i}", [P, TS, NE]) for i in range(2)]
        combT = arena[0:NE, A_X:A_X + TS * P].rearrange("p (t n) -> p t n", t=TS)

        turned = ps[:, 0:4, :].rearrange("p a (b m) -> p (a b) m", m=P)[:, 0:NB, :]

        s_const = sem("s_const")
        s_pad = sem("s_pad")
        s_w = sem("s_w")
        s_xl = sem("s_xl")
        s_edges = sem("s_edges")
        s_step = sem("s_step")
        s_once = sem("s_once")
        s_aonce = sem("s_aonce")
        s_xn = sem("s_xn")
        s_xTp = sem("s_xTp")
        s_xT = sem("s_xT")
        s_proj = sem("s_proj")
        s_q = sem("s_q")
        s_kv = sem("s_kv")
        s_base = sem("s_base")
        s_tab = sem("s_tab")
        s_ksub = sem("s_ksub")
        s_kexp = sem("s_kexp")
        s_qTp = sem("s_qTp")
        s_qT = sem("s_qT")
        s_mixp = sem("s_mixp")
        s_arow = sem("s_arow")
        s_afin = sem("s_afin")
        s_key = sem("s_key")
        s_cnt = sem("s_cnt")
        s_turned = sem("s_turned")
        s_right = sem("s_right")
        s_gtd = sem("s_gtd")
        s_row = sem("s_row")
        s_srt = sem("s_srt")
        s_zero = sem("s_zero")
        s_kd = [sem(f"s_kd{i}") for i in range(RING)]
        s_gat = [sem(f"s_gat{i}") for i in range(RING)]
        s_loc = sem("s_loc")
        s_hot = sem("s_hot")
        s_hTp = sem("s_hTp")
        s_hT = sem("s_hT")
        s_el = sem("s_el")
        s_z = sem("s_z")
        s_e = sem("s_e")
        s_wx = sem("s_wx")
        s_agg = sem("s_agg")
        s_acc = sem("s_acc")
        s_ew = sem("s_ew")
        s_pd = sem("s_pd")
        s_pa = sem("s_pa")
        s_pp = sem("s_pp")
        s_yin = sem("s_yin")
        s_carry = sem("s_carry")
        s_carry_pool = sem("s_carry_pool")
        s_h = sem("s_h")
        s_g = sem("s_g")
        s_y = sem("s_y")
        s_moe = sem("s_moe")
        s_out = [sem("s_out0"), sem("s_out1")]
        block = ctx.enter_context(nc.Block())

        at = {}

        def sl(i, n=1):
            return slice(i, i + n) if isinstance(i, int) else bass.ds(i, n)

        NW = 16
        PD = ["den", "rden", "avg", "bias", "neg", "elu", "x2", "stats", "mv", "rstd", "nmr", "lmax", "lsub", "lsum",
              "lrec", "prob", "top", "topi", "topf", "psum", "pmax", "prec", "w", "eq1", "c1", "eq2", "c2", "comb"] + [f"b2{u}" for u in range(4)]
        PA = ["eexp", "sd", "y"] + [f"yT{t}" for t in range(TS)] + ["lexp", "cTa", "cTb"]
        PP = [f"yTp{t}" for t in range(TS)] + ["logits", "cTpa", "cTpb"] + [f"b2p{u}" for u in range(4)]

        def count(names, st, name):
            return st * len(names) + names.index(name) + 1

        UNITS = [(0, 2), (2, 4), (4, 6), (6, 7)]
        NU = len(UNITS)

        def gathered(g, u):
            return (g - u) * (16 * GT // RING) + 16 * GT

        def loaded(g, u):
            return (g - u) * (16 // RING) + 16

        @block.vector
        def _(dve):
            n = [0]

            def step(ins, name=None):
                ins.then_inc(s_step, 1)
                n[0] += 1
                if name:
                    at[name] = n[0]
                dve.wait_ge(s_step, n[0])

            dve.wait_ge(s_const, 4)
            step(dve.memset(eps_t[:, :], LN_EPS))
            step(dve.memset(ctxm[:, :], 0.0))
            step(dve.tensor_copy(lane[:, :], lane_i[:, :]))
            step(dve.tensor_scalar(nthr[:, :], lane[:, 0:T], -float(P), 0.5, ALU.mult, ALU.add))
            step(dve.tensor_reduce(sign7[:, :], ident[:, :].rearrange("p (a b) -> p a b", b=2)[:, :, 1], AX.X, ALU.add))
            step(dve.tensor_scalar(sign7[:, :], sign7[:, :], 2.0, -1.0, ALU.mult, ALU.add))
            step(dve.memset(el_all[:, :, HD:HD + 1], 1e30), "const")

            dve.wait_ge(s_once, 1)
            small = ps[:, 4, :]
            dve.tensor_copy(wT[:, :, :], small[0:C, 0:KC * P].rearrange("p (k n) -> p k n", k=KC))
            dve.tensor_copy(wlrT[:, :], small[0:C, KC * P:KC * P + 2 * HD])
            o = KC * P + 2 * HD
            dve.tensor_copy(rwT[:, :, :], small[:, o:o + KC * NE].rearrange("p (k e) -> p k e", k=KC))
            o += KC * NE
            dve.tensor_copy(b1_t[:, :, :], small[:, o:o + NE * KC].rearrange("p (e k) -> p e k", k=KC))
            o += NE * KC
            step(dve.tensor_copy(gpre_t[:, :], small[:, o:o + KC]), "small")
            for k in range(KC):
                step(dve.tensor_scalar(wcat[:, k, CQ:], wcat[:, k, CQ:], gpre_t[:, k:k + 1], None, ALU.mult))
            dve.wait_ge(s_once, 2)
            step(dve.tensor_copy(wcat[:, :, C:CQ], ps[:, 5, 0:KC * 2 * HD].rearrange("p (k h) -> p k h", k=KC)), "wcat")

            dve.wait_ge(s_xl, 16 * 5)
            for t in range(T):
                ins = dve.bn_stats(stats[:, t, :], base[:, t, :])
            step(ins)
            for t in range(T):
                ins = dve.bn_aggr(mv[:, t, :], stats[:, t, :])
            step(ins, "mv")
            dve.wait_ge(s_aonce, 1)
            step(dve.reciprocal(rstd[:, :], tmpT[:, :]))
            step(dve.scalar_tensor_tensor(out=nmr[:, :], in0=mv[:, :, 0], scalar=-1.0, in1=rstd[:, :], op0=ALU.mult, op1=ALU.mult), "nmr")
            step(dve.tensor_tensor(tmpT[:, :], mv[:, :, 1], rstd[:, :], ALU.mult))
            step(dve.tensor_tensor(tmpT[:, :], tmpT[:, :], rstd[:, :], ALU.mult), "norm2")
            dve.wait_ge(s_aonce, 2)
            step(dve.tensor_scalar(tmpT[:, :], tmpT[:, :], TINY, None, ALU.max))
            step(dve.reciprocal(rsc[:, :], tmpT[:, :]))
            step(dve.tensor_scalar(rsc[:, :], rsc[:, :], float(D) ** 0.5, None, ALU.mult), "rsc")

            def copy_xT(i, u):
                dve.wait_ge(s_xTp, i + 1)
                after(dve, s_proj, i, 2)
                dve.tensor_copy(xnT[u][:, :, :], ps[:, 4 + u, 0:D].rearrange("p (k n) -> p k n", k=KC)).then_inc(s_xT, 1)

            def store_q(i, u):
                dve.wait_ge(s_proj, i + 1)
                dve.tensor_copy(tb[:, sl(i), :], ps[:, 6 + u:7 + u, 0:GW])
                dve.tensor_copy(el_all[:, sl(i), 0:HD], ps[:, 6 + u:7 + u, GW:CQ])
                dve.tensor_scalar(q_all[:, sl(i), :], ps[:, 6 + u:7 + u, CQ:CQ + HID], rsc[:, sl(i)], None, ALU.mult).then_inc(s_q, 1)

            def project(i, u):
                copy_xT(i, u)
                if not (isinstance(i, int) and i == 0):
                    store_q(i - 1, 1 - u)
            run(dve, T, 2, 2, project)
            store_q(T - 1, (T - 1) % 2)

            dve.wait_ge(s_kv, T)
            dve.wait_ge(s_q, T)
            step(dve.tensor_reduce(kmaxp[:, :], kv[:, 0:T - 1, 0:HID].rearrange("p t c -> p c t"), AX.X, ALU.max))
            step(dve.tensor_tensor(kmaxp[0:TAIL, :], kmaxp[0:TAIL, :], kv[0:TAIL, T - 1, 0:HID], ALU.max), "kmaxp")
            dve.wait_ge(s_once, 3)
            step(dve.tensor_reduce(kmx[:, 0:1], ps[:, 0, 0:P], AX.X, ALU.max))
            step(dve.tensor_reduce(kmx[:, 1:2], mk_t[:, 0, :], AX.X, ALU.max))
            step(dve.tensor_tensor(kmx[:, 0:1], kmx[:, 0:1], kmx[:, 1:2], ALU.max))
            step(dve.tensor_scalar(kmx[:, 2:3], kmx[:, 0:1], -1.0, None, ALU.mult), "nkmx")
            dve.wait_ge(s_base, T)
            step(dve.tensor_scalar(kdiag[:, :], ident[:, :], kmx[:, 0:1], None, ALU.mult), "kdiag")
            dve.wait_ge(s_once, 4)
            step(dve.tensor_copy(kmaxb[:, :], ps[:, 1, 0:P]))
            for c in range(NS):
                kc = kv[:, TS * c:TS * c + TS, 0:HID]
                dve.tensor_tensor(kc, kc, bcast(kmaxb[:, :], 1, TS), ALU.subtract).then_inc(s_ksub, 1)
            q4 = q_all[:, :, :].rearrange("p t (h d) -> p (t h) d", h=MH)
            step(dve.tensor_reduce(qst[:, 0, :], q4, AX.X, ALU.max))
            step(dve.tensor_tensor(q4, q4, bcast(qst[:, 0, :], 2, MD), ALU.subtract), "qsub")
            dve.wait_ge(s_aonce, 4)
            step(dve.tensor_reduce(qst[:, 0, :], q4, AX.X, ALU.add))
            step(dve.reciprocal(qst[:, 1, :], qst[:, 0, :]))
            step(dve.tensor_tensor(q4, q4, bcast(qst[:, 1, :], 2, MD), ALU.mult), "q")
            dve.wait_ge(s_once, 5)
            step(dve.tensor_copy(memT[:, :, :], ps[0:MEM, 2, 0:2 * P].rearrange("p (a n) -> p a n", a=2)), "memT")
            dve.wait_ge(s_once, 6)
            for h in range(MH):
                r = slice(h * MD, h * MD + MD)
                ins = dve.tensor_scalar(ctxm[r, r], ps[r, 3, r], SCALE, None, ALU.mult)
            step(ins)
            step(dve.reciprocal(kmx[:, 3:4], ps[:, 4, 0:1]), "ctxm")
            dve.wait_ge(s_once, 7)
            step(dve.tensor_scalar(mixw[:, :], ps[:, 5, 0:D], kmx[:, 3:4], None, ALU.mult), "mixw")

            def att_row(i, u):
                dve.wait_ge(s_mixp, i + 1)
                dve.tensor_tensor(att[:, sl(i), :], ps[:, u:u + 1, 0:D], rows_b[:, 0:1, :], ALU.add).then_inc(s_arow, 1)
            run(dve, T, 2, 2, att_row)
            dve.wait_ge(s_arow, T)
            for t in range(T):
                if t:
                    dve.wait_ge(s_step, n[0])
                ins = dve.tensor_tensor_reduce(sq[:, :], att[:, t, :], att[:, t, :], 1.0, 0.0, ALU.mult, ALU.add, ss[:, t:t + 1])
                ins.then_inc(s_step, 1)
                n[0] += 1
            at["ss"] = n[0]
            dve.wait_ge(s_aonce, 5)
            step(dve.tensor_scalar(ss[:, :], ss[:, :], TINY, None, ALU.max))
            step(dve.reciprocal(tmpT[:, :], ss[:, :]))
            step(dve.tensor_scalar(tmpT[:, :], tmpT[:, :], float(D) ** 0.5, None, ALU.mult))

            def scale_row(i, u):
                dve.scalar_tensor_tensor(out=att[:, sl(i), :], in0=att[:, sl(i), :], scalar=tmpT[:, sl(i)],
                                         in1=rows_b[:, 1:2, :], op0=ALU.mult, op1=ALU.mult).then_inc(s_afin, 1)
            run(dve, T, 7, 0, scale_row)
            dve.wait_ge(s_afin, T)
            dve.wait_ge(s_base, T)
            step(dve.tensor_tensor(base[:, :, :], base[:, :, :], att, ALU.add), "att")

            dve.wait_ge(s_edges, 96)
            step(dve.tensor_scalar(right.bitcast(I32), src_i, NODE_BITS, KEY_BASE, ALU.logical_shift_left, ALU.bitwise_or))
            dve.tensor_tensor(keys[0].bitcast(I32), right.bitcast(I32), dst_i, ALU.bitwise_or).then_inc(s_key, 1)
            m, cur, done, entries = 1, 0, [1, 1], 0
            for kind, side, k, j in plan:
                a, b = keys[cur], keys[1 - cur]
                if (k, j) == (ROW_BITS, ROW_BITS - 1):
                    dve.wait_ge(s_key, m)
                    dve.tensor_scalar(b, a, sign7[:, 0:1], None, ALU.mult).then_inc(s_key, 1)
                    m += 1
                    done, cur = [m, m], 1 - cur
                    a, b = b, a
                if kind == "plain" and j >= 2 * ROW_BITS:
                    dve.wait_ge(s_key, m)
                    reads, lone = outer(a, 1 << (j - 2 * ROW_BITS), NB)
                    for (al, ah), (bl, bh) in zip(reads, outer(b, 1 << (j - 2 * ROW_BITS), NB)[0]):
                        dve.tensor_tensor(bl, al, ah, ALU.min).then_inc(s_key, 1)
                        dve.tensor_tensor(bh, al, ah, ALU.max).then_inc(s_key, 1)
                        m += 2
                    dve.tensor_copy(b[:, lone[0]:lone[1], :], a[:, lone[0]:lone[1], :]).then_inc(s_key, 1)
                    m += 1
                    done = [m, m]
                elif kind == "plain":
                    w = 1 << (j if side == "A" else j - ROW_BITS)
                    for h, part in enumerate(HALVES):
                        dve.wait_ge(s_key, done[h])
                        if side == "A" and k < ROW_BITS:
                            views = [(directed(a, w, 1 << (k - 1 - j), d, part), directed(b, w, 1 << (k - 1 - j), d, part), d) for d in range(2)]
                        else:
                            views = [(inner(a, w, part), inner(b, w, part), 1)]
                        for (al, ah), (bl, bh), up in views:
                            dve.tensor_tensor(bl, al, ah, ALU.min if up else ALU.max).then_inc(s_key, 1)
                            dve.tensor_tensor(bh, al, ah, ALU.max if up else ALU.min).then_inc(s_key, 1)
                            m += 2
                        done[h] = m
                else:
                    parts = ((0, NB),) if side == "B" and k > 2 * ROW_BITS else HALVES
                    for h, part in enumerate(parts):
                        entries += 1
                        dve.wait_ge(s_right, entries)
                        pairs, lone = enter_pairs(k, part, NB) if side == "B" else ([(lambda v: inner(v, P // 2, part), 0)], None)
                        for pick, sign in pairs:
                            left, rite, (bl, bh) = pick(turned)[0], pick(right)[1], pick(b)
                            for o_, op in ((bl, ALU.min), (bh, ALU.max)):
                                if sign == 0:
                                    dve.tensor_tensor(o_, left, rite, op).then_inc(s_key, 1)
                                else:
                                    x0, x1 = (left, rite) if sign > 0 else (rite, left)
                                    dve.scalar_tensor_tensor(out=o_, in0=x0, scalar=-1.0, in1=x1, op0=ALU.mult, op1=op).then_inc(s_key, 1)
                                m += 1
                        if lone:
                            dve.tensor_scalar(b[:, lone[0]:lone[1], :], turned[:, lone[0]:lone[1], :], float(lone[2]), None, ALU.mult).then_inc(s_key, 1)
                            m += 1
                        done[h] = m
                    if len(parts) == 1:
                        done = [m, m]
                cur = 1 - cur
                at[(kind, side, k, j)] = (list(done), cur)

            dve.wait_ge(s_once, 8)
            step(dve.tensor_scalar(starts[:, 0:T], ps[:, 5, 0:T], -0.5, NB * BLK * 0.5, ALU.mult, ALU.add))
            step(dve.memset(starts[:, T:T + 1], float(E)))
            step(dve.tensor_tensor(gtab[:, 0, :], starts[:, 1:T + 1], starts[:, 0:T], ALU.subtract))
            step(dve.tensor_scalar(gtab[:, 1, :], gtab[:, 0, :], float(GE - 1), None, ALU.add))
            step(dve.tensor_copy(gtab[:, 2, :].bitcast(I32), gtab[:, 1, :]))
            step(dve.tensor_scalar(gtab[:, 3, :].bitcast(I32), gtab[:, 2, :].bitcast(I32), GE.bit_length() - 1, None, ALU.logical_shift_right))
            step(dve.tensor_copy(gtab[:, 1, :], gtab[:, 3, :].bitcast(I32)))
            step(dve.tensor_tensor_scan(gtab[:, 2, :], ones[:, 0:T], gtab[:, 1, :], 0.0, ALU.mult, ALU.add))
            step(dve.tensor_copy(rowf[:, :], row_i[:, :]))
            step(dve.tensor_scalar(gidx[:, :], lane[:, 0:GT], rowf[:, 0:1], None, ALU.add))
            before = gsel[:, :, :]
            step(dve.tensor_tensor(before, bcast(gtab[:, 2, :], 1, GT), bcast(gidx[:, :], 2, T), ALU.is_le))
            step(dve.tensor_reduce(gsum[:, 0, :], before, AX.X, ALU.add))
            step(dve.tensor_tensor(before, before, bcast(gtab[:, 1, :], 1, GT), ALU.mult))
            step(dve.tensor_reduce(gsum[:, 1, :], before, AX.X, ALU.add))
            step(dve.tensor_tensor(before, bcast(gtab[:, 2, :], 1, GT), bcast(gidx[:, :], 2, T), ALU.is_le))
            step(dve.tensor_tensor(before, before, bcast(gtab[:, 0, :], 1, GT), ALU.mult))
            step(dve.tensor_reduce(gsum[:, 2, :], before, AX.X, ALU.add))
            step(dve.tensor_tensor(gidx[:, :], gidx[:, :], gsum[:, 1, :], ALU.subtract))
            step(dve.scalar_tensor_tensor(out=gsum[:, 2, :], in0=gidx[:, :], scalar=float(GE), in1=gsum[:, 2, :], op0=ALU.mult, op1=ALU.add))
            step(dve.tensor_scalar(gsum[:, 2, :], gsum[:, 2, :], float(E), 2.0, ALU.min, ALU.mult))
            step(dve.tensor_scalar(gsum[:, 0, :], gsum[:, 0, :], float(T - 1), None, ALU.min))
            step(dve.tensor_copy(gout[:, :, 0], gsum[:, 2, :]))
            step(dve.tensor_copy(gout[:, :, 1], gsum[:, 0, :]))
            step(dve.tensor_scalar(gsum[:, 3, :], gsum[:, 0, :], float(P), None, ALU.mult), "groups")

            dve.wait_ge(s_key, m)
            dve.wait_ge(s_cnt, T)
            res, tmp = keys[cur], keys[1 - cur]
            step(dve.tensor_scalar(tmp.bitcast(I32), res.bitcast(I32), NODE_BITS, PAD_NODE, ALU.logical_shift_right, ALU.bitwise_and))
            step(dve.tensor_scalar(pair[:, :, :, 1].bitcast(I32), res.bitcast(I32), PAD_NODE, None, ALU.bitwise_and))
            step(dve.tensor_copy(pair[:, :, :, 0], tmp.bitcast(I32)), "pair")

            dve.wait_ge(s_zero, 1)
            dve.wait_ge(s_row, 32)

            def logits(g, u):
                par = u % 2
                dve.wait_ge(s_el, g + 1)
                dve.wait_ge(s_gat[u], gathered(g, u))
                zz = [zed[par][:, k_, :].rearrange("p (c h) -> p c h", c=GT) for k_ in range(3)]
                pz = ps[:, 2 + par, 0:GT * (HD + 1)].rearrange("p (c h) -> p c h", c=GT)
                dve.tensor_tensor(zz[0], pz[:, :, 0:HD], gat[u][:, :, C:GW], ALU.add).then_inc(s_z, 1)
                dve.wait_ge(s_z, g * 3 + 1)
                dve.scalar_tensor_tensor(out=zz[1], in0=zz[0], scalar=0.2, in1=zz[0], op0=ALU.mult, op1=ALU.max).then_inc(s_z, 1)
                dve.wait_ge(s_z, g * 3 + 2)
                dve.tensor_tensor(zz[2], pz[:, :, HD:HD + 1].broadcast_to([P, GT, HD]), zz[1], ALU.min).then_inc(s_z, 1)

            def one_hot(g, u):
                par = u % 2
                dve.wait_ge(s_kd[u], loaded(g, u))
                after(dve, s_agg, g, 2)
                dve.tensor_scalar(loc[par][:, :], kd[u][:, :, 0], bases[:, sl(g)], None, ALU.subtract).then_inc(s_loc, 1)
                dve.wait_ge(s_loc, g + 1)
                dve.tensor_tensor(hot[par][:, :, :], bcast(lane[:, :], 1, GT), bcast(loc[par][:, :], 2, P), ALU.is_equal).then_inc(s_hot, 1)

            def weigh(g, u):
                par = u % 2
                dve.wait_ge(s_e, g + 1)
                e4 = bcast(wx[par][:, :, D:RW], 3, C)
                x4 = bcast(gat[u][:, :, 0:C], 2, HD)
                dve.tensor_tensor(wx[par][:, :, 0:D].rearrange("p c (h d) -> p c h d", h=HD), x4, e4, ALU.mult).then_inc(s_wx, 1)

            def add_up(g, par):
                dve.wait_ge(s_agg, g + 1)
                after(dve, s_acc, g, 1)
                b = dve.value_load(trow[0:1, sl(g * 2 + 1)], min_val=0, max_val=T - 1)
                dve.tensor_tensor(acc[:, bass.ds(b, 1), :], ps[:, 4 + par:5 + par, 0:RW], acc[:, bass.ds(b, 1), :], ALU.add).then_inc(s_acc, 1)

            def group(g, u):
                first = isinstance(g, int)
                if not (first and g < 1):
                    logits(g - 1, (u - 1) % RING)
                one_hot(g, u)
                if not (first and g < 1):
                    weigh(g - 1, (u - 1) % RING)
                if not (first and g < 2):
                    add_up(g - 2, u % 2)
            run(dve, NG, RING, RING, group)
            logits(NG - 1, RING - 1)
            weigh(NG - 1, RING - 1)
            add_up(NG - 2, 0)
            add_up(NG - 1, 1)
            dve.wait_ge(s_acc, NG)

            def did(ins, st, name, plain=False):
                ins.then_inc(s_pd, 1)
                dve.wait_ge(s_pd, count(PD, st, name))
                if plain:
                    dve.sem_inc(s_carry, 1)

            def prepare(st, par, e):
                accs = acc[:, sl(st * TS, TS), :]
                rows = base[:, sl(st * TS, TS), :]
                m4 = mid.rearrange("p t (h d) -> p t h d", h=HD)
                dn = [den[:, k_, :].rearrange("p (t h) -> p t h", t=TS) for k_ in range(2)]
                r = [rt[:, k_, :].rearrange("p (t e) -> p t e", t=TS) for k_ in range(6)]
                lg = ps[:, 6, 0:TS * NE].rearrange("p (t e) -> p t e", t=TS)
                if e == 0:
                    did(dve.tensor_scalar(dn[0], accs[:, :, D:RW], TINY, None, ALU.max), st, "den")
                    did(dve.reciprocal(dn[1], dn[0]), st, "rden")
                    after(dve, s_yin, st, 1)
                    did(dve.tensor_tensor(m4, accs[:, :, 0:D].rearrange("p t (h d) -> p t h d", h=HD), bcast(dn[1], 3, C), ALU.mult), st, "avg")
                if e == 1:
                    m3 = mid.rearrange("p t (h d) -> p (t h) d", h=HD)
                    did(dve.tensor_tensor(m3, m3, bcast(gnnb_t[:, :], 1, TS * HD), ALU.add), st, "bias")
                    did(dve.tensor_scalar(low, mid, 0.0, None, ALU.min), st, "neg")
                    dve.wait_ge(s_pa, count(PA, st, "eexp"))
                    did(dve.scalar_tensor_tensor(out=mid, in0=mid, scalar=0.0, in1=low, op0=ALU.max, op1=ALU.add), st, "elu")
                    did(dve.scalar_tensor_tensor(out=rows, in0=mid, scalar=-1.0, in1=rows, op0=ALU.add, op1=ALU.add), st, "x2")
                if e == 2:
                    for t in range(TS):
                        ins = dve.bn_stats(st2[:, t, :], base[:, sl(st * TS + t), :])
                    did(ins, st, "stats", True)
                    for t in range(TS):
                        ins = dve.bn_aggr(mv2[:, t, :], st2[:, t, :])
                    did(ins, st, "mv")
                    dve.wait_ge(s_pa, count(PA, st, "sd"))
                    did(dve.reciprocal(ln2[:, 1, :], ln2[:, 0, :]), st, "rstd")
                    did(dve.scalar_tensor_tensor(out=ln2[:, 2, :], in0=mv2[:, :, 0], scalar=-1.0, in1=ln2[:, 1, :], op0=ALU.mult, op1=ALU.mult), st, "nmr")
                if e == 5:
                    dve.wait_ge(s_pp, count(PP, st, "logits"))
                    did(dve.tensor_reduce(rs[:, 0, :], lg, AX.X, ALU.max), st, "lmax")
                    did(dve.tensor_tensor(r[0], lg, bcast(rs[:, 0, :], 2, NE), ALU.subtract), st, "lsub")
                if e == 6:
                    dve.wait_ge(s_pa, count(PA, st, "lexp"))
                    did(dve.tensor_reduce(rs[:, 1, :], r[1], AX.X, ALU.add), st, "lsum")
                    did(dve.reciprocal(rs[:, 2, :], rs[:, 1, :]), st, "lrec")
                    did(dve.tensor_tensor(r[2], r[1], bcast(rs[:, 2, :], 2, NE), ALU.mult), st, "prob", True)
                    for t in range(TS):
                        ins = dve.max(top[:, t, :], r[2][:, t, :])
                    did(ins, st, "top", True)
                    for t in range(TS):
                        ins = dve.max_index(topi[:, t, :], top[:, t, :], r[2][:, t, :])
                    did(ins, st, "topi")
                    did(dve.tensor_copy(topf[:, :, 0:2], topi[:, :, 0:2]), st, "topf")
                    did(dve.tensor_tensor(rs[:, 3, :], top[:, :, 0], top[:, :, 1], ALU.add), st, "psum")
                    did(dve.tensor_scalar(rs[:, 3, :], rs[:, 3, :], TINY, None, ALU.max), st, "pmax")
                    did(dve.reciprocal(rs[:, 0, :], rs[:, 3, :]), st, "prec")
                    did(dve.tensor_tensor(top[:, :, 2:4], top[:, :, 0:2], bcast(rs[:, 0, :], 2, 2), ALU.mult), st, "w")
                    for c, (q0, q1) in enumerate((("eq1", "c1"), ("eq2", "c2"))):
                        did(dve.tensor_tensor(r[3 + c], bcast(lane[:, 0:NE], 1, TS), topf[:, :, c:c + 1].broadcast_to([P, TS, NE]), ALU.is_equal), st, q0)
                        did(dve.tensor_tensor(r[3 + c], r[3 + c], top[:, :, 2 + c:3 + c].broadcast_to([P, TS, NE]), ALU.mult), st, q1)
                    did(dve.tensor_tensor(comb[par][:, :, :], r[3], r[4], ALU.add), st, "comb")
                if e == 7:
                    dve.wait_ge(s_yin, st + 1)
                    for u, (t0, t1) in enumerate(UNITS):
                        dve.wait_ge(s_pp, count(PP, st, f"b2p{u}"))
                        tok = base[:, sl(st * TS + t0, t1 - t0), :]
                        did(dve.tensor_tensor(tok, ps[:, 6 + u % 2, 0:(t1 - t0) * D].rearrange("p (t c) -> p t c", c=D),
                                              tok, ALU.add), st, f"b2{u}")

            def gather_in(st, par, e, u):
                unit = (st * NE + e) * NU + u
                dve.wait_ge(s_y, unit + 1)
                if not (isinstance(unit, int) and unit < NU):
                    dve.wait_ge(s_moe, unit - NU + 1)
                t0, t1 = UNITS[u]
                for t in range(t0, t1):
                    tok = base[:, sl(st * TS + t), :]
                    ins = dve.scalar_tensor_tensor(out=tok, in0=ps[:, 4 + u % 2:5 + u % 2, (t - t0) * D:(t - t0 + 1) * D],
                                                   scalar=comb[par][:, t, e:e + 1], in1=tok, op0=ALU.mult, op1=ALU.add)
                ins.then_inc(s_moe, 1)

            def supertile(st, par, last=False):
                for e in range(NE):
                    if not last:
                        prepare(st + 1, 1 - par, e)
                    for u in range(NU):
                        gather_in(st, par, e, u)
            for e in range(NE):
                prepare(0, 0, e)
            run(dve, NS - 1, 2, 2, lambda st, par: supertile(st, par))
            supertile(NS - 1, (NS - 1) % 2, True)

        @block.tensor
        def _(pe):
            pe.wait_ge(s_const, 4)
            pe.wait_ge(s_w, 16 * NW)
            small = ps[:, 4, :]
            for k in range(KC):
                pe.transpose(small[0:C, k * P:k * P + P], wcat[:, k, 0:C], ident[:, :])
            o = KC * P
            pe.transpose(small[0:C, o:o + 2 * HD], wlr[:, :], ident[0:2 * HD, 0:2 * HD])
            o += 2 * HD
            for k in range(KC):
                pe.transpose(small[:, o:o + NE], rw_s[:, k * P:k * P + P], ident[0:NE, 0:NE])
                o += NE
            pe.transpose(small[:, o:o + NE * KC], b1_r[:, :], ident[0:NE * KC, 0:NE * KC])
            o += NE * KC
            pe.transpose(small[:, o:o + KC], gpre_r[:, :], ident[0:KC, 0:KC]).then_inc(s_once, 1)
            pe.wait_ge(s_step, at["small"])
            for k in range(KC):
                ins = pe.matmul(ps[:, 5, k * 2 * HD:(k + 1) * 2 * HD], wT[:, k, :], wlrT[:, :], start=True, stop=True)
            ins.then_inc(s_once, 1)
            pe.wait_ge(s_step, at["wcat"])

            def turn_x(i, u):
                pe.wait_ge(s_xn, i + 1)
                after(pe, s_xT, i, 2)
                for k in range(KC):
                    ins = pe.transpose(ps[:, 4 + u, k * P:k * P + P], xn[u][:, k * P:k * P + P], ident[:, :])
                ins.then_inc(s_xTp, 1)

            def project(i, u):
                pe.wait_ge(s_xT, i + 1)
                after(pe, s_kv, i, 2)
                for k in range(KC):
                    ins = pe.matmul(ps[:, 6 + u, 0:CQ + 3 * HID], xnT[u][:, k, :], wcat[:, k, :], start=(k == 0), stop=(k == KC - 1))
                ins.then_inc(s_proj, 1)

            def tile(i, u):
                turn_x(i, u)
                if not (isinstance(i, int) and i == 0):
                    project(i - 1, 1 - u)
            run(pe, T, 2, 4, tile)
            project(T - 1, (T - 1) % 2)

            pe.wait_ge(s_step, at["kmaxp"])
            pe.transpose(ps[:, 0, 0:P], kmaxp[:, :], ident[:, :]).then_inc(s_once, 1)
            pe.wait_ge(s_step, at["kdiag"])
            pe.matmul(ps[:, 1, 0:P], ones[:, :], kdiag[:, :], start=True, stop=True).then_inc(s_once, 1)
            pe.wait_ge(s_aonce, 3)
            pe.transpose(ps[0:MEM, 2, 0:P], mexp[:, :], ident[:, :])
            pe.transpose(ps[0:MEM, 2, P:2 * P], mk_t[:, 1, :], ident[:, :]).then_inc(s_once, 1)
            for t in range(T):
                if t % TS == 0:
                    pe.wait_ge(s_kexp, t // TS + 1)
                r = slice(0, P if t < T - 1 else TAIL)
                pe.matmul(ps[:, 3, 0:HID], kv[r, t, HID:2 * HID], kv[r, t, 0:HID], start=(t == 0), stop=False)
                pe.matmul(ps[:, 4, 0:1], kv[r, t, 0:HID], ones[r, 0:1], start=(t == 0), stop=False)
            pe.wait_ge(s_step, at["memT"])
            pe.matmul(ps[:, 3, 0:HID], memT[:, 1, :], memT[:, 0, :], start=False, stop=True)
            pe.matmul(ps[:, 4, 0:1], memT[:, 0, :], ones[0:MEM, 0:1], start=False, stop=True).then_inc(s_once, 1)
            pe.wait_ge(s_step, at["ctxm"])
            pe.matmul(ps[:, 5, 0:D], ctxm[:, :], wout_s[:, :], start=True, stop=True).then_inc(s_once, 1)
            pe.wait_ge(s_step, at["mixw"])
            pe.wait_ge(s_step, at["q"])

            def turn_q(i, u):
                after(pe, s_qT, i, 2)
                pe.transpose(ps[:, 6 + u:7 + u, 0:P], q_all[:, i, :] if isinstance(i, int) else q_all[:, sl(i), :], ident[:, :]).then_inc(s_qTp, 1)

            def mix(i, u):
                pe.wait_ge(s_qT, i + 1)
                after(pe, s_arow, i, 2)
                pe.matmul(ps[:, u, 0:D], qT[u], mixw[:, :], start=True, stop=True).then_inc(s_mixp, 1)

            for t in range(T):
                turn_q(t, t % 2)
                if t:
                    mix(t - 1, (t - 1) % 2)
            mix(T - 1, (T - 1) % 2)

            for i, (_, side, k, j) in enters:
                done, cur = at[plan[i - 1]]
                for h, part in enumerate(HALVES):
                    pe.wait_ge(s_key, done[h])
                    for t in range(*part):
                        ins = pe.transpose(turned[:, t, :], keys[cur][:, t, :], ident[:, :])
                    ins.then_inc(s_turned, 1)

            pe.wait_ge(s_cnt, T)
            pe.matmul(ps[:, 5, 0:T], ones[:, :], cnt[:, :], start=True, stop=True).then_inc(s_once, 1)
            pe.wait_ge(s_row, 32)

            def turn_hot(g, u):
                par = u % 2
                pe.wait_ge(s_hot, g + 1)
                after(pe, s_hT, g, 2)
                for c in range(GT):
                    ins = pe.transpose(ps[:, par, c * P:c * P + P], hot[par][:, c, :], ident[:, :])
                ins.then_inc(s_hTp, 1)

            def aggregate(g, u):
                par = u % 2
                pe.wait_ge(s_wx, g + 1)
                after(pe, s_acc, g, 2)
                for c in range(GT):
                    ins = pe.matmul(ps[:, 4 + par, 0:RW], hot[par][:, c, :], wx[par][:, c, :], start=(c == 0), stop=(c == GT - 1))
                ins.then_inc(s_agg, 1)

            def spread_el(g, u):
                par = u % 2
                pe.wait_ge(s_hT, g + 1)
                after(pe, s_z, g, 2, 3)
                b = pe.value_load(trow[0:1, sl(g * 2 + 1)], min_val=0, max_val=T - 1)
                for c in range(GT):
                    ins = pe.matmul(ps[:, 2 + par, c * (HD + 1):(c + 1) * (HD + 1)], hotT[par][:, c, :],
                                    el_all[:, bass.ds(b, 1), :].rearrange("p a h -> p (a h)"), start=True, stop=True)
                ins.then_inc(s_el, 1)

            def group(g, u):
                turn_hot(g, u)
                if not (isinstance(g, int) and g < 1):
                    aggregate(g - 1, (u - 1) % RING)
                spread_el(g, u)
            run(pe, NG, RING, RING, group)
            aggregate(NG - 1, RING - 1)

            def prepare(st, par, e):
                if e == 4:
                    pe.wait_ge(s_pa, count(PA, st, "y"))
                    after(pe, s_pd, st, 1, len(PD))
                    for t in range(TS):
                        if t >= 2:
                            pe.wait_ge(s_pa, count(PA, st, f"yT{t - 2}"))
                        for k in range(KC):
                            ins = pe.transpose(ps[:, 6 + t % 2, k * P:k * P + P], mid[:, t, k * P:k * P + P], ident[:, :])
                        ins.then_inc(s_pp, 1)
                if e == 5:
                    pe.wait_ge(s_pa, count(PA, st, f"yT{TS - 1}"))
                    for t in range(TS):
                        for k in range(KC):
                            ins = pe.matmul(ps[:, 6, t * NE:(t + 1) * NE], yT[par][:, k, t * P:t * P + P], rwT[:, k, :], start=(k == 0), stop=(k == KC - 1))
                    ins.then_inc(s_pp, 1)
                if e == 7:
                    pe.wait_ge(s_pd, count(PD, st, "comb"))
                    for t in range(4):
                        ins = pe.transpose(ps[0:NE, 7, t * P:t * P + P], comb[par][:, t, :], ident[:, :])
                    ins.then_inc(s_pp, 1)
                    for t in range(4, TS):
                        ins = pe.transpose(ps[0:NE, 6, (t - 4) * P:(t - 3) * P], comb[par][:, t, :], ident[:, :])
                    ins.then_inc(s_pp, 1)
                    for u, (t0, t1) in enumerate(UNITS):
                        if u == 0:
                            pe.wait_ge(s_pa, count(PA, st, "cTb"))
                        if u >= 2:
                            pe.wait_ge(s_pd, count(PD, st, f"b2{u - 2}"))
                        for t in range(t0, t1):
                            ins = pe.matmul(ps[:, 6 + u % 2, (t - t0) * D:(t - t0 + 1) * D], combT[:, t, :], b2_s[:, :], start=True, stop=True)
                        ins.then_inc(s_pp, 1)

            def hidden(st, par, e):
                for f in range(KC):
                    for c in range(2):
                        bank = (st * NE + e) * 4 + f * 2 + c
                        after(pe, s_g, bank, 4)
                        for k in range(KC):
                            ins = pe.matmul(ps[:, f * 2 + c, 0:HALFT], w1_s[:, e, k, f * P:f * P + P],
                                            yT[par][:, k, c * HALFT:(c + 1) * HALFT], start=(k == 0), stop=(k == KC - 1))
                        ins.then_inc(s_h, 1)

            def outward(st, par, e):
                pe.wait_ge(s_g, (st * NE + e) * 4 + 4)
                for u, (t0, t1) in enumerate(UNITS):
                    unit = (st * NE + e) * NU + u
                    after(pe, s_moe, unit, 2)
                    for t in range(t0, t1):
                        for k in range(KC):
                            ins = pe.matmul(ps[:, 4 + u % 2, (t - t0) * D:(t - t0 + 1) * D], hT[e % 2][:, k, t * P:t * P + P],
                                            w2_s[:, e, k, :], start=(k == 0), stop=(k == KC - 1))
                    ins.then_inc(s_y, 1)

            def supertile(st, par, last=False):
                for e in range(NE):
                    if not last:
                        prepare(st + 1, 1 - par, e)
                    if e < NE - 1:
                        hidden(st, par, e + 1)
                    elif not last:
                        hidden(st + 1, 1 - par, 0)
                    outward(st, par, e)
            for e in range(NE):
                prepare(0, 0, e)
            pe.wait_ge(s_ew, 32 * NE)
            hidden(0, 0, 0)
            run(pe, NS - 1, 2, 2, lambda st, par: supertile(st, par))
            supertile(NS - 1, (NS - 1) % 2, True)

        @block.scalar
        def _(act):
            act.wait_ge(s_step, at["mv"])
            act.activation(tmpT[:, :], mv[:, :, 1], ACT.Sqrt, bias=eps_t[:, 0:1]).then_inc(s_aonce, 1)
            act.wait_ge(s_step, at["norm2"])
            act.activation(tmpT[:, :], tmpT[:, :], ACT.Sqrt, scale=float(D)).then_inc(s_aonce, 1)
            act.wait_ge(s_step, at["rsc"])

            def normalise(i, u):
                after(act, s_xTp, i, 2)
                after(act, s_base, i, 2)
                act.activation(xn[u][:, :], base[:, i, :] if isinstance(i, int) else base[:, sl(i), :].rearrange("p a c -> p (a c)"),
                               ACT.Identity, bias=nmr[:, sl(i)], scale=rstd[:, sl(i)]).then_inc(s_xn, 1)

            def store_kv(i, u):
                act.wait_ge(s_q, i + 1)
                act.activation(kv[:, sl(i), :], ps[:, 6 + u:7 + u, CQ + HID:CQ + 3 * HID], ACT.Copy, scale=rsc[:, sl(i)]).then_inc(s_kv, 1)

            def tile(i, u):
                normalise(i, u)
                if not (isinstance(i, int) and i < 2):
                    store_kv(i - 2, u)
            run(act, T, 2, 2, tile)
            store_kv(T - 2, (T - 2) % 2)
            store_kv(T - 1, (T - 1) % 2)

            act.wait_ge(s_step, at["nkmx"])
            act.activation(mexp[:, :], mk_t[:, 0, :], ACT.Exp, bias=kmx[:, 2:3]).then_inc(s_aonce, 1)
            for c in range(NS):
                act.wait_ge(s_ksub, c + 1)
                kc = kv[:, TS * c:TS * c + TS, 0:HID]
                act.activation(kc, kc, ACT.Exp).then_inc(s_kexp, 1)
            act.wait_ge(s_step, at["qsub"])
            act.activation(q_all[:, :, :], q_all[:, :, :], ACT.Exp).then_inc(s_aonce, 1)

            def copy_qT(i, u):
                act.wait_ge(s_qTp, i + 1)
                after(act, s_mixp, i, 2)
                act.activation(qT[u], ps[:, 6 + u, 0:P], ACT.Copy).then_inc(s_qT, 1)
            run(act, T, 2, 2, copy_qT)
            act.wait_ge(s_step, at["ss"])
            act.activation(ss[:, :], ss[:, :], ACT.Sqrt).then_inc(s_aonce, 1)

            act.wait_ge(s_edges, 96)
            act.wait_ge(s_qTp, T)
            for b in range(T):
                if b >= 2:
                    act.wait_ge(s_cnt, b - 1)
                junk = arena[:, (b % 2) * n_sort:(b % 2 + 1) * n_sort].rearrange("p (t l) -> p t l", t=NB)
                act.activation(junk, src_i, ACT.Sign, bias=nthr[:, b:b + 1], accum_out=cnt[:, b:b + 1]).then_inc(s_cnt, 1)

            turns = 0
            for i, (_, side, k, j) in enters:
                parts = ((0, NB),) if side == "B" and k > 2 * ROW_BITS else HALVES
                for part in parts:
                    turns += 2 // len(parts)
                    act.wait_ge(s_turned, turns)
                    pairs = enter_pairs(k, part, NB)[0] if side == "B" else [(lambda v: inner(v, P // 2, part), 0)]
                    for pick, _ in pairs:
                        ins = act.activation(pick(right)[1], pick(turned)[1], ACT.Copy)
                    ins.then_inc(s_right, 1)

            act.wait_ge(s_srt, 16)
            act.wait_ge(s_tab, 16)
            act.wait_ge(s_step, at["pair"])
            for e in range(NE):
                act.dma_start(w1_s[:, e, :, :], w1[e].rearrange("(k p) f -> p k f", p=P)).then_inc(s_ew, 16)
                act.dma_start(w2_s[:, e, :, :], w2[e].rearrange("(k p) f -> p k f", p=P)).then_inc(s_ew, 16)

            def weights(g, u):
                par = u % 2
                act.wait_ge(s_z, g * 3 + 3)
                after(act, s_agg, g, 2)
                act.activation(wx[par][:, :, D:RW], zed[par][:, 2, :].rearrange("p (c h) -> p c h", c=GT), ACT.Exp).then_inc(s_e, 1)

            def copy_hot(g, u):
                par = u % 2
                act.wait_ge(s_hTp, g + 1)
                after(act, s_el, g, 2)
                act.activation(hotT[par][:, :, :], ps[:, par, :].rearrange("p (c n) -> p c n", c=GT), ACT.Copy).then_inc(s_hT, 1)

            def group(g, u):
                if not (isinstance(g, int) and g < 1):
                    weights(g - 1, (u - 1) % RING)
                copy_hot(g, u)
            run(act, NG, RING, RING, group)
            weights(NG - 1, RING - 1)

            def did(ins):
                ins.then_inc(s_pa, 1)

            def prepare(st, par, e):
                if e == 1:
                    act.wait_ge(s_pd, count(PD, st, "neg"))
                    did(act.activation(low, low, ACT.Exp))
                if e == 2:
                    act.wait_ge(s_pd, count(PD, st, "mv"))
                    did(act.activation(ln2[:, 0, :], mv2[:, :, 1], ACT.Sqrt, bias=eps_t[:, 0:1]))
                if e == 3:
                    act.wait_ge(s_pd, count(PD, st, "nmr"))
                    for t in range(TS):
                        ins = act.activation(mid[:, t:t + 1, :], base[:, sl(st * TS + t), :], ACT.Identity, bias=ln2[:, 2, t:t + 1], scale=ln2[:, 1, t:t + 1])
                    did(ins)
                if e == 4:
                    for t in range(TS):
                        act.wait_ge(s_pp, count(PP, st, f"yTp{t}"))
                        did(act.activation(yT[par][:, :, t * P:t * P + P], ps[:, 6 + t % 2, 0:D].rearrange("p (k n) -> p k n", k=KC), ACT.Copy))
                if e == 5:
                    act.wait_ge(s_pd, count(PD, st, "lsub"))
                    did(act.activation(rt[:, 1, :], rt[:, 0, :], ACT.Exp))
                if e == 7:
                    act.wait_ge(s_pp, count(PP, st, "cTpa"))
                    did(act.activation(combT[:, 0:4, :], ps[0:NE, 7, :].rearrange("p (t n) -> p t n", t=4), ACT.Copy))
                    act.wait_ge(s_pp, count(PP, st, "cTpb"))
                    did(act.activation(combT[:, 4:TS, :], ps[0:NE, 6, 0:(TS - 4) * P].rearrange("p (t n) -> p t n", t=TS - 4), ACT.Copy))

            def gelus(st, par, e):
                last_unit = (st * NE + e - 1) * NU
                if not (isinstance(last_unit, int) and last_unit <= 0):
                    act.wait_ge(s_y, last_unit)
                for f in range(KC):
                    for c in range(2):
                        act.wait_ge(s_h, (st * NE + e) * 4 + f * 2 + c + 1)
                        act.activation(hT[e % 2][:, f, c * HALFT:(c + 1) * HALFT], ps[:, f * 2 + c, 0:HALFT], ACT.Gelu,
                                       bias=b1_t[:, e, f:f + 1]).then_inc(s_g, 1)

            def supertile(st, par, last=False):
                for e in range(NE):
                    if not last:
                        prepare(st + 1, 1 - par, e)
                    if e < NE - 1:
                        gelus(st, par, e + 1)
                    elif not last:
                        gelus(st + 1, 1 - par, 0)
            for e in range(NE):
                prepare(0, 0, e)
            gelus(0, 0, 0)
            run(act, NS - 1, 2, 2, lambda st, par: supertile(st, par))
            supertile(NS - 1, (NS - 1) % 2, True)

        @block.gpsimd
        def _(pool):
            pool.memset(src_i[:, NB - 1, :], PAD_NODE).then_inc(s_pad, 1)
            pool.memset(dst_i[:, NB - 1, :], 0).then_inc(s_pad, 1)
            pool.memset(base[:, T - 1, :], 0.0).then_inc(s_pad, 1)
            pool.memset(ident[:, :], 0.0).then_inc(s_pad, 1)
            pool.memset(ones[:, :], 1.0).then_inc(s_const, 1)
            pool.iota(lane_i[:, :], [[1, P]], base=0, channel_multiplier=0).then_inc(s_const, 1)
            pool.iota(row_i[:, :], [[1, 1]], base=0, channel_multiplier=GT).then_inc(s_const, 1)
            pool.wait_ge(s_pad, 4)
            pool.affine_select(out=ident[:, :], in_=ident[:, :], compare_op=ALU.not_equal, fill=1.0, base=0,
                               pattern=[[-1, P]], channel_multiplier=1).then_inc(s_const, 1)

            def add_x(i, u):
                pool.wait_ge(s_xn, i + 1)
                b = base[:, sl(i), :]
                pool.tensor_tensor(b, b, xn[u][:, :].unsqueeze(1), ALU.add).then_inc(s_base, 1)
            run(pool, T, 2, 2, add_x)
            pool.wait_ge(s_step, at["att"])
            pool.memset(big[:, :], 0.0).then_inc(s_zero, 1)
            pool.wait_ge(s_tab, 16)

            def gather(g, u):
                pool.wait_ge(s_kd[u], loaded(g, u))
                after(pool, s_wx, g, RING)
                pool.sem_inc(s_carry_pool, 1)
                for c in range(GT):
                    pool.indirect_dma_start(gat[u][:, c, :], None, table_d,
                                            bass.IndirectOffsetOnAxis(ap=kd[u][:, c, 1:2].bitcast(I32), axis=0)).then_inc(s_gat[u], 16)
            run(pool, NG, RING, RING, gather)

            def seed(st, par):
                pool.wait_ge(s_pa, count(PA, st, "y"))
                tok = base[:, sl(st * TS, TS), :]
                pool.tensor_tensor(tok, tok, mid, ALU.add).then_inc(s_yin, 1)
            run(pool, NS, 2, 2, seed)

        @block.sync
        def _(sp):
            loads = [(wcat[:, k, 0:C], W[k * P:k * P + P, :]) for k in range(KC)]
            loads += [(wcat[:, k, CQ:], w_qkv[k * P:k * P + P, :]) for k in range(KC)]
            loads += [(wlr[0:HD, :], Wr), (wlr[HD:2 * HD, :], Wl), (rw_s[:, :], router_w), (wout_s[:, :], w_out), (b2_s[:, :], b2)]
            loads += [(b1_r[:, :], b1.rearrange("e (k p) -> (e k) p", p=P)), (gpre_r[:, :], g_pre.rearrange("(k p) -> k p", p=P))]
            loads += [(mk_t[:, a, :], mem_kv[a].rearrange("h d m -> (h d) m")) for a in range(2)]
            for dst_, src_ in loads:
                sp.dma_start(dst_, src_).then_inc(s_w, 16)
            sp.dma_start(rows_b[:, 0, :], b_out.partition_broadcast(P)).then_inc(s_w, 16)
            sp.dma_start(rows_b[:, 1, :], g_out.partition_broadcast(P)).then_inc(s_w, 16)
            sp.dma_start(gnnb_t[:, :], gnn_b.partition_broadcast(P)).then_inc(s_w, 16)
            sp.wait_ge(s_pad, 4)
            xm = x[0:(T - 1) * P, :].rearrange("(t p) c -> p t c", p=P)
            for c in range(4):
                sp.dma_start(base[:, 12 * c:12 * c + 12, :], xm[:, 12 * c:12 * c + 12, :]).then_inc(s_xl, 16)
            sp.dma_start(base[0:TAIL, T - 1, :], x[(T - 1) * P:N, :]).then_inc(s_xl, 16)
            for buf, d in ((src_i, src), (dst_i, dst)):
                sp.dma_start(buf[:, 0:NB - 1, :], d[0:FULL].rearrange("(t m l) -> m t l", m=P, l=P)).then_inc(s_edges, 16)
                sp.dma_start(buf[0:ROWS, NB - 1, :], d[FULL:FULL + ROWS * P].rearrange("(m l) -> m l", l=P)).then_inc(s_edges, 16)
                sp.dma_start(buf[ROWS:ROWS + 1, NB - 1, 0:REST], d[FULL + ROWS * P:E].rearrange("(m l) -> m l", m=1)).then_inc(s_edges, 16)
            sp.wait_ge(s_q, T)
            sp.dma_start(table_d.rearrange("(t p) c -> p t c", p=P), tb).then_inc(s_tab, 16)
            sp.wait_ge(s_step, at["groups"])
            sp.dma_start(groups_d.rearrange("(p c) a -> p (c a)", c=GT), gout[:, :, :].rearrange("p c a -> p (c a)")).then_inc(s_gtd, 16)
            sp.dma_start(bases_d.rearrange("(p c) -> p c", c=GT), gsum[:, 3, :]).then_inc(s_gtd, 16)
            sp.wait_ge(s_gtd, 32)
            sp.dma_start(trow[:, :], groups_d.rearrange("(a p) c -> a (p c)", a=1)).then_inc(s_row, 16)
            sp.dma_start(bases[:, :], bases_d.partition_broadcast(P)).then_inc(s_row, 16)
            sp.wait_ge(s_step, at["pair"])
            sp.dma_start(sorted_d.rearrange("(t m c) -> m t c", m=P, c=2 * P), pair.rearrange("p t l c -> p t (l c)")).then_inc(s_srt, 16)
            sp.wait_ge(s_srt, 16)
            sp.wait_ge(s_row, 32)

            def load_group(g, u):
                if not (isinstance(g, int) and g < RING):
                    sp.wait_ge(s_loc, g - RING + 1)
                    sp.wait_ge(s_gat[u], gathered(g, u) - 16 * GT)
                first = sp.value_load(trow[0:1, sl(g * 2)], min_val=0, max_val=E * 2)
                sp.dma_start(kd[u][:, :, :].rearrange("p c a -> p (c a)"),
                             sorted_d[bass.ds(first, GE * 2)].rearrange("(p c) -> p c", p=P)).then_inc(s_kd[u], 16)
            run(sp, NG, RING, RING, load_group)

            def store(st, par):
                sp.wait_ge(s_moe, (st + 1) * (NE * NU))
                rows = out[0:(T - 1) * P, :].rearrange("(t p) c -> p t c", p=P)
                if isinstance(st, int) and st == NS - 1:
                    sp.dma_start(rows[:, TS * st:T - 1, :], base[:, TS * st:T - 1, :]).then_inc(s_out[par], 16)
                    sp.dma_start(out[(T - 1) * P:N, :], base[0:TAIL, T - 1, :]).then_inc(s_out[par], 16)
                else:
                    sp.dma_start(rows[:, sl(st * TS, TS), :], base[:, sl(st * TS, TS), :]).then_inc(s_out[par], 16)
            run(sp, NS - 1, 2, 2, store)
            store(NS - 1, (NS - 1) % 2)
            sp.wait_ge(s_out[0], 16 * ((NS + 1) // 2 + 1))
            sp.wait_ge(s_out[1], 16 * (NS // 2))


_INS = ["x", "src", "dst", "L0_gnn_W", "L0_gnn_Wl", "L0_gnn_Wr", "L0_gnn_b", "L0_mix_w_qkv", "L0_mix_mem_kv", "L0_mix_w_out",
        "L0_mix_b_out", "L0_mix_g_out", "L0_mix_g_pre", "L0_ffn_router_w", "L0_ffn_w1", "L0_ffn_b1", "L0_ffn_w2", "L0_ffn_b2"]
_OUTS = [((6250, 256), "float32")]


def kernel(**inputs):
    import numpy as _np
    import concourse.bacc as _bacc
    from concourse import mybir as _mybir
    from concourse.bass_utils import run_bass_kernel_spmd as _run

    nc = _bacc.Bacc("TRN2", target_bir_lowering=False, num_devices=1)
    arrays, args = {}, []
    for name in _INS:
        a = _np.ascontiguousarray(inputs[name])
        arrays[f"in_{name}_dram"] = a
        args.append(nc.dram_tensor(f"in_{name}_dram", a.shape, _mybir.dt.from_np(a.dtype), kind="ExternalInput").ap())
    for i, (shape, dtype) in enumerate(_OUTS):
        dt = _mybir.dt.from_np(_np.dtype(dtype))
        args.append(nc.dram_tensor(f"out_{i}_dram", shape, dt, kind="ExternalOutput").ap())
    gps_layer(nc, *args)
    r = _run(nc, [arrays], core_ids=[0])
    return r.results[0]["out_0_dram"]
```

```python
import concourse.bass as bass
from concourse import mybir
from contextlib import ExitStack

ALU = mybir.AluOpType
ACT = mybir.ActivationFunctionType
AX = mybir.AxisListType
F32 = mybir.dt.float32
I32 = mybir.dt.int32
U32 = mybir.dt.uint32

P = 128
LN_EPS = 1e-5
TINY = 1e-12

ROW_BITS = 7
NODE_BITS = 13
PAD_NODE = (1 << NODE_BITS) - 1
KEY_BASE = 0x20000000


def make_plan(levels):
    plan = []
    for k in range(1, ROW_BITS + 1):
        plan += [("plain", "A", k, j) for j in range(k - 1, -1, -1)]
    for k in range(ROW_BITS + 1, levels + 1):
        plan.append(("enter", "B", k, k - 1))
        plan += [("plain", "B", k, j) for j in range(k - 2, ROW_BITS - 1, -1)]
        plan.append(("enter", "A", k, ROW_BITS - 1))
        plan += [("plain", "A", k, j) for j in range(ROW_BITS - 2, -1, -1)]
    return plan


def inner(x, w, part):
    v = x[:, part[0]:part[1], :].rearrange("p t (g b l) -> p (t g) b l", b=2, l=w)
    return v[:, :, 0, :], v[:, :, 1, :]


def directed(x, w, a, d, part):
    v = x[:, part[0]:part[1], :].rearrange("p t (g d a b l) -> p (t g) d a b l", d=2, a=a, b=2, l=w)
    return v[:, :, d, :, 0, :], v[:, :, d, :, 1, :]


def outer(x, u, nb):
    n = nb // (2 * u) * (2 * u)
    pairs = []
    if n:
        v = x[:, 0:n, :].rearrange("p (q b u) m -> p q b (u m)", b=2, u=u)
        pairs.append((v[:, :, 0, :], v[:, :, 1, :]))
    left = nb - n - u
    if left > 0:
        pairs.append((x[:, n:n + left, :], x[:, n + u:nb, :]))
        return pairs, (n + left, n + u)
    return pairs, (n, nb)


def enter_pairs(k, part, nb):
    top = ROW_BITS * 2
    if k < top:
        return [(lambda x, d=d: directed(x, 1 << (k - ROW_BITS - 1), 1, d, part), 2 * d - 1) for d in range(2)], None
    if k == top:
        last = nb - 1
        end = min(part[1], last)
        res = []
        for d in range(2):
            first = part[0] + (part[0] + d) % 2
            res.append((lambda x, s=first: tuple(x[:, s:end:2, c * 64:c * 64 + 64] for c in range(2)), 2 * d - 1))
        if part[1] == nb:
            res.append((lambda x: tuple(x[:, last:nb, c * 64:c * 64 + 64] for c in range(2)), 1))
        return res, None
    if k == top + 1:
        def pick(x, d):
            v = x[:, 0:12, :].rearrange("p (q d b) m -> p q d b m", d=2, b=2)
            return v[:, :, d, 0, :], v[:, :, d, 1, :]
        return [(lambda x, d=d: pick(x, d), 2 * d - 1) for d in range(2)], (12, 13, 1)
    if k == top + 2:
        return [(lambda x, q=q: (x[:, 4 * q:4 * q + 2, :], x[:, 4 * q + 2:4 * q + 4, :]), 1 if q == 1 else -1)
                for q in range(3)], (12, 13, 1)
    if k == top + 3:
        return [(lambda x: (x[:, 0:4, :], x[:, 4:8, :]), -1), (lambda x: (x[:, 8:9, :], x[:, 12:13, :]), 1)], (9, 12, -1)
    return [(lambda x: (x[:, 0:5, :], x[:, 8:13, :]), 1)], (5, 8, -1)


def run(eng, n, unroll, head, body):
    end = head + (n - head) // unroll * unroll
    for i in range(head):
        body(i, i % unroll)
    if end > head:
        with eng.Fori(0, (end - head) // unroll) as turn:
            for u in range(unroll):
                body(turn * unroll + (head + u), (head + u) % unroll)
    for i in range(end, n):
        body(i, i % unroll)


def after(eng, sem, i, lag, per=1):
    if isinstance(i, int) and i < lag:
        return
    eng.wait_ge(sem, (i - lag + 1) * per)


def bcast(ap, axis, n):
    v = ap.unsqueeze(axis)
    shape = list(v.shape)
    shape[axis] = n
    return v.broadcast_to(shape)


def gps_layer(nc, x, src, dst, W, Wl, Wr, gnn_b, w_qkv, mem_kv, w_out, b_out, g_out, g_pre,
              router_w, w1, b1, w2, b2, out):
    N, D = x.shape
    E = src.shape[0]
    HD, C = Wl.shape
    _, MH, MD, MEM = mem_kv.shape
    HID = MH * MD
    NE, _, F = w1.shape
    T = -(-N // P)
    TAIL = N - (T - 1) * P
    SCALE = float(MD) ** -0.5
    KC = D // P
    TS = 7
    NS = T // TS
    HALFT = TS * P // 2
    assert T == TS * NS and HID == P and D == HD * C and F == D

    BLK = P * P
    NB = -(-E // BLK)
    LEVELS = (NB * BLK - 1).bit_length()
    assert NB == 13 and LEVELS == 18 and N <= PAD_NODE
    FULL = (NB - 1) * BLK
    ROWS = (E - FULL) // P
    REST = E - FULL - ROWS * P
    HALVES = ((0, 8), (8, NB))

    GT = 2
    GE = GT * P
    RING = 8
    HOTS = 8
    NG = (E + T * (GE - 1)) // GE
    GW = C + HD
    RW = D + HD
    GC = -(-NG // P)
    assert RING % HOTS == 0 and NB * BLK - E >= GE

    plan = make_plan(LEVELS)
    enters = [(n, s) for n, s in enumerate(plan) if s[0] == "enter"]

    table_d = nc.dram_tensor("gather_table", (T * P, GW), F32).ap()
    sorted_d = nc.dram_tensor("sorted_edges", (NB * BLK * 2,), F32).ap()
    groups_d = nc.dram_tensor("group_table", (2, P * GC), I32).ap()
    bases_d = nc.dram_tensor("group_bases", (P * GC,), F32).ap()

    with ExitStack() as ctx:
        def sb(name, shape, dt=F32):
            return ctx.enter_context(nc.sbuf_tensor(name, shape, dt))

        def sem(name):
            return ctx.enter_context(nc.semaphore(name))

        ps = ctx.enter_context(nc.psum_tensor("ps", [P, 8, 512], F32))

        ident = sb("ident", [P, P])
        ones = sb("ones", [P, P])
        lane = sb("lane", [P, P])
        lane_i = sb("lane_i", [P, P], I32)
        row_i = sb("row_i", [P, 1], I32)
        rowf = sb("rowf", [P, 1])
        sign7 = sb("sign7", [P, 1])
        eps_t = sb("eps_t", [P, 1])
        base = sb("base", [P, T, D])
        mv = sb("mv", [P, T, 2])
        rstd = sb("rstd", [P, T])
        nmr = sb("nmr", [P, T])
        rsc = sb("rsc", [P, T])
        tmpT = sb("tmpT", [P, T])
        el_all = sb("el_all", [P, T, HD + 1])
        big = sb("big", [P, T * RW])
        kv = big[:, 0:T * 2 * HID].rearrange("p (t c) -> p t c", t=T)
        att = big[:, 0:T * D].rearrange("p (t c) -> p t c", t=T)
        acc = big[:, :].rearrange("p (t c) -> p t c", t=T)

        n_sort = NB * P
        A_Q, A_TB = 0, T * HID
        A_E = A_TB + T * GW
        A_K = A_E + 2 * n_sort
        A_END1 = A_K + 3 * n_sort
        A_W1, A_W2 = 0, NE * KC * F
        A_Y = A_W2 + NE * KC * D
        A_H = A_Y + 2 * KC * TS * P
        A_X = A_H + 2 * KC * TS * P
        A_END2 = A_X + 2 * TS * D
        A_G = A_Y
        arena = sb("arena", [P, max(A_END1, A_END2)])
        q_all = arena[:, A_Q:A_TB].rearrange("p (t c) -> p t c", t=T)
        tb = arena[:, A_TB:A_E].rearrange("p (t c) -> p t c", t=T)
        src_i = arena[:, A_E:A_E + n_sort].bitcast(I32).rearrange("p (t l) -> p t l", t=NB)
        dst_i = arena[:, A_E + n_sort:A_K].bitcast(I32).rearrange("p (t l) -> p t l", t=NB)
        pair = arena[:, A_E:A_K].rearrange("p (t l c) -> p t l c", t=NB, c=2)
        keys = [arena[:, A_K + i * n_sort:A_K + (i + 1) * n_sort].rearrange("p (t l) -> p t l", t=NB) for i in range(2)]
        right = arena[:, A_K + 2 * n_sort:A_END1].rearrange("p (t l) -> p t l", t=NB)
        w1_s = arena[:, A_W1:A_W2].rearrange("p (e k f) -> p e k f", e=NE, k=KC)
        w2_s = arena[:, A_W2:A_Y].rearrange("p (e k f) -> p e k f", e=NE, k=KC)
        yT = [arena[:, A_Y + i * KC * TS * P:A_Y + (i + 1) * KC * TS * P].rearrange("p (k n) -> p k n", k=KC) for i in range(2)]
        hT = [arena[:, A_H + i * KC * TS * P:A_H + (i + 1) * KC * TS * P].rearrange("p (k n) -> p k n", k=KC) for i in range(2)]
        low = arena[:, A_X:A_X + TS * D].rearrange("p (t c) -> p t c", t=TS)
        mid = arena[:, A_X + TS * D:A_END2].rearrange("p (t c) -> p t c", t=TS)

        spare = arena[:, A_END1:A_END2]
        stats = spare[:, 0:T * 6].rearrange("p (t s) -> p t s", t=T)
        wT = spare[0:C, T * 6:T * 6 + KC * P].rearrange("p (k n) -> p k n", k=KC)
        b1_r = spare[0:NE * KC, T * 6 + KC * P:T * 6 + (KC + 1) * P]
        gpre_r = spare[0:KC, T * 6 + (KC + 1) * P:T * 6 + (KC + 2) * P]

        junk = spare[:, 0:NB * P // 2].bitcast(mybir.dt.bfloat16).rearrange("p (t l) -> p t l", t=NB)
        bases = spare[:, 0:P * GC]
        assert P * GC <= A_END2 - A_END1 and A_G + GT * (RING * GW + (HOTS + 2) * P + 2 * RW) <= A_END1

        wcat = sb("wcat", [P, KC, GW + HD + 3 * HID])
        CQ = GW + HD
        wlr = sb("wlr", [2 * HD, C])
        wlrT = sb("wlrT", [C, 2 * HD])
        gpre_t = sb("gpre_t", [P, KC])
        wout_s = sb("wout_s", [P, D])
        rows_b = sb("rows_b", [P, 2, D])
        gnnb_t = sb("gnnb_t", [P, C])
        mk_t = sb("mk_t", [P, 2, MEM])
        rw_s = sb("rw_s", [NE, D])
        rwT = sb("rwT", [P, KC, NE])
        b1_t = sb("b1_t", [P, NE, KC])
        b2_s = sb("b2_s", [NE, D])

        xn = [sb(f"xn{i}", [P, D]) for i in range(2)]
        xnT = [sb(f"xnT{i}", [P, KC, P]) for i in range(2)]
        kmx = sb("kmx", [P, 4])
        kmaxp = sb("kmaxp", [P, P])
        kdiag, kmaxb = xn[1][:, 0:P], xn[1][:, P:2 * P]
        mexp = sb("mexp", [P, MEM])
        memT = sb("memT", [MEM, 2, P])
        ctxm = sb("ctxm", [P, P])
        mixw = sb("mixw", [P, D])
        qst = sb("qst", [P, 2, T * MH])
        qT = xnT[0][:, 0, :], xnT[1][:, 0, :]
        sq = xn[0]
        ss = sb("ss", [P, T])
        cnt = sb("cnt", [P, T])
        starts = sb("starts", [P, T + 1])
        gtab = sb("gtab", [P, 4, T])
        gsel = spare[:, 0:GC * T].rearrange("p (g t) -> p g t", g=GC)
        gidx = sb("gidx", [P, GC])
        gsum = sb("gsum", [P, 4, GC])
        gout = sb("gout", [P, 2, GC], I32)
        nthr = sb("nthr", [P, T])
        DLAG, PLAG = 5, 1
        trow = sb("trow", [3, P * GC + RING], I32)
        kd = [sb(f"kd{i}", [P, GT, 2]) for i in range(RING)]

        def ring(start, n, width):
            return [arena[:, start + i * GT * width:start + (i + 1) * GT * width].rearrange("p (c w) -> p c w", c=GT) for i in range(n)]
        gat = ring(A_G, RING, GW)
        hot = ring(A_G + RING * GT * GW, HOTS, P)
        hotT = ring(A_G + RING * GT * GW + HOTS * GT * P, 2, P)
        wx = ring(A_G + RING * GT * GW + (HOTS + 2) * GT * P, 2, RW)
        loc = [sb(f"loc{i}", [P, GT]) for i in range(2)]
        zed = [sb(f"zed{i}", [P, 3, GT * HD]) for i in range(2)]
        den = sb("den", [P, 2, TS * HD])
        st2 = sb("st2", [P, TS, 6])
        mv2 = sb("mv2", [P, TS, 2])
        ln2 = sb("ln2", [P, 3, TS])
        rt = sb("rt", [P, 6, TS * NE])
        top = sb("top", [P, TS, 8])
        topi = sb("topi", [P, TS, 8], U32)
        topf = sb("topf", [P, TS, 8])
        rs = sb("rs", [P, 4, TS])
        comb = [sb(f"comb{i}", [P, TS, NE]) for i in range(2)]
        combT = arena[0:NE, A_X:A_X + TS * P].rearrange("p (t n) -> p t n", t=TS)

        turned = ps[:, 0:4, :].rearrange("p a (b m) -> p (a b) m", m=P)[:, 0:NB, :]

        s_const = sem("s_const")
        s_pad = sem("s_pad")
        s_w = sem("s_w")
        s_xl = sem("s_xl")
        s_edges = sem("s_edges")
        s_step = sem("s_step")
        s_once = sem("s_once")
        s_aonce = sem("s_aonce")
        s_xn = sem("s_xn")
        s_xTp = sem("s_xTp")
        s_xT = sem("s_xT")
        s_proj = sem("s_proj")
        s_kv = sem("s_kv")
        s_base = sem("s_base")
        s_tab = sem("s_tab")
        s_ksub = sem("s_ksub")
        s_kexp = sem("s_kexp")
        s_qTp = sem("s_qTp")
        s_qT = sem("s_qT")
        s_mixp = sem("s_mixp")
        s_arow = sem("s_arow")
        s_afin = sem("s_afin")
        s_key = sem("s_key")
        s_cnt = sem("s_cnt")
        s_turned = sem("s_turned")
        s_right = sem("s_right")
        s_gtd = sem("s_gtd")
        s_row = sem("s_row")
        s_srt = sem("s_srt")
        s_zero = sem("s_zero")
        s_kd = [sem(f"s_kd{i}") for i in range(RING)]
        s_gat = [sem(f"s_gat{i}") for i in range(RING)]
        s_loc = sem("s_loc")
        s_hot = sem("s_hot")
        s_hTp = sem("s_hTp")
        s_hT = sem("s_hT")
        s_el = sem("s_el")
        s_z = sem("s_z")
        s_e = sem("s_e")
        s_wx = sem("s_wx")
        s_agg = sem("s_agg")
        s_acc = sem("s_acc")
        s_ew = sem("s_ew")
        s_pd = sem("s_pd")
        s_pa = sem("s_pa")
        s_pp = sem("s_pp")
        s_yin = sem("s_yin")
        s_carry = sem("s_carry")
        s_carry_pool = sem("s_carry_pool")
        s_carry_sp = sem("s_carry_sp")
        s_h = sem("s_h")
        s_g = sem("s_g")
        s_y = sem("s_y")
        s_moe = sem("s_moe")
        s_out = [sem("s_out0"), sem("s_out1")]
        block = ctx.enter_context(nc.Block())

        at = {}

        def sl(i, n=1):
            return slice(i, i + n) if isinstance(i, int) else bass.ds(i, n)

        NW = 16
        PD = ["den", "rden", "avg", "bias", "neg", "elu", "x2", "stats", "mv", "rstd", "nmr", "lmax", "lsub", "lsum",
              "lrec", "prob", "top", "topi", "topf", "psum", "pmax", "prec", "w", "eq1", "c1", "eq2", "c2", "comb"] + [f"b2{u}" for u in range(4)]
        PA = ["eexp", "sd", "y"] + [f"yT{t}" for t in range(TS)] + ["lexp", "cTa", "cTb"]
        PP = [f"yTp{t}" for t in range(TS)] + ["logits", "cTpa", "cTpb"] + [f"b2p{u}" for u in range(4)]

        def count(names, st, name):
            return st * len(names) + names.index(name) + 1

        UNITS = [(0, 2), (2, 4), (4, 6), (6, 7)]
        NU = len(UNITS)

        def gathered(g, u):
            return (g - u) * (16 * GT // RING) + 16 * GT

        def loaded(g, u):
            return (g - u) * (16 // RING) + 16

        def blocks_of(eng, row, g):
            return nc.values_load_multi_w_load_instructions(
                trow[row:row + 1, sl(g, RING)], engines=[eng.engine], min_val=0, max_val=T - 1,
                skip_runtime_bounds_check_because="DVE clamps the block to T - 1 where it works the table out, and the rest of the row is zero")[1]

        @block.vector
        def _(dve):
            n = [0]

            def step(ins, name=None):
                ins.then_inc(s_step, 1)
                n[0] += 1
                if name:
                    at[name] = n[0]
                dve.wait_ge(s_step, n[0])

            dve.wait_ge(s_const, 4)
            step(dve.memset(eps_t[:, :], LN_EPS))
            step(dve.memset(ctxm[:, :], 0.0))
            step(dve.tensor_copy(lane[:, :], lane_i[:, :]))
            step(dve.tensor_scalar(nthr[:, :], lane[:, 0:T], -float(P), 0.5, ALU.mult, ALU.add))
            step(dve.tensor_reduce(sign7[:, :], ident[:, :].rearrange("p (a b) -> p a b", b=2)[:, :, 1], AX.X, ALU.add))
            step(dve.tensor_scalar(sign7[:, :], sign7[:, :], 2.0, -1.0, ALU.mult, ALU.add))
            step(dve.memset(el_all[:, :, HD:HD + 1], 1e30), "const")

            dve.wait_ge(s_once, 1)
            small = ps[:, 4, :]
            dve.tensor_copy(wT[:, :, :], small[0:C, 0:KC * P].rearrange("p (k n) -> p k n", k=KC))
            dve.tensor_copy(wlrT[:, :], small[0:C, KC * P:KC * P + 2 * HD])
            o = KC * P + 2 * HD
            dve.tensor_copy(rwT[:, :, :], small[:, o:o + KC * NE].rearrange("p (k e) -> p k e", k=KC))
            o += KC * NE
            dve.tensor_copy(b1_t[:, :, :], small[:, o:o + NE * KC].rearrange("p (e k) -> p e k", k=KC))
            o += NE * KC
            step(dve.tensor_copy(gpre_t[:, :], small[:, o:o + KC]), "small")
            for k in range(KC):
                step(dve.tensor_scalar(wcat[:, k, CQ:], wcat[:, k, CQ:], gpre_t[:, k:k + 1], None, ALU.mult))
            dve.wait_ge(s_once, 2)
            step(dve.tensor_copy(wcat[:, :, C:CQ], ps[:, 5, 0:KC * 2 * HD].rearrange("p (k h) -> p k h", k=KC)), "wcat")

            dve.wait_ge(s_xl, 16 * 5)
            for t in range(T):
                ins = dve.bn_stats(stats[:, t, :], base[:, t, :])
            step(ins)
            for t in range(T):
                ins = dve.bn_aggr(mv[:, t, :], stats[:, t, :])
            step(ins, "mv")
            dve.wait_ge(s_aonce, 1)
            step(dve.reciprocal(rstd[:, :], tmpT[:, :]))
            step(dve.scalar_tensor_tensor(out=nmr[:, :], in0=mv[:, :, 0], scalar=-1.0, in1=rstd[:, :], op0=ALU.mult, op1=ALU.mult), "nmr")
            step(dve.tensor_tensor(tmpT[:, :], mv[:, :, 1], rstd[:, :], ALU.mult))
            step(dve.tensor_tensor(tmpT[:, :], tmpT[:, :], rstd[:, :], ALU.mult), "norm2")
            dve.wait_ge(s_aonce, 2)
            step(dve.tensor_scalar(tmpT[:, :], tmpT[:, :], TINY, None, ALU.max))
            step(dve.reciprocal(rsc[:, :], tmpT[:, :]))
            step(dve.tensor_scalar(rsc[:, :], rsc[:, :], float(D) ** 0.5, None, ALU.mult), "rsc")

            dve.wait_ge(s_edges, 96)
            step(dve.tensor_scalar(right.bitcast(I32), src_i, NODE_BITS, KEY_BASE, ALU.logical_shift_left, ALU.bitwise_or))
            dve.tensor_tensor(keys[0].bitcast(I32), right.bitcast(I32), dst_i, ALU.bitwise_or).then_inc(s_key, 1)
            m, cur, done, entries = 1, 0, [1, 1], 0
            for kind, side, k, j in plan:
                a, b = keys[cur], keys[1 - cur]
                if (k, j) == (ROW_BITS, ROW_BITS - 1):
                    dve.wait_ge(s_key, m)
                    dve.tensor_scalar(b, a, sign7[:, 0:1], None, ALU.mult).then_inc(s_key, 1)
                    m += 1
                    done, cur = [m, m], 1 - cur
                    a, b = b, a
                if kind == "plain" and j >= 2 * ROW_BITS:
                    dve.wait_ge(s_key, m)
                    reads, lone = outer(a, 1 << (j - 2 * ROW_BITS), NB)
                    for (al, ah), (bl, bh) in zip(reads, outer(b, 1 << (j - 2 * ROW_BITS), NB)[0]):
                        dve.tensor_tensor(bl, al, ah, ALU.min).then_inc(s_key, 1)
                        dve.tensor_tensor(bh, al, ah, ALU.max).then_inc(s_key, 1)
                        m += 2
                    dve.tensor_copy(b[:, lone[0]:lone[1], :], a[:, lone[0]:lone[1], :]).then_inc(s_key, 1)
                    m += 1
                    done = [m, m]
                elif kind == "plain":
                    w = 1 << (j if side == "A" else j - ROW_BITS)
                    for h, part in enumerate(HALVES):
                        dve.wait_ge(s_key, done[h])
                        if side == "A" and k < ROW_BITS:
                            views = [(directed(a, w, 1 << (k - 1 - j), d, part), directed(b, w, 1 << (k - 1 - j), d, part), d) for d in range(2)]
                        else:
                            views = [(inner(a, w, part), inner(b, w, part), 1)]
                        for (al, ah), (bl, bh), up in views:
                            dve.tensor_tensor(bl, al, ah, ALU.min if up else ALU.max).then_inc(s_key, 1)
                            dve.tensor_tensor(bh, al, ah, ALU.max if up else ALU.min).then_inc(s_key, 1)
                            m += 2
                        done[h] = m
                else:
                    parts = ((0, NB),) if side == "B" and k > 2 * ROW_BITS else HALVES
                    for h, part in enumerate(parts):
                        entries += 1
                        dve.wait_ge(s_right, entries)
                        pairs, lone = enter_pairs(k, part, NB) if side == "B" else ([(lambda v: inner(v, P // 2, part), 0)], None)
                        for pick, sign in pairs:
                            left, rite, (bl, bh) = pick(turned)[0], pick(right)[1], pick(b)
                            for o_, op in ((bl, ALU.min), (bh, ALU.max)):
                                if sign == 0:
                                    dve.tensor_tensor(o_, left, rite, op).then_inc(s_key, 1)
                                else:
                                    x0, x1 = (left, rite) if sign > 0 else (rite, left)
                                    dve.scalar_tensor_tensor(out=o_, in0=x0, scalar=-1.0, in1=x1, op0=ALU.mult, op1=op).then_inc(s_key, 1)
                                m += 1
                        if lone:
                            dve.tensor_scalar(b[:, lone[0]:lone[1], :], turned[:, lone[0]:lone[1], :], float(lone[2]), None, ALU.mult).then_inc(s_key, 1)
                            m += 1
                        done[h] = m
                    if len(parts) == 1:
                        done = [m, m]
                cur = 1 - cur
                at[(kind, side, k, j)] = (list(done), cur)

            dve.wait_ge(s_once, 3)
            step(dve.tensor_scalar(starts[:, 0:T], ps[:, 5, 0:T], -0.5, NB * BLK * 0.5, ALU.mult, ALU.add))
            step(dve.memset(starts[:, T:T + 1], float(E)))
            step(dve.tensor_tensor(gtab[:, 0, :], starts[:, 1:T + 1], starts[:, 0:T], ALU.subtract))
            step(dve.tensor_scalar(gtab[:, 1, :], gtab[:, 0, :], float(GE - 1), None, ALU.add))
            step(dve.tensor_copy(gtab[:, 2, :].bitcast(I32), gtab[:, 1, :]))
            step(dve.tensor_scalar(gtab[:, 3, :].bitcast(I32), gtab[:, 2, :].bitcast(I32), GE.bit_length() - 1, None, ALU.logical_shift_right))
            step(dve.tensor_copy(gtab[:, 1, :], gtab[:, 3, :].bitcast(I32)))
            step(dve.tensor_tensor_scan(gtab[:, 2, :], ones[:, 0:T], gtab[:, 1, :], 0.0, ALU.mult, ALU.add))
            step(dve.tensor_copy(rowf[:, :], row_i[:, :]))
            step(dve.tensor_scalar(gidx[:, :], lane[:, 0:GC], rowf[:, 0:1], None, ALU.add))
            before = gsel[:, :, :]
            step(dve.tensor_tensor(before, bcast(gtab[:, 2, :], 1, GC), bcast(gidx[:, :], 2, T), ALU.is_le))
            step(dve.tensor_reduce(gsum[:, 0, :], before, AX.X, ALU.add))
            step(dve.tensor_tensor(before, before, bcast(gtab[:, 1, :], 1, GC), ALU.mult))
            step(dve.tensor_reduce(gsum[:, 1, :], before, AX.X, ALU.add))
            step(dve.tensor_tensor(before, bcast(gtab[:, 2, :], 1, GC), bcast(gidx[:, :], 2, T), ALU.is_le))
            step(dve.tensor_tensor(before, before, bcast(gtab[:, 0, :], 1, GC), ALU.mult))
            step(dve.tensor_reduce(gsum[:, 2, :], before, AX.X, ALU.add))
            step(dve.tensor_tensor(gidx[:, :], gidx[:, :], gsum[:, 1, :], ALU.subtract))
            step(dve.scalar_tensor_tensor(out=gsum[:, 2, :], in0=gidx[:, :], scalar=float(GE), in1=gsum[:, 2, :], op0=ALU.mult, op1=ALU.add))
            step(dve.tensor_scalar(gsum[:, 2, :], gsum[:, 2, :], float(E), 2.0, ALU.min, ALU.mult))
            step(dve.tensor_scalar(gsum[:, 0, :], gsum[:, 0, :], float(T - 1), None, ALU.min))
            step(dve.tensor_copy(gout[:, 0, :], gsum[:, 2, :]))
            step(dve.tensor_copy(gout[:, 1, :], gsum[:, 0, :]))
            step(dve.tensor_scalar(gsum[:, 3, :], gsum[:, 0, :], -float(P), None, ALU.mult), "groups")

            dve.wait_ge(s_key, m)
            dve.wait_ge(s_cnt, T)
            res, tmp = keys[cur], keys[1 - cur]
            step(dve.tensor_scalar(tmp.bitcast(I32), res.bitcast(I32), NODE_BITS, PAD_NODE, ALU.logical_shift_right, ALU.bitwise_and))
            step(dve.tensor_scalar(pair[:, :, :, 1].bitcast(I32), res.bitcast(I32), PAD_NODE, None, ALU.bitwise_and))
            step(dve.tensor_copy(pair[:, :, :, 0], tmp.bitcast(I32)), "pair")

            dve.wait_ge(s_kv, T)
            step(dve.tensor_reduce(kmaxp[:, :], kv[:, 0:T - 1, 0:HID].rearrange("p t c -> p c t"), AX.X, ALU.max))
            step(dve.tensor_tensor(kmaxp[0:TAIL, :], kmaxp[0:TAIL, :], kv[0:TAIL, T - 1, 0:HID], ALU.max), "kmaxp")
            dve.wait_ge(s_once, 4)
            step(dve.tensor_reduce(kmx[:, 0:1], ps[:, 0, 0:P], AX.X, ALU.max))
            step(dve.tensor_reduce(kmx[:, 1:2], mk_t[:, 0, :], AX.X, ALU.max))
            step(dve.tensor_tensor(kmx[:, 0:1], kmx[:, 0:1], kmx[:, 1:2], ALU.max))
            step(dve.tensor_scalar(kmx[:, 2:3], kmx[:, 0:1], -1.0, None, ALU.mult), "nkmx")
            dve.wait_ge(s_base, T)
            step(dve.tensor_scalar(kdiag[:, :], ident[:, :], kmx[:, 0:1], None, ALU.mult), "kdiag")
            dve.wait_ge(s_once, 5)
            step(dve.tensor_copy(kmaxb[:, :], ps[:, 1, 0:P]))
            for c in range(NS):
                kc = kv[:, TS * c:TS * c + TS, 0:HID]
                dve.tensor_tensor(kc, kc, bcast(kmaxb[:, :], 1, TS), ALU.subtract).then_inc(s_ksub, 1)
            q4 = q_all[:, :, :].rearrange("p t (h d) -> p (t h) d", h=MH)
            step(dve.tensor_reduce(qst[:, 0, :], q4, AX.X, ALU.max))
            step(dve.tensor_tensor(q4, q4, bcast(qst[:, 0, :], 2, MD), ALU.subtract), "qsub")
            dve.wait_ge(s_aonce, 4)
            step(dve.tensor_reduce(qst[:, 0, :], q4, AX.X, ALU.add))
            step(dve.reciprocal(qst[:, 1, :], qst[:, 0, :]))
            step(dve.tensor_tensor(q4, q4, bcast(qst[:, 1, :], 2, MD), ALU.mult), "q")
            dve.wait_ge(s_once, 6)
            step(dve.tensor_copy(memT[:, :, :], ps[0:MEM, 2, 0:2 * P].rearrange("p (a n) -> p a n", a=2)), "memT")
            dve.wait_ge(s_once, 7)
            for h in range(MH):
                r = slice(h * MD, h * MD + MD)
                ins = dve.tensor_scalar(ctxm[r, r], ps[r, 3, r], SCALE, None, ALU.mult)
            step(ins)
            step(dve.reciprocal(kmx[:, 3:4], ps[:, 4, 0:1]), "ctxm")
            dve.wait_ge(s_once, 8)
            step(dve.tensor_scalar(mixw[:, :], ps[:, 5, 0:D], kmx[:, 3:4], None, ALU.mult), "mixw")

            def att_row(i, u):
                dve.wait_ge(s_mixp, i + 1)
                dve.tensor_tensor(att[:, sl(i), :], ps[:, u:u + 1, 0:D], rows_b[:, 0:1, :], ALU.add).then_inc(s_arow, 1)
            run(dve, T, 2, 2, att_row)
            dve.wait_ge(s_arow, T)
            for t in range(T):
                if t:
                    dve.wait_ge(s_step, n[0])
                ins = dve.tensor_tensor_reduce(sq[:, :], att[:, t, :], att[:, t, :], 1.0, 0.0, ALU.mult, ALU.add, ss[:, t:t + 1])
                ins.then_inc(s_step, 1)
                n[0] += 1
            at["ss"] = n[0]
            dve.wait_ge(s_aonce, 5)
            step(dve.tensor_scalar(ss[:, :], ss[:, :], TINY, None, ALU.max))
            step(dve.reciprocal(tmpT[:, :], ss[:, :]))
            step(dve.tensor_scalar(tmpT[:, :], tmpT[:, :], float(D) ** 0.5, None, ALU.mult))

            def scale_row(i, u):
                dve.scalar_tensor_tensor(out=att[:, sl(i), :], in0=att[:, sl(i), :], scalar=tmpT[:, sl(i)],
                                         in1=rows_b[:, 1:2, :], op0=ALU.mult, op1=ALU.mult).then_inc(s_afin, 1)
            run(dve, T, 7, 0, scale_row)
            dve.wait_ge(s_afin, T)
            dve.wait_ge(s_base, T)
            step(dve.tensor_tensor(base[:, :, :], base[:, :, :], att, ALU.add), "att")

            dve.wait_ge(s_row, 64)

            home = [None]

            def logit(g, u, part):
                par = u % 2
                zz = [zed[par][:, k_, :].rearrange("p (c h) -> p c h", c=GT) for k_ in range(3)]
                pz = ps[:, 2 + par, 0:GT * (HD + 1)].rearrange("p (c h) -> p c h", c=GT)
                if part == 0:
                    dve.wait_ge(s_el, g + 1)
                    dve.wait_ge(s_gat[u], gathered(g, u))
                    dve.tensor_tensor(zz[0], pz[:, :, 0:HD], gat[u][:, :, C:GW], ALU.add).then_inc(s_z, 1)
                if part == 1:
                    dve.wait_ge(s_z, g * 3 + 1)
                    dve.scalar_tensor_tensor(out=zz[1], in0=zz[0], scalar=0.2, in1=zz[0], op0=ALU.mult, op1=ALU.max).then_inc(s_z, 1)
                if part == 2:
                    dve.wait_ge(s_z, g * 3 + 2)
                    dve.tensor_tensor(zz[2], pz[:, :, HD:HD + 1].broadcast_to([P, GT, HD]), zz[1], ALU.min).then_inc(s_z, 1)

            def one_hot(g, u):
                dve.wait_ge(s_loc, g + 1)
                after(dve, s_agg, g, HOTS)
                dve.tensor_tensor(hot[u % HOTS][:, :, :], bcast(lane[:, :], 1, GT), bcast(loc[u % 2][:, :], 2, P), ALU.is_equal).then_inc(s_hot, 1)

            def weigh(g, u):
                par = u % 2
                dve.wait_ge(s_e, g + 1)
                e4 = bcast(wx[par][:, :, D:RW], 3, C)
                x4 = bcast(gat[u][:, :, 0:C], 2, HD)
                dve.tensor_tensor(wx[par][:, :, 0:D].rearrange("p c (h d) -> p c h d", h=HD), x4, e4, ALU.mult).then_inc(s_wx, 1)

            def add_up(g, par, b):
                dve.wait_ge(s_agg, g + 1)
                if isinstance(g, int) and g == 0:
                    dve.wait_ge(s_zero, 1)
                after(dve, s_acc, g, 1)
                dve.tensor_tensor(acc[:, bass.ds(b, 1), :], ps[:, 4 + par:5 + par, 0:RW], acc[:, bass.ds(b, 1), :], ALU.add).then_inc(s_acc, 1)

            def group(g, u):
                now = g if isinstance(g, int) else NG // 2
                thinks = 2 <= now < NG + 2
                if u == 0:
                    home[0] = blocks_of(dve, 1, g)
                if thinks:
                    logit(g - 2, (u - 2) % RING, 0)
                if now < NG:
                    one_hot(g, u)
                if thinks:
                    logit(g - 2, (u - 2) % RING, 1)
                if 5 <= now < NG + 5:
                    add_up(g - 5, (u - 5) % 2, home[0][u])
                if thinks:
                    logit(g - 2, (u - 2) % RING, 2)
                if 3 <= now < NG + 3:
                    weigh(g - 3, (u - 3) % RING)
            run(dve, NG, RING, RING, group)
            for g in range(NG, NG + 5):
                group(g, g % RING)
            dve.wait_ge(s_acc, NG)

            def did(ins, st, name, plain=False):
                ins.then_inc(s_pd, 1)
                dve.wait_ge(s_pd, count(PD, st, name))
                if plain:
                    dve.sem_inc(s_carry, 1)

            def prepare(st, par, e):
                accs = acc[:, sl(st * TS, TS), :]
                rows = base[:, sl(st * TS, TS), :]
                m4 = mid.rearrange("p t (h d) -> p t h d", h=HD)
                dn = [den[:, k_, :].rearrange("p (t h) -> p t h", t=TS) for k_ in range(2)]
                r = [rt[:, k_, :].rearrange("p (t e) -> p t e", t=TS) for k_ in range(6)]
                lg = ps[:, 6, 0:TS * NE].rearrange("p (t e) -> p t e", t=TS)
                if e == 0:
                    did(dve.tensor_scalar(dn[0], accs[:, :, D:RW], TINY, None, ALU.max), st, "den")
                    did(dve.reciprocal(dn[1], dn[0]), st, "rden")
                    after(dve, s_yin, st, 1)
                    did(dve.tensor_tensor(m4, accs[:, :, 0:D].rearrange("p t (h d) -> p t h d", h=HD), bcast(dn[1], 3, C), ALU.mult), st, "avg")
                if e == 1:
                    m3 = mid.rearrange("p t (h d) -> p (t h) d", h=HD)
                    did(dve.tensor_tensor(m3, m3, bcast(gnnb_t[:, :], 1, TS * HD), ALU.add), st, "bias")
                    did(dve.tensor_scalar(low, mid, 0.0, None, ALU.min), st, "neg")
                    dve.wait_ge(s_pa, count(PA, st, "eexp"))
                    did(dve.scalar_tensor_tensor(out=mid, in0=mid, scalar=0.0, in1=low, op0=ALU.max, op1=ALU.add), st, "elu")
                    did(dve.scalar_tensor_tensor(out=rows, in0=mid, scalar=-1.0, in1=rows, op0=ALU.add, op1=ALU.add), st, "x2")
                if e == 2:
                    for t in range(TS):
                        ins = dve.bn_stats(st2[:, t, :], base[:, sl(st * TS + t), :])
                    did(ins, st, "stats", True)
                    for t in range(TS):
                        ins = dve.bn_aggr(mv2[:, t, :], st2[:, t, :])
                    did(ins, st, "mv")
                    dve.wait_ge(s_pa, count(PA, st, "sd"))
                    did(dve.reciprocal(ln2[:, 1, :], ln2[:, 0, :]), st, "rstd")
                    did(dve.scalar_tensor_tensor(out=ln2[:, 2, :], in0=mv2[:, :, 0], scalar=-1.0, in1=ln2[:, 1, :], op0=ALU.mult, op1=ALU.mult), st, "nmr")
                if e == 5:
                    dve.wait_ge(s_pp, count(PP, st, "logits"))
                    did(dve.tensor_reduce(rs[:, 0, :], lg, AX.X, ALU.max), st, "lmax")
                    did(dve.tensor_tensor(r[0], lg, bcast(rs[:, 0, :], 2, NE), ALU.subtract), st, "lsub")
                if e == 6:
                    dve.wait_ge(s_pa, count(PA, st, "lexp"))
                    did(dve.tensor_reduce(rs[:, 1, :], r[1], AX.X, ALU.add), st, "lsum")
                    did(dve.reciprocal(rs[:, 2, :], rs[:, 1, :]), st, "lrec")
                    did(dve.tensor_tensor(r[2], r[1], bcast(rs[:, 2, :], 2, NE), ALU.mult), st, "prob", True)
                    for t in range(TS):
                        ins = dve.max(top[:, t, :], r[2][:, t, :])
                    did(ins, st, "top", True)
                    for t in range(TS):
                        ins = dve.max_index(topi[:, t, :], top[:, t, :], r[2][:, t, :])
                    did(ins, st, "topi")
                    did(dve.tensor_copy(topf[:, :, 0:2], topi[:, :, 0:2]), st, "topf")
                    did(dve.tensor_tensor(rs[:, 3, :], top[:, :, 0], top[:, :, 1], ALU.add), st, "psum")
                    did(dve.tensor_scalar(rs[:, 3, :], rs[:, 3, :], TINY, None, ALU.max), st, "pmax")
                    did(dve.reciprocal(rs[:, 0, :], rs[:, 3, :]), st, "prec")
                    did(dve.tensor_tensor(top[:, :, 2:4], top[:, :, 0:2], bcast(rs[:, 0, :], 2, 2), ALU.mult), st, "w")
                    for c, (q0, q1) in enumerate((("eq1", "c1"), ("eq2", "c2"))):
                        did(dve.tensor_tensor(r[3 + c], bcast(lane[:, 0:NE], 1, TS), topf[:, :, c:c + 1].broadcast_to([P, TS, NE]), ALU.is_equal), st, q0)
                        did(dve.tensor_tensor(r[3 + c], r[3 + c], top[:, :, 2 + c:3 + c].broadcast_to([P, TS, NE]), ALU.mult), st, q1)
                    did(dve.tensor_tensor(comb[par][:, :, :], r[3], r[4], ALU.add), st, "comb")
                if e == 7:
                    dve.wait_ge(s_yin, st + 1)
                    for u, (t0, t1) in enumerate(UNITS):
                        dve.wait_ge(s_pp, count(PP, st, f"b2p{u}"))
                        tok = base[:, sl(st * TS + t0, t1 - t0), :]
                        did(dve.tensor_tensor(tok, ps[:, 6 + u % 2, 0:(t1 - t0) * D].rearrange("p (t c) -> p t c", c=D),
                                              tok, ALU.add), st, f"b2{u}")

            def gather_in(st, par, e, u):
                unit = (st * NE + e) * NU + u
                dve.wait_ge(s_y, unit + 1)
                if not (isinstance(unit, int) and unit < NU):
                    dve.wait_ge(s_moe, unit - NU + 1)
                t0, t1 = UNITS[u]
                for t in range(t0, t1):
                    tok = base[:, sl(st * TS + t), :]
                    ins = dve.scalar_tensor_tensor(out=tok, in0=ps[:, 4 + u % 2:5 + u % 2, (t - t0) * D:(t - t0 + 1) * D],
                                                   scalar=comb[par][:, t, e:e + 1], in1=tok, op0=ALU.mult, op1=ALU.add)
                ins.then_inc(s_moe, 1)

            def supertile(st, par, last=False):
                for e in range(NE):
                    if not last:
                        prepare(st + 1, 1 - par, e)
                    for u in range(NU):
                        gather_in(st, par, e, u)
            for e in range(NE):
                prepare(0, 0, e)
            run(dve, NS - 1, 2, 2, lambda st, par: supertile(st, par))
            supertile(NS - 1, (NS - 1) % 2, True)

        @block.tensor
        def _(pe):
            pe.wait_ge(s_const, 4)
            pe.wait_ge(s_w, 16 * NW)
            small = ps[:, 4, :]
            for k in range(KC):
                pe.transpose(small[0:C, k * P:k * P + P], wcat[:, k, 0:C], ident[:, :])
            o = KC * P
            pe.transpose(small[0:C, o:o + 2 * HD], wlr[:, :], ident[0:2 * HD, 0:2 * HD])
            o += 2 * HD
            for k in range(KC):
                pe.transpose(small[:, o:o + NE], rw_s[:, k * P:k * P + P], ident[0:NE, 0:NE])
                o += NE
            pe.transpose(small[:, o:o + NE * KC], b1_r[:, :], ident[0:NE * KC, 0:NE * KC])
            o += NE * KC
            pe.transpose(small[:, o:o + KC], gpre_r[:, :], ident[0:KC, 0:KC]).then_inc(s_once, 1)
            pe.wait_ge(s_step, at["small"])
            for k in range(KC):
                ins = pe.matmul(ps[:, 5, k * 2 * HD:(k + 1) * 2 * HD], wT[:, k, :], wlrT[:, :], start=True, stop=True)
            ins.then_inc(s_once, 1)
            pe.wait_ge(s_step, at["wcat"])

            def turn_x(i, u):
                pe.wait_ge(s_xn, i + 1)
                after(pe, s_xT, i, 2)
                for k in range(KC):
                    ins = pe.transpose(ps[:, 4 + u, k * P:k * P + P], xn[u][:, k * P:k * P + P], ident[:, :])
                ins.then_inc(s_xTp, 1)

            def project(i, u):
                pe.wait_ge(s_xT, i + 1)
                after(pe, s_kv, i, 2)
                for k in range(KC):
                    ins = pe.matmul(ps[:, 6 + u, 0:CQ + 3 * HID], xnT[u][:, k, :], wcat[:, k, :], start=(k == 0), stop=(k == KC - 1))
                ins.then_inc(s_proj, 1)

            def tile(i, u):
                turn_x(i, u)
                if not (isinstance(i, int) and i == 0):
                    project(i - 1, 1 - u)
            run(pe, T, 2, 4, tile)
            project(T - 1, (T - 1) % 2)

            for i, (_, side, k, j) in enters:
                done, cur = at[plan[i - 1]]
                for h, part in enumerate(HALVES):
                    pe.wait_ge(s_key, done[h])
                    for t in range(*part):
                        ins = pe.transpose(turned[:, t, :], keys[cur][:, t, :], ident[:, :])
                    ins.then_inc(s_turned, 1)

            pe.wait_ge(s_cnt, T)
            pe.matmul(ps[:, 5, 0:T], ones[:, :], cnt[:, :], start=True, stop=True).then_inc(s_once, 1)
            pe.wait_ge(s_step, at["kmaxp"])
            pe.transpose(ps[:, 0, 0:P], kmaxp[:, :], ident[:, :]).then_inc(s_once, 1)
            pe.wait_ge(s_step, at["kdiag"])
            pe.matmul(ps[:, 1, 0:P], ones[:, :], kdiag[:, :], start=True, stop=True).then_inc(s_once, 1)
            pe.wait_ge(s_aonce, 3)
            pe.transpose(ps[0:MEM, 2, 0:P], mexp[:, :], ident[:, :])
            pe.transpose(ps[0:MEM, 2, P:2 * P], mk_t[:, 1, :], ident[:, :]).then_inc(s_once, 1)
            for t in range(T):
                if t % TS == 0:
                    pe.wait_ge(s_kexp, t // TS + 1)
                r = slice(0, P if t < T - 1 else TAIL)
                pe.matmul(ps[:, 3, 0:HID], kv[r, t, HID:2 * HID], kv[r, t, 0:HID], start=(t == 0), stop=False)
                pe.matmul(ps[:, 4, 0:1], kv[r, t, 0:HID], ones[r, 0:1], start=(t == 0), stop=False)
            pe.wait_ge(s_step, at["memT"])
            pe.matmul(ps[:, 3, 0:HID], memT[:, 1, :], memT[:, 0, :], start=False, stop=True)
            pe.matmul(ps[:, 4, 0:1], memT[:, 0, :], ones[0:MEM, 0:1], start=False, stop=True).then_inc(s_once, 1)
            pe.wait_ge(s_step, at["ctxm"])
            pe.matmul(ps[:, 5, 0:D], ctxm[:, :], wout_s[:, :], start=True, stop=True).then_inc(s_once, 1)
            pe.wait_ge(s_step, at["mixw"])
            pe.wait_ge(s_step, at["q"])

            def turn_q(i, u):
                after(pe, s_qT, i, 2)
                pe.transpose(ps[:, 6 + u:7 + u, 0:P], q_all[:, i, :] if isinstance(i, int) else q_all[:, sl(i), :], ident[:, :]).then_inc(s_qTp, 1)

            def mix(i, u):
                pe.wait_ge(s_qT, i + 1)
                after(pe, s_arow, i, 2)
                pe.matmul(ps[:, u, 0:D], qT[u], mixw[:, :], start=True, stop=True).then_inc(s_mixp, 1)

            for t in range(T):
                turn_q(t, t % 2)
                if t:
                    mix(t - 1, (t - 1) % 2)
            mix(T - 1, (T - 1) % 2)

            pe.wait_ge(s_row, 64)

            def turn_hot(g, u):
                par = u % 2
                pe.wait_ge(s_hot, g + 1)
                after(pe, s_hT, g, 2)
                for c in range(GT):
                    ins = pe.transpose(ps[:, par, c * P:c * P + P], hot[u % HOTS][:, c, :], ident[:, :])
                ins.then_inc(s_hTp, 1)

            def aggregate(g, u):
                par = u % 2
                pe.wait_ge(s_wx, g + 1)
                after(pe, s_acc, g, 2)
                for c in range(GT):
                    ins = pe.matmul(ps[:, 4 + par, 0:RW], hot[u % HOTS][:, c, :], wx[par][:, c, :], start=(c == 0), stop=(c == GT - 1))
                ins.then_inc(s_agg, 1)

            home = [None]

            def spread_el(g, u, b):
                par = u % 2
                pe.wait_ge(s_hT, g + 1)
                after(pe, s_z, g, 2, 3)
                for c in range(GT):
                    ins = pe.matmul(ps[:, 2 + par, c * (HD + 1):(c + 1) * (HD + 1)], hotT[par][:, c, :],
                                    el_all[:, bass.ds(b, 1), :].rearrange("p a h -> p (a h)"), start=True, stop=True)
                ins.then_inc(s_el, 1)

            def group(g, u):
                now = g if isinstance(g, int) else NG // 2
                if u == 0:
                    home[0] = blocks_of(pe, 2, g)
                if 4 <= now < NG + 4:
                    aggregate(g - 4, (u - 4) % RING)
                if 1 <= now < NG + 1:
                    spread_el(g - 1, (u - 1) % RING, home[0][u])
                if now < NG:
                    turn_hot(g, u)
            run(pe, NG, RING, RING, group)
            for g in range(NG, NG + 4):
                group(g, g % RING)

            def prepare(st, par, e):
                if e == 4:
                    pe.wait_ge(s_pa, count(PA, st, "y"))
                    after(pe, s_pd, st, 1, len(PD))
                    for t in range(TS):
                        if t >= 2:
                            pe.wait_ge(s_pa, count(PA, st, f"yT{t - 2}"))
                        for k in range(KC):
                            ins = pe.transpose(ps[:, 6 + t % 2, k * P:k * P + P], mid[:, t, k * P:k * P + P], ident[:, :])
                        ins.then_inc(s_pp, 1)
                if e == 5:
                    pe.wait_ge(s_pa, count(PA, st, f"yT{TS - 1}"))
                    for t in range(TS):
                        for k in range(KC):
                            ins = pe.matmul(ps[:, 6, t * NE:(t + 1) * NE], yT[par][:, k, t * P:t * P + P], rwT[:, k, :], start=(k == 0), stop=(k == KC - 1))
                    ins.then_inc(s_pp, 1)
                if e == 7:
                    pe.wait_ge(s_pd, count(PD, st, "comb"))
                    for t in range(4):
                        ins = pe.transpose(ps[0:NE, 7, t * P:t * P + P], comb[par][:, t, :], ident[:, :])
                    ins.then_inc(s_pp, 1)
                    for t in range(4, TS):
                        ins = pe.transpose(ps[0:NE, 6, (t - 4) * P:(t - 3) * P], comb[par][:, t, :], ident[:, :])
                    ins.then_inc(s_pp, 1)
                    for u, (t0, t1) in enumerate(UNITS):
                        if u == 0:
                            pe.wait_ge(s_pa, count(PA, st, "cTb"))
                        if u >= 2:
                            pe.wait_ge(s_pd, count(PD, st, f"b2{u - 2}"))
                        for t in range(t0, t1):
                            ins = pe.matmul(ps[:, 6 + u % 2, (t - t0) * D:(t - t0 + 1) * D], combT[:, t, :], b2_s[:, :], start=True, stop=True)
                        ins.then_inc(s_pp, 1)

            def hidden(st, par, e):
                for f in range(KC):
                    for c in range(2):
                        bank = (st * NE + e) * 4 + f * 2 + c
                        after(pe, s_g, bank, 4)
                        for k in range(KC):
                            ins = pe.matmul(ps[:, f * 2 + c, 0:HALFT], w1_s[:, e, k, f * P:f * P + P],
                                            yT[par][:, k, c * HALFT:(c + 1) * HALFT], start=(k == 0), stop=(k == KC - 1))
                        ins.then_inc(s_h, 1)

            def outward(st, par, e):
                pe.wait_ge(s_g, (st * NE + e) * 4 + 4)
                for u, (t0, t1) in enumerate(UNITS):
                    unit = (st * NE + e) * NU + u
                    after(pe, s_moe, unit, 2)
                    for t in range(t0, t1):
                        for k in range(KC):
                            ins = pe.matmul(ps[:, 4 + u % 2, (t - t0) * D:(t - t0 + 1) * D], hT[e % 2][:, k, t * P:t * P + P],
                                            w2_s[:, e, k, :], start=(k == 0), stop=(k == KC - 1))
                    ins.then_inc(s_y, 1)

            def supertile(st, par, last=False):
                for e in range(NE):
                    if not last:
                        prepare(st + 1, 1 - par, e)
                    if e < NE - 1:
                        hidden(st, par, e + 1)
                    elif not last:
                        hidden(st + 1, 1 - par, 0)
                    outward(st, par, e)
            for e in range(NE):
                prepare(0, 0, e)
            pe.wait_ge(s_ew, 32 * NE)
            hidden(0, 0, 0)
            run(pe, NS - 1, 2, 2, lambda st, par: supertile(st, par))
            supertile(NS - 1, (NS - 1) % 2, True)

        @block.scalar
        def _(act):
            act.wait_ge(s_step, at["mv"])
            act.activation(tmpT[:, :], mv[:, :, 1], ACT.Sqrt, bias=eps_t[:, 0:1]).then_inc(s_aonce, 1)
            act.wait_ge(s_step, at["norm2"])
            act.activation(tmpT[:, :], tmpT[:, :], ACT.Sqrt, scale=float(D)).then_inc(s_aonce, 1)
            act.wait_ge(s_step, at["rsc"])

            def normalise(i, u):
                after(act, s_xTp, i, 2)
                after(act, s_base, i, 2)
                act.activation(xn[u][:, :], base[:, i, :] if isinstance(i, int) else base[:, sl(i), :].rearrange("p a c -> p (a c)"),
                               ACT.Identity, bias=nmr[:, sl(i)], scale=rstd[:, sl(i)]).then_inc(s_xn, 1)

            def copy_xT(i, u):
                act.wait_ge(s_xTp, i + 1)
                after(act, s_proj, i, 2)
                act.activation(xnT[u][:, :, :], ps[:, 4 + u, 0:D].rearrange("p (k n) -> p k n", k=KC), ACT.Copy).then_inc(s_xT, 1)

            def store(i, u):
                act.wait_ge(s_proj, i + 1)
                proj = ps[:, 6 + u:7 + u, :]
                act.activation(tb[:, sl(i), :], proj[:, :, 0:GW], ACT.Copy)
                act.activation(el_all[:, sl(i), 0:HD], proj[:, :, GW:CQ], ACT.Copy)
                act.activation(q_all[:, sl(i), :], proj[:, :, CQ:CQ + HID], ACT.Copy, scale=rsc[:, sl(i)])
                act.activation(kv[:, sl(i), :], proj[:, :, CQ + HID:CQ + 3 * HID], ACT.Copy, scale=rsc[:, sl(i)]).then_inc(s_kv, 1)

            def tile(i, u):
                now = i if isinstance(i, int) else T // 2
                if now < T:
                    normalise(i, u)
                if 1 <= now < T + 1:
                    copy_xT(i - 1, 1 - u)
                if 2 <= now:
                    store(i - 2, u)
            run(act, T, 2, 2, tile)
            tile(T, T % 2)
            tile(T + 1, (T + 1) % 2)

            def count_sources(blocks):
                for b in blocks:
                    if b:
                        act.wait_ge(s_cnt, b)
                    act.activation(junk, src_i, ACT.Sign, bias=nthr[:, b:b + 1], accum_out=cnt[:, b:b + 1]).then_inc(s_cnt, 1)

            act.wait_ge(s_edges, 96)
            turns = 0
            counted, share = 0, -(-T // (len(enters) // 2))
            for i, (_, side, k, j) in enters:
                parts = ((0, NB),) if side == "B" and k > 2 * ROW_BITS else HALVES
                for part in parts:
                    turns += 2 // len(parts)
                    act.wait_ge(s_turned, turns)
                    pairs = enter_pairs(k, part, NB)[0] if side == "B" else [(lambda v: inner(v, P // 2, part), 0)]
                    for pick, _ in pairs:
                        ins = act.activation(pick(right)[1], pick(turned)[1], ACT.Copy)
                    ins.then_inc(s_right, 1)
                if side == "A":
                    count_sources(range(counted, min(T, counted + share)))
                    counted = min(T, counted + share)

            act.wait_ge(s_step, at["nkmx"])
            act.activation(mexp[:, :], mk_t[:, 0, :], ACT.Exp, bias=kmx[:, 2:3]).then_inc(s_aonce, 1)
            for c in range(NS):
                act.wait_ge(s_ksub, c + 1)
                kc = kv[:, TS * c:TS * c + TS, 0:HID]
                act.activation(kc, kc, ACT.Exp).then_inc(s_kexp, 1)
            act.wait_ge(s_step, at["qsub"])
            act.activation(q_all[:, :, :], q_all[:, :, :], ACT.Exp).then_inc(s_aonce, 1)

            def copy_qT(i, u):
                act.wait_ge(s_qTp, i + 1)
                after(act, s_mixp, i, 2)
                act.activation(qT[u], ps[:, 6 + u, 0:P], ACT.Copy).then_inc(s_qT, 1)
            run(act, T, 2, 2, copy_qT)
            act.wait_ge(s_step, at["ss"])
            act.activation(ss[:, :], ss[:, :], ACT.Sqrt).then_inc(s_aonce, 1)

            act.wait_ge(s_srt, 16)
            act.wait_ge(s_tab, 16)
            act.wait_ge(s_step, at["pair"])
            for e in range(NE):
                act.dma_start(w1_s[:, e, :, :], w1[e].rearrange("(k p) f -> p k f", p=P)).then_inc(s_ew, 16)
                act.dma_start(w2_s[:, e, :, :], w2[e].rearrange("(k p) f -> p k f", p=P)).then_inc(s_ew, 16)

            def weights(g, u):
                par = u % 2
                act.wait_ge(s_z, g * 3 + 3)
                after(act, s_agg, g, 2)
                act.activation(wx[par][:, :, D:RW], zed[par][:, 2, :].rearrange("p (c h) -> p c h", c=GT), ACT.Exp).then_inc(s_e, 1)

            def copy_hot(g, u):
                par = u % 2
                act.wait_ge(s_hTp, g + 1)
                after(act, s_el, g, 2)
                act.activation(hotT[par][:, :, :], ps[:, par, 0:GT * P].rearrange("p (c n) -> p c n", c=GT), ACT.Copy).then_inc(s_hT, 1)

            def locate(g, u):
                act.wait_ge(s_kd[u], loaded(g, u))
                after(act, s_hot, g, 2)
                act.activation(loc[u % 2][:, :], kd[u][:, :, 0], ACT.Identity, bias=bases[:, sl(g)]).then_inc(s_loc, 1)

            def group(g, u):
                now = g if isinstance(g, int) else NG // 2
                if now < NG:
                    locate(g, u)
                if 1 <= now < NG + 1:
                    copy_hot(g - 1, (u - 1) % RING)
                if 3 <= now < NG + 3:
                    weights(g - 3, (u - 3) % RING)
            act.wait_ge(s_row, 64)
            run(act, NG, RING, RING, group)
            for g in range(NG, NG + 3):
                group(g, g % RING)

            def did(ins):
                ins.then_inc(s_pa, 1)

            def prepare(st, par, e):
                if e == 1:
                    act.wait_ge(s_pd, count(PD, st, "neg"))
                    did(act.activation(low, low, ACT.Exp))
                if e == 2:
                    act.wait_ge(s_pd, count(PD, st, "mv"))
                    did(act.activation(ln2[:, 0, :], mv2[:, :, 1], ACT.Sqrt, bias=eps_t[:, 0:1]))
                if e == 3:
                    act.wait_ge(s_pd, count(PD, st, "nmr"))
                    for t in range(TS):
                        ins = act.activation(mid[:, t:t + 1, :], base[:, sl(st * TS + t), :], ACT.Identity, bias=ln2[:, 2, t:t + 1], scale=ln2[:, 1, t:t + 1])
                    did(ins)
                if e == 4:
                    for t in range(TS):
                        act.wait_ge(s_pp, count(PP, st, f"yTp{t}"))
                        did(act.activation(yT[par][:, :, t * P:t * P + P], ps[:, 6 + t % 2, 0:D].rearrange("p (k n) -> p k n", k=KC), ACT.Copy))
                if e == 5:
                    act.wait_ge(s_pd, count(PD, st, "lsub"))
                    did(act.activation(rt[:, 1, :], rt[:, 0, :], ACT.Exp))
                if e == 7:
                    act.wait_ge(s_pp, count(PP, st, "cTpa"))
                    did(act.activation(combT[:, 0:4, :], ps[0:NE, 7, :].rearrange("p (t n) -> p t n", t=4), ACT.Copy))
                    act.wait_ge(s_pp, count(PP, st, "cTpb"))
                    did(act.activation(combT[:, 4:TS, :], ps[0:NE, 6, 0:(TS - 4) * P].rearrange("p (t n) -> p t n", t=TS - 4), ACT.Copy))

            def gelus(st, par, e):
                last_unit = (st * NE + e - 1) * NU
                if not (isinstance(last_unit, int) and last_unit <= 0):
                    act.wait_ge(s_y, last_unit)
                for f in range(KC):
                    for c in range(2):
                        act.wait_ge(s_h, (st * NE + e) * 4 + f * 2 + c + 1)
                        act.activation(hT[e % 2][:, f, c * HALFT:(c + 1) * HALFT], ps[:, f * 2 + c, 0:HALFT], ACT.Gelu,
                                       bias=b1_t[:, e, f:f + 1]).then_inc(s_g, 1)

            def supertile(st, par, last=False):
                for e in range(NE):
                    if not last:
                        prepare(st + 1, 1 - par, e)
                    if e < NE - 1:
                        gelus(st, par, e + 1)
                    elif not last:
                        gelus(st + 1, 1 - par, 0)
            for e in range(NE):
                prepare(0, 0, e)
            gelus(0, 0, 0)
            run(act, NS - 1, 2, 2, lambda st, par: supertile(st, par))
            supertile(NS - 1, (NS - 1) % 2, True)

        @block.gpsimd
        def _(pool):
            pool.memset(src_i[:, NB - 1, :], PAD_NODE).then_inc(s_pad, 1)
            pool.memset(dst_i[:, NB - 1, :], 0).then_inc(s_pad, 1)
            pool.memset(trow[:, :], 0).then_inc(s_pad, 1)
            pool.memset(base[:, T - 1, :], 0.0).then_inc(s_pad, 1)
            pool.memset(ident[:, :], 0.0).then_inc(s_pad, 1)
            pool.memset(ones[:, :], 1.0).then_inc(s_const, 1)
            pool.iota(lane_i[:, :], [[1, P]], base=0, channel_multiplier=0).then_inc(s_const, 1)
            pool.iota(row_i[:, :], [[1, 1]], base=0, channel_multiplier=GC).then_inc(s_const, 1)
            pool.wait_ge(s_pad, 5)
            pool.affine_select(out=ident[:, :], in_=ident[:, :], compare_op=ALU.not_equal, fill=1.0, base=0,
                               pattern=[[-1, P]], channel_multiplier=1).then_inc(s_const, 1)

            def add_x(i, u):
                pool.wait_ge(s_xn, i + 1)
                b = base[:, sl(i), :]
                pool.tensor_tensor(b, b, xn[u][:, :].unsqueeze(1), ALU.add).then_inc(s_base, 1)
            run(pool, T, 2, 2, add_x)
            pool.wait_ge(s_tab, 16)

            def gather(g, u):
                pool.wait_ge(s_kd[u], loaded(g, u))
                after(pool, s_wx, g, RING)
                pool.sem_inc(s_carry_pool, 1)
                for c in range(GT):
                    pool.indirect_dma_start(gat[u][:, c, :], None, table_d,
                                            bass.IndirectOffsetOnAxis(ap=kd[u][:, c, 1:2].bitcast(I32), axis=0)).then_inc(s_gat[u], 16)
                if isinstance(g, int) and g == RING - 1:
                    pool.wait_ge(s_step, at["att"])
                    pool.memset(big[:, :], 0.0).then_inc(s_zero, 1)
            run(pool, NG, RING, RING, gather)

            def seed(st, par):
                pool.wait_ge(s_pa, count(PA, st, "y"))
                tok = base[:, sl(st * TS, TS), :]
                pool.tensor_tensor(tok, tok, mid, ALU.add).then_inc(s_yin, 1)
            run(pool, NS, 2, 2, seed)

        @block.sync
        def _(sp):
            loads = [(wcat[:, k, 0:C], W[k * P:k * P + P, :]) for k in range(KC)]
            loads += [(wcat[:, k, CQ:], w_qkv[k * P:k * P + P, :]) for k in range(KC)]
            loads += [(wlr[0:HD, :], Wr), (wlr[HD:2 * HD, :], Wl), (rw_s[:, :], router_w), (wout_s[:, :], w_out), (b2_s[:, :], b2)]
            loads += [(b1_r[:, :], b1.rearrange("e (k p) -> (e k) p", p=P)), (gpre_r[:, :], g_pre.rearrange("(k p) -> k p", p=P))]
            loads += [(mk_t[:, a, :], mem_kv[a].rearrange("h d m -> (h d) m")) for a in range(2)]
            for dst_, src_ in loads:
                sp.dma_start(dst_, src_).then_inc(s_w, 16)
            sp.dma_start(rows_b[:, 0, :], b_out.partition_broadcast(P)).then_inc(s_w, 16)
            sp.dma_start(rows_b[:, 1, :], g_out.partition_broadcast(P)).then_inc(s_w, 16)
            sp.dma_start(gnnb_t[:, :], gnn_b.partition_broadcast(P)).then_inc(s_w, 16)
            sp.wait_ge(s_pad, 5)
            xm = x[0:(T - 1) * P, :].rearrange("(t p) c -> p t c", p=P)
            for c in range(4):
                sp.dma_start(base[:, 12 * c:12 * c + 12, :], xm[:, 12 * c:12 * c + 12, :]).then_inc(s_xl, 16)
            sp.dma_start(base[0:TAIL, T - 1, :], x[(T - 1) * P:N, :]).then_inc(s_xl, 16)
            for buf, d in ((src_i, src), (dst_i, dst)):
                sp.dma_start(buf[:, 0:NB - 1, :], d[0:FULL].rearrange("(t m l) -> m t l", m=P, l=P)).then_inc(s_edges, 16)
                sp.dma_start(buf[0:ROWS, NB - 1, :], d[FULL:FULL + ROWS * P].rearrange("(m l) -> m l", l=P)).then_inc(s_edges, 16)
                sp.dma_start(buf[ROWS:ROWS + 1, NB - 1, 0:REST], d[FULL + ROWS * P:E].rearrange("(m l) -> m l", m=1)).then_inc(s_edges, 16)
            sp.wait_ge(s_kv, T)
            sp.dma_start(table_d.rearrange("(t p) c -> p t c", p=P), tb).then_inc(s_tab, 16)
            sp.wait_ge(s_step, at["groups"])
            sp.dma_start(groups_d.rearrange("a (p c) -> p a c", c=GC), gout[:, :, :]).then_inc(s_gtd, 16)
            sp.dma_start(bases_d.rearrange("(p c) -> p c", c=GC), gsum[:, 3, :]).then_inc(s_gtd, 16)
            sp.wait_ge(s_gtd, 32)
            sp.dma_start(trow[0:1, 0:P * GC], groups_d[0:1, :]).then_inc(s_row, 16)
            sp.dma_start(trow[1:2, DLAG:DLAG + P * GC], groups_d[1:2, :]).then_inc(s_row, 16)
            sp.dma_start(trow[2:3, PLAG:PLAG + P * GC], groups_d[1:2, :]).then_inc(s_row, 16)
            sp.dma_start(bases[:, :], bases_d.partition_broadcast(P)).then_inc(s_row, 16)
            sp.wait_ge(s_step, at["pair"])
            sp.dma_start(sorted_d.rearrange("(t m c) -> m t c", m=P, c=2 * P), pair.rearrange("p t l c -> p t (l c)")).then_inc(s_srt, 16)
            sp.wait_ge(s_srt, 16)
            sp.wait_ge(s_row, 64)

            def load_group(g, u):
                first = sp.value_load(trow[0:1, sl(g)], min_val=0, max_val=E * 2)
                if not (isinstance(g, int) and g < RING):
                    sp.wait_ge(s_loc, g - RING + 1)
                    sp.wait_ge(s_gat[u], gathered(g, u) - 16 * GT)
                    sp.sem_inc(s_carry_sp, 1)
                sp.dma_start(kd[u][:, :, :].rearrange("p c a -> p (c a)"),
                             sorted_d[bass.ds(first, GE * 2)].rearrange("(p c) -> p c", p=P)).then_inc(s_kd[u], 16)
            run(sp, NG, RING, RING, load_group)

            def store(st, par):
                sp.wait_ge(s_moe, (st + 1) * (NE * NU))
                rows = out[0:(T - 1) * P, :].rearrange("(t p) c -> p t c", p=P)
                if isinstance(st, int) and st == NS - 1:
                    sp.dma_start(rows[:, TS * st:T - 1, :], base[:, TS * st:T - 1, :]).then_inc(s_out[par], 16)
                    sp.dma_start(out[(T - 1) * P:N, :], base[0:TAIL, T - 1, :]).then_inc(s_out[par], 16)
                else:
                    sp.dma_start(rows[:, sl(st * TS, TS), :], base[:, sl(st * TS, TS), :]).then_inc(s_out[par], 16)
            run(sp, NS - 1, 2, 2, store)
            store(NS - 1, (NS - 1) % 2)
            sp.wait_ge(s_out[0], 16 * ((NS + 1) // 2 + 1))
            sp.wait_ge(s_out[1], 16 * (NS // 2))


_INS = ["x", "src", "dst", "L0_gnn_W", "L0_gnn_Wl", "L0_gnn_Wr", "L0_gnn_b", "L0_mix_w_qkv", "L0_mix_mem_kv", "L0_mix_w_out",
        "L0_mix_b_out", "L0_mix_g_out", "L0_mix_g_pre", "L0_ffn_router_w", "L0_ffn_w1", "L0_ffn_b1", "L0_ffn_w2", "L0_ffn_b2"]
_OUTS = [((6250, 256), "float32")]


def kernel(**inputs):
    import numpy as _np
    import concourse.bacc as _bacc
    from concourse import mybir as _mybir
    from concourse.bass_utils import run_bass_kernel_spmd as _run

    nc = _bacc.Bacc("TRN2", target_bir_lowering=False, num_devices=1)
    arrays, args = {}, []
    for name in _INS:
        a = _np.ascontiguousarray(inputs[name])
        arrays[f"in_{name}_dram"] = a
        args.append(nc.dram_tensor(f"in_{name}_dram", a.shape, _mybir.dt.from_np(a.dtype), kind="ExternalInput").ap())
    for i, (shape, dtype) in enumerate(_OUTS):
        dt = _mybir.dt.from_np(_np.dtype(dtype))
        args.append(nc.dram_tensor(f"out_{i}_dram", shape, dt, kind="ExternalOutput").ap())
    gps_layer(nc, *args)
    r = _run(nc, [arrays], core_ids=[0])
    return r.results[0]["out_0_dram"]
```

```python
import concourse.bass as bass
from concourse import mybir
from contextlib import ExitStack

ALU = mybir.AluOpType
ACT = mybir.ActivationFunctionType
AX = mybir.AxisListType
F32 = mybir.dt.float32
I32 = mybir.dt.int32
U32 = mybir.dt.uint32

P = 128
LN_EPS = 1e-5
TINY = 1e-12

ROW_BITS = 7
NODE_BITS = 13
PAD_NODE = (1 << NODE_BITS) - 1
KEY_BASE = 0x20000000


def make_plan(levels):
    plan = []
    for k in range(1, ROW_BITS + 1):
        plan += [("plain", "A", k, j) for j in range(k - 1, -1, -1)]
    for k in range(ROW_BITS + 1, levels + 1):
        plan.append(("enter", "B", k, k - 1))
        plan += [("plain", "B", k, j) for j in range(k - 2, ROW_BITS - 1, -1)]
        plan.append(("enter", "A", k, ROW_BITS - 1))
        plan += [("plain", "A", k, j) for j in range(ROW_BITS - 2, -1, -1)]
    return plan


def inner(x, w, part):
    v = x[:, part[0]:part[1], :].rearrange("p t (g b l) -> p (t g) b l", b=2, l=w)
    return v[:, :, 0, :], v[:, :, 1, :]


def directed(x, w, a, d, part):
    v = x[:, part[0]:part[1], :].rearrange("p t (g d a b l) -> p (t g) d a b l", d=2, a=a, b=2, l=w)
    return v[:, :, d, :, 0, :], v[:, :, d, :, 1, :]


def outer(x, u, nb):
    n = nb // (2 * u) * (2 * u)
    pairs = []
    if n:
        v = x[:, 0:n, :].rearrange("p (q b u) m -> p q b (u m)", b=2, u=u)
        pairs.append((v[:, :, 0, :], v[:, :, 1, :]))
    left = nb - n - u
    if left > 0:
        pairs.append((x[:, n:n + left, :], x[:, n + u:nb, :]))
        return pairs, (n + left, n + u)
    return pairs, (n, nb)


def enter_pairs(k, part, nb):
    top = ROW_BITS * 2
    if k < top:
        return [(lambda x, d=d: directed(x, 1 << (k - ROW_BITS - 1), 1, d, part), 2 * d - 1) for d in range(2)], None
    if k == top:
        last = nb - 1
        end = min(part[1], last)
        res = []
        for d in range(2):
            first = part[0] + (part[0] + d) % 2
            res.append((lambda x, s=first: tuple(x[:, s:end:2, c * 64:c * 64 + 64] for c in range(2)), 2 * d - 1))
        if part[1] == nb:
            res.append((lambda x: tuple(x[:, last:nb, c * 64:c * 64 + 64] for c in range(2)), 1))
        return res, None
    if k == top + 1:
        def pick(x, d):
            v = x[:, 0:12, :].rearrange("p (q d b) m -> p q d b m", d=2, b=2)
            return v[:, :, d, 0, :], v[:, :, d, 1, :]
        return [(lambda x, d=d: pick(x, d), 2 * d - 1) for d in range(2)], (12, 13, 1)
    if k == top + 2:
        return [(lambda x, q=q: (x[:, 4 * q:4 * q + 2, :], x[:, 4 * q + 2:4 * q + 4, :]), 1 if q == 1 else -1)
                for q in range(3)], (12, 13, 1)
    if k == top + 3:
        return [(lambda x: (x[:, 0:4, :], x[:, 4:8, :]), -1), (lambda x: (x[:, 8:9, :], x[:, 12:13, :]), 1)], (9, 12, -1)
    return [(lambda x: (x[:, 0:5, :], x[:, 8:13, :]), 1)], (5, 8, -1)


def run(eng, n, unroll, head, body):
    end = head + (n - head) // unroll * unroll
    for i in range(head):
        body(i, i % unroll)
    if end > head:
        with eng.Fori(0, (end - head) // unroll) as turn:
            for u in range(unroll):
                body(turn * unroll + (head + u), (head + u) % unroll)
    for i in range(end, n):
        body(i, i % unroll)


def after(eng, sem, i, lag, per=1):
    if isinstance(i, int) and i < lag:
        return
    eng.wait_ge(sem, (i - lag + 1) * per)


def bcast(ap, axis, n):
    v = ap.unsqueeze(axis)
    shape = list(v.shape)
    shape[axis] = n
    return v.broadcast_to(shape)


def gps_layer(nc, x, src, dst, W, Wl, Wr, gnn_b, w_qkv, mem_kv, w_out, b_out, g_out, g_pre,
              router_w, w1, b1, w2, b2, out):
    N, D = x.shape
    E = src.shape[0]
    HD, C = Wl.shape
    _, MH, MD, MEM = mem_kv.shape
    HID = MH * MD
    NE, _, F = w1.shape
    T = -(-N // P)
    TAIL = N - (T - 1) * P
    SCALE = float(MD) ** -0.5
    KC = D // P
    TS = 7
    NS = T // TS
    HALFT = TS * P // 2
    assert T == TS * NS and HID == P and D == HD * C and F == D

    BLK = P * P
    NB = -(-E // BLK)
    LEVELS = (NB * BLK - 1).bit_length()
    assert NB == 13 and LEVELS == 18 and N <= PAD_NODE
    FULL = (NB - 1) * BLK
    ROWS = (E - FULL) // P
    REST = E - FULL - ROWS * P
    HALVES = ((0, 8), (8, NB))

    GT = 2
    GE = GT * P
    RING = 8
    HOTS = 8
    NG = (E + T * (GE - 1)) // GE
    GW = C + HD
    RW = D + HD
    GC = -(-NG // P)
    assert RING % HOTS == 0 and NB * BLK - E >= GE

    plan = make_plan(LEVELS)
    enters = [(n, s) for n, s in enumerate(plan) if s[0] == "enter"]

    table_d = nc.dram_tensor("gather_table", (T * P, GW), F32).ap()
    sorted_d = nc.dram_tensor("sorted_edges", (NB * BLK * 2,), F32).ap()
    groups_d = nc.dram_tensor("group_table", (2, P * GC), I32).ap()
    bases_d = nc.dram_tensor("group_bases", (P * GC,), F32).ap()

    with ExitStack() as ctx:
        def sb(name, shape, dt=F32):
            return ctx.enter_context(nc.sbuf_tensor(name, shape, dt))

        def sem(name):
            return ctx.enter_context(nc.semaphore(name))

        ps = ctx.enter_context(nc.psum_tensor("ps", [P, 8, 512], F32))

        ident = sb("ident", [P, P])
        ones = sb("ones", [P, P])
        lane = sb("lane", [P, P])
        lane_i = sb("lane_i", [P, P], I32)
        row_i = sb("row_i", [P, 1], I32)
        rowf = sb("rowf", [P, 1])
        sign7 = sb("sign7", [P, 1])
        eps_t = sb("eps_t", [P, 1])
        base = sb("base", [P, T, D])
        mv = sb("mv", [P, T, 2])
        rstd = sb("rstd", [P, T])
        nmr = sb("nmr", [P, T])
        rsc = sb("rsc", [P, T])
        tmpT = sb("tmpT", [P, T])
        el_all = sb("el_all", [P, T, HD + 1])
        big = sb("big", [P, T * RW])
        kv = big[:, 0:T * 2 * HID].rearrange("p (t c) -> p t c", t=T)
        att = big[:, 0:T * D].rearrange("p (t c) -> p t c", t=T)
        acc = big[:, :].rearrange("p (t c) -> p t c", t=T)

        n_sort = NB * P
        A_Q, A_TB = 0, T * HID
        A_E = A_TB + T * GW
        A_K = A_E + 2 * n_sort
        A_END1 = A_K + 3 * n_sort
        A_W1, A_W2 = 0, NE * KC * F
        A_Y = A_W2 + NE * KC * D
        A_H = A_Y + 2 * KC * TS * P
        A_X = A_H + 2 * KC * TS * P
        A_END2 = A_X + 2 * TS * D
        A_G = A_K
        arena = sb("arena", [P, max(A_END1, A_END2)])
        q_all = arena[:, A_Q:A_TB].rearrange("p (t c) -> p t c", t=T)
        tb = arena[:, A_TB:A_E].rearrange("p (t c) -> p t c", t=T)
        src_i = arena[:, A_E:A_E + n_sort].bitcast(I32).rearrange("p (t l) -> p t l", t=NB)
        dst_i = arena[:, A_E + n_sort:A_K].bitcast(I32).rearrange("p (t l) -> p t l", t=NB)
        pair = arena[:, A_E:A_K].rearrange("p (t l c) -> p t l c", t=NB, c=2)
        keys = [arena[:, A_K + i * n_sort:A_K + (i + 1) * n_sort].rearrange("p (t l) -> p t l", t=NB) for i in range(2)]
        right = arena[:, A_K + 2 * n_sort:A_END1].rearrange("p (t l) -> p t l", t=NB)
        w1_s = arena[:, A_W1:A_W2].rearrange("p (e k f) -> p e k f", e=NE, k=KC)
        w2_s = arena[:, A_W2:A_Y].rearrange("p (e k f) -> p e k f", e=NE, k=KC)
        yT = [arena[:, A_Y + i * KC * TS * P:A_Y + (i + 1) * KC * TS * P].rearrange("p (k n) -> p k n", k=KC) for i in range(2)]
        hT = [arena[:, A_H + i * KC * TS * P:A_H + (i + 1) * KC * TS * P].rearrange("p (k n) -> p k n", k=KC) for i in range(2)]
        low = arena[:, A_X:A_X + TS * D].rearrange("p (t c) -> p t c", t=TS)
        mid = arena[:, A_X + TS * D:A_END2].rearrange("p (t c) -> p t c", t=TS)

        spare = arena[:, A_END1:A_END2]
        stats = spare[:, 0:T * 6].rearrange("p (t s) -> p t s", t=T)
        wT = spare[0:C, T * 6:T * 6 + KC * P].rearrange("p (k n) -> p k n", k=KC)
        b1_r = spare[0:NE * KC, T * 6 + KC * P:T * 6 + (KC + 1) * P]
        gpre_r = spare[0:KC, T * 6 + (KC + 1) * P:T * 6 + (KC + 2) * P]

        junk = spare[:, 0:NB * P // 2].bitcast(mybir.dt.bfloat16).rearrange("p (t l) -> p t l", t=NB)
        bases = spare[:, 0:P * GC]
        assert P * GC <= A_END2 - A_END1 and A_G + GT * (RING * GW + (HOTS + 2) * P + 2 * RW) <= A_END1

        wcat = sb("wcat", [P, KC, GW + HD + 3 * HID])
        CQ = GW + HD
        wlr = sb("wlr", [2 * HD, C])
        wlrT = sb("wlrT", [C, 2 * HD])
        gpre_t = sb("gpre_t", [P, KC])
        wout_s = sb("wout_s", [P, D])
        rows_b = sb("rows_b", [P, 2, D])
        gnnb_t = sb("gnnb_t", [P, C])
        mk_t = sb("mk_t", [P, 2, MEM])
        rw_s = sb("rw_s", [NE, D])
        rwT = sb("rwT", [P, KC, NE])
        b1_t = sb("b1_t", [P, NE, KC])
        b2_s = sb("b2_s", [NE, D])

        xn = [sb(f"xn{i}", [P, D]) for i in range(2)]
        xnT = [sb(f"xnT{i}", [P, KC, P]) for i in range(2)]
        kmx = sb("kmx", [P, 4])
        kmaxp = sb("kmaxp", [P, P])
        kdiag, kmaxb = xn[1][:, 0:P], xn[1][:, P:2 * P]
        mexp = sb("mexp", [P, MEM])
        memT = sb("memT", [MEM, 2, P])
        ctxm = sb("ctxm", [P, P])
        mixw = sb("mixw", [P, D])
        qst = sb("qst", [P, 2, T * MH])
        qT = xnT[0][:, 0, :], xnT[1][:, 0, :]
        sq = xn[0]
        ss = sb("ss", [P, T])
        cnt = sb("cnt", [P, T])
        starts = sb("starts", [P, T + 1])
        gtab = sb("gtab", [P, 4, T])
        gsel = spare[:, 0:GC * T].rearrange("p (g t) -> p g t", g=GC)
        gidx = sb("gidx", [P, GC])
        gsum = sb("gsum", [P, 4, GC])
        gout = sb("gout", [P, 2, GC], I32)
        nthr = sb("nthr", [P, T])
        DLAG, PLAG = 5, 1
        trow = sb("trow", [3, P * GC + RING], I32)
        kd = [sb(f"kd{i}", [P, GT, 2]) for i in range(RING)]

        def ring(start, n, width):
            return [arena[:, start + i * GT * width:start + (i + 1) * GT * width].rearrange("p (c w) -> p c w", c=GT) for i in range(n)]
        gat = ring(A_G, RING, GW)
        hot = ring(A_G + RING * GT * GW, HOTS, P)
        hotT = ring(A_G + RING * GT * GW + HOTS * GT * P, 2, P)
        wx = ring(A_G + RING * GT * GW + (HOTS + 2) * GT * P, 2, RW)
        loc = [sb(f"loc{i}", [P, GT]) for i in range(2)]
        zed = [sb(f"zed{i}", [P, 3, GT * HD]) for i in range(2)]
        den = sb("den", [P, 2, TS * HD])
        st2 = sb("st2", [P, TS, 6])
        mv2 = sb("mv2", [P, TS, 2])
        ln2 = sb("ln2", [P, 3, TS])
        rt = sb("rt", [P, 6, TS * NE])
        top = sb("top", [P, TS, 8])
        topi = sb("topi", [P, TS, 8], U32)
        topf = sb("topf", [P, TS, 8])
        rs = sb("rs", [P, 4, TS])
        comb = [sb(f"comb{i}", [P, TS, NE]) for i in range(2)]
        combT = arena[0:NE, A_X:A_X + TS * P].rearrange("p (t n) -> p t n", t=TS)

        turned = ps[:, 0:4, :].rearrange("p a (b m) -> p (a b) m", m=P)[:, 0:NB, :]

        s_const = sem("s_const")
        s_pad = sem("s_pad")
        s_w = sem("s_w")
        s_xl = sem("s_xl")
        s_edges = sem("s_edges")
        s_step = sem("s_step")
        s_once = sem("s_once")
        s_aonce = sem("s_aonce")
        s_xn = sem("s_xn")
        s_xTp = sem("s_xTp")
        s_xT = sem("s_xT")
        s_proj = sem("s_proj")
        s_kv = sem("s_kv")
        s_base = sem("s_base")
        s_tab = sem("s_tab")
        s_ksub = sem("s_ksub")
        s_kexp = sem("s_kexp")
        s_qTp = sem("s_qTp")
        s_qT = sem("s_qT")
        s_mixp = sem("s_mixp")
        s_soft = sem("s_soft")
        s_scaled = sem("s_scaled")
        s_arow = sem("s_arow")
        s_key = sem("s_key")
        s_cnt = sem("s_cnt")
        s_turned = sem("s_turned")
        s_right = sem("s_right")
        s_gtd = sem("s_gtd")
        s_row = sem("s_row")
        s_srt = sem("s_srt")
        s_zero = sem("s_zero")
        s_first = sem("s_first")
        s_kd = [sem(f"s_kd{i}") for i in range(RING)]
        s_gat = [sem(f"s_gat{i}") for i in range(RING)]
        s_loc = sem("s_loc")
        s_hot = sem("s_hot")
        s_hTp = sem("s_hTp")
        s_hT = sem("s_hT")
        s_el = sem("s_el")
        s_z = sem("s_z")
        s_e = sem("s_e")
        s_wx = sem("s_wx")
        s_agg = sem("s_agg")
        s_acc = sem("s_acc")
        s_ew = sem("s_ew")
        s_pd = sem("s_pd")
        s_pa = sem("s_pa")
        s_pp = sem("s_pp")
        s_yin = sem("s_yin")
        s_carry = sem("s_carry")
        s_carry_pool = sem("s_carry_pool")
        s_carry_sp = sem("s_carry_sp")
        s_h = sem("s_h")
        s_g = sem("s_g")
        s_y = sem("s_y")
        s_moe = sem("s_moe")
        s_out = [sem("s_out0"), sem("s_out1")]
        block = ctx.enter_context(nc.Block())

        at = {}

        def sl(i, n=1):
            return slice(i, i + n) if isinstance(i, int) else bass.ds(i, n)

        NW = 16
        FIRST = 1
        assert RING * GE <= FIRST * BLK
        EARLY = 30
        LATE = [(EARLY, 39), (39, T)]
        COUNTS = [0, 0, 13, 8, 12, 16]
        assert sum(COUNTS) == T
        CTX = [(0, 21), (21, T)]
        ROWS_AT = 6
        CHUNKS = [(0, 11), (11, 24), (24, 38), (38, T)]
        assert (LEVELS - ROW_BITS) == ROWS_AT + len(CHUNKS) + 1
        PD = ["den", "rden", "avg", "bias", "neg", "elu", "x2", "stats", "mv", "rstd", "nmr", "lmax", "lsub", "lsum",
              "lrec", "prob", "top", "topi", "topf", "psum", "pmax", "prec", "w", "eq1", "c1", "eq2", "c2", "comb"] + [f"b2{u}" for u in range(4)]
        PA = ["eexp", "sd", "y"] + [f"yT{t}" for t in range(TS)] + ["lexp", "cTa", "cTb"]
        PP = [f"yTp{t}" for t in range(TS)] + ["logits", "cTpa", "cTpb"] + [f"b2p{u}" for u in range(4)]

        def count(names, st, name):
            return st * len(names) + names.index(name) + 1

        UNITS = [(0, 2), (2, 4), (4, 6), (6, 7)]
        NU = len(UNITS)

        def gathered(g, u):
            return (g - u) * (16 * GT // RING) + 16 * GT

        def loaded(g, u):
            return (g - u) * (16 // RING) + 16

        def blocks_of(eng, row, g):
            return nc.values_load_multi_w_load_instructions(
                trow[row:row + 1, sl(g, RING)], engines=[eng.engine], min_val=0, max_val=T - 1,
                skip_runtime_bounds_check_because="DVE clamps the block to T - 1 where it works the table out, and the rest of the row is zero")[1]

        @block.vector
        def _(dve):
            n = [0]

            def step(ins, name=None):
                ins.then_inc(s_step, 1)
                n[0] += 1
                if name:
                    at[name] = n[0]
                dve.wait_ge(s_step, n[0])

            dve.wait_ge(s_const, 4)
            step(dve.memset(eps_t[:, :], LN_EPS))
            step(dve.memset(ctxm[:, :], 0.0))
            step(dve.tensor_copy(lane[:, :], lane_i[:, :]))
            step(dve.tensor_scalar(nthr[:, :], lane[:, 0:T], -float(P), 0.5, ALU.mult, ALU.add))
            step(dve.tensor_reduce(sign7[:, :], ident[:, :].rearrange("p (a b) -> p a b", b=2)[:, :, 1], AX.X, ALU.add))
            step(dve.tensor_scalar(sign7[:, :], sign7[:, :], 2.0, -1.0, ALU.mult, ALU.add))
            step(dve.memset(el_all[:, :, HD:HD + 1], 1e30), "const")

            dve.wait_ge(s_once, 1)
            small = ps[:, 4, :]
            dve.tensor_copy(wT[:, :, :], small[0:C, 0:KC * P].rearrange("p (k n) -> p k n", k=KC))
            dve.tensor_copy(wlrT[:, :], small[0:C, KC * P:KC * P + 2 * HD])
            o = KC * P + 2 * HD
            dve.tensor_copy(rwT[:, :, :], small[:, o:o + KC * NE].rearrange("p (k e) -> p k e", k=KC))
            o += KC * NE
            dve.tensor_copy(b1_t[:, :, :], small[:, o:o + NE * KC].rearrange("p (e k) -> p e k", k=KC))
            o += NE * KC
            step(dve.tensor_copy(gpre_t[:, :], small[:, o:o + KC]), "small")
            for k in range(KC):
                step(dve.tensor_scalar(wcat[:, k, CQ:], wcat[:, k, CQ:], gpre_t[:, k:k + 1], None, ALU.mult))
            dve.wait_ge(s_once, 2)
            step(dve.tensor_copy(wcat[:, :, C:CQ], ps[:, 5, 0:KC * 2 * HD].rearrange("p (k h) -> p k h", k=KC)), "wcat")

            dve.wait_ge(s_xl, 16 * 5)
            for t in range(T):
                ins = dve.bn_stats(stats[:, t, :], base[:, t, :])
            step(ins)
            for t in range(T):
                ins = dve.bn_aggr(mv[:, t, :], stats[:, t, :])
            step(ins, "mv")
            dve.wait_ge(s_aonce, 1)
            step(dve.reciprocal(rstd[:, :], tmpT[:, :]))
            step(dve.scalar_tensor_tensor(out=nmr[:, :], in0=mv[:, :, 0], scalar=-1.0, in1=rstd[:, :], op0=ALU.mult, op1=ALU.mult), "nmr")
            step(dve.tensor_tensor(tmpT[:, :], mv[:, :, 1], rstd[:, :], ALU.mult))
            step(dve.tensor_tensor(tmpT[:, :], tmpT[:, :], rstd[:, :], ALU.mult), "norm2")
            dve.wait_ge(s_aonce, 2)
            step(dve.tensor_scalar(tmpT[:, :], tmpT[:, :], TINY, None, ALU.max))
            step(dve.reciprocal(rsc[:, :], tmpT[:, :]))
            step(dve.tensor_scalar(rsc[:, :], rsc[:, :], float(D) ** 0.5, None, ALU.mult), "rsc")

            q4 = q_all[:, :, :].rearrange("p t (h d) -> p (t h) d", h=MH)

            def attention(level, place):
                piece = (level, place)
                if piece == (2, 0):
                    dve.wait_ge(s_kv, T)
                    step(dve.tensor_reduce(kmaxp[:, :], kv[:, 0:T - 1, 0:HID].rearrange("p t c -> p c t"), AX.X, ALU.max))
                    step(dve.tensor_tensor(kmaxp[0:TAIL, :], kmaxp[0:TAIL, :], kv[0:TAIL, T - 1, 0:HID], ALU.max), "kmaxp")
                if piece == (2, 1):
                    dve.wait_ge(s_once, 3)
                    step(dve.tensor_reduce(kmx[:, 0:1], ps[:, 4, 0:P], AX.X, ALU.max))
                    step(dve.tensor_reduce(kmx[:, 1:2], mk_t[:, 0, :], AX.X, ALU.max))
                    step(dve.tensor_tensor(kmx[:, 0:1], kmx[:, 0:1], kmx[:, 1:2], ALU.max))
                    step(dve.tensor_scalar(kmx[:, 2:3], kmx[:, 0:1], -1.0, None, ALU.mult), "nkmx")
                    dve.wait_ge(s_base, T)
                    step(dve.tensor_scalar(kdiag[:, :], ident[:, :], kmx[:, 0:1], None, ALU.mult), "kdiag")
                if piece == (2, 2):
                    dve.wait_ge(s_once, 4)
                    step(dve.tensor_copy(kmaxb[:, :], ps[:, 5, 0:P]), "kmaxb")
                if piece == (2, 3):
                    step(dve.tensor_reduce(qst[:, 0, :], q4, AX.X, ALU.max), "qmax")
                if piece == (3, 0):
                    dve.wait_ge(s_once, 5)
                    step(dve.tensor_copy(memT[:, :, :], ps[0:MEM, 6, 0:2 * P].rearrange("p (a n) -> p a n", a=2)), "memT")
                if piece == (5, 0):
                    dve.wait_ge(s_once, 6)
                    for h in range(MH):
                        r = slice(h * MD, h * MD + MD)
                        ins = dve.tensor_scalar(ctxm[r, r], ps[r, 7, r], SCALE, None, ALU.mult)
                    step(ins)
                    step(dve.reciprocal(kmx[:, 3:4], ps[:, 4, 0:1]), "ctxm")
                    dve.wait_ge(s_aonce, 4)
                    step(dve.tensor_reduce(qst[:, 0, :], q4, AX.X, ALU.add))
                    step(dve.reciprocal(qst[:, 1, :], qst[:, 0, :]), "qrec")
                if piece == (5, 2):
                    dve.wait_ge(s_once, 7)
                    step(dve.tensor_scalar(mixw[:, :], ps[:, 5, 0:D], kmx[:, 3:4], None, ALU.mult), "mixw")
                if piece == (6, 1):
                    dve.wait_ge(s_once, 8)
                    step(dve.tensor_scalar(starts[:, 0:T], ps[:, 5, 0:T], -0.5, NB * BLK * 0.5, ALU.mult, ALU.add), "starts")
                if piece == (6, 2):
                    step(dve.memset(starts[:, T:T + 1], float(E)))
                    step(dve.tensor_tensor(gtab[:, 0, :], starts[:, 1:T + 1], starts[:, 0:T], ALU.subtract))
                    step(dve.tensor_scalar(gtab[:, 1, :], gtab[:, 0, :], float(GE - 1), None, ALU.add))
                    step(dve.tensor_copy(gtab[:, 2, :].bitcast(I32), gtab[:, 1, :]))
                    step(dve.tensor_scalar(gtab[:, 3, :].bitcast(I32), gtab[:, 2, :].bitcast(I32), GE.bit_length() - 1, None, ALU.logical_shift_right))
                    step(dve.tensor_copy(gtab[:, 1, :], gtab[:, 3, :].bitcast(I32)))
                    step(dve.tensor_tensor_scan(gtab[:, 2, :], ones[:, 0:T], gtab[:, 1, :], 0.0, ALU.mult, ALU.add))
                    step(dve.tensor_copy(rowf[:, :], row_i[:, :]))
                    step(dve.tensor_scalar(gidx[:, :], lane[:, 0:GC], rowf[:, 0:1], None, ALU.add))
                    before = gsel[:, :, :]
                    step(dve.tensor_tensor(before, bcast(gtab[:, 2, :], 1, GC), bcast(gidx[:, :], 2, T), ALU.is_le))
                    step(dve.tensor_reduce(gsum[:, 0, :], before, AX.X, ALU.add))
                    step(dve.tensor_tensor(before, before, bcast(gtab[:, 1, :], 1, GC), ALU.mult))
                    step(dve.tensor_reduce(gsum[:, 1, :], before, AX.X, ALU.add))
                    step(dve.tensor_tensor(before, bcast(gtab[:, 2, :], 1, GC), bcast(gidx[:, :], 2, T), ALU.is_le))
                    step(dve.tensor_tensor(before, before, bcast(gtab[:, 0, :], 1, GC), ALU.mult))
                    step(dve.tensor_reduce(gsum[:, 2, :], before, AX.X, ALU.add))
                    step(dve.tensor_tensor(gidx[:, :], gidx[:, :], gsum[:, 1, :], ALU.subtract))
                    step(dve.scalar_tensor_tensor(out=gsum[:, 2, :], in0=gidx[:, :], scalar=float(GE), in1=gsum[:, 2, :], op0=ALU.mult, op1=ALU.add))
                    step(dve.tensor_scalar(gsum[:, 2, :], gsum[:, 2, :], float(E), 2.0, ALU.min, ALU.mult))
                    step(dve.tensor_scalar(gsum[:, 0, :], gsum[:, 0, :], float(T - 1), None, ALU.min))
                    step(dve.tensor_copy(gout[:, 0, :], gsum[:, 2, :]))
                    step(dve.tensor_copy(gout[:, 1, :], gsum[:, 0, :]))
                    step(dve.tensor_scalar(gsum[:, 3, :], gsum[:, 0, :], -float(P), None, ALU.mult), "groups")
                if level > ROWS_AT and place == 0:
                    c = level - 1 - ROWS_AT
                    r = slice(*CHUNKS[c])
                    dve.wait_ge(s_aonce, 5 + c)
                    step(dve.tensor_scalar(ss[:, r], ss[:, r], TINY / float(D) ** 0.5, None, ALU.max))
                    step(dve.reciprocal(tmpT[:, r], ss[:, r]), f"scale{c}")

            dve.wait_ge(s_edges, 96)
            step(dve.tensor_scalar(right.bitcast(I32), src_i, NODE_BITS, KEY_BASE, ALU.logical_shift_left, ALU.bitwise_or))
            dve.tensor_tensor(keys[0].bitcast(I32), right.bitcast(I32), dst_i, ALU.bitwise_or).then_inc(s_key, 1)
            m, cur, done, entries = 1, 0, [1, 1], 0
            for kind, side, k, j in plan:
                a, b = keys[cur], keys[1 - cur]
                if (k, j) == (ROW_BITS, ROW_BITS - 1):
                    dve.wait_ge(s_key, m)
                    dve.tensor_scalar(b, a, sign7[:, 0:1], None, ALU.mult).then_inc(s_key, 1)
                    m += 1
                    done, cur = [m, m], 1 - cur
                    a, b = b, a
                if kind == "plain" and j >= 2 * ROW_BITS:
                    dve.wait_ge(s_key, m)
                    reads, lone = outer(a, 1 << (j - 2 * ROW_BITS), NB)
                    for (al, ah), (bl, bh) in zip(reads, outer(b, 1 << (j - 2 * ROW_BITS), NB)[0]):
                        dve.tensor_tensor(bl, al, ah, ALU.min).then_inc(s_key, 1)
                        dve.tensor_tensor(bh, al, ah, ALU.max).then_inc(s_key, 1)
                        m += 2
                    dve.tensor_copy(b[:, lone[0]:lone[1], :], a[:, lone[0]:lone[1], :]).then_inc(s_key, 1)
                    m += 1
                    done = [m, m]
                elif kind == "plain":
                    w = 1 << (j if side == "A" else j - ROW_BITS)
                    for h, part in enumerate(HALVES):
                        dve.wait_ge(s_key, done[h])
                        if side == "A" and k < ROW_BITS:
                            views = [(directed(a, w, 1 << (k - 1 - j), d, part), directed(b, w, 1 << (k - 1 - j), d, part), d) for d in range(2)]
                        else:
                            views = [(inner(a, w, part), inner(b, w, part), 1)]
                        for (al, ah), (bl, bh), up in views:
                            dve.tensor_tensor(bl, al, ah, ALU.min if up else ALU.max).then_inc(s_key, 1)
                            dve.tensor_tensor(bh, al, ah, ALU.max if up else ALU.min).then_inc(s_key, 1)
                            m += 2
                        done[h] = m
                else:
                    parts = ((0, NB),) if side == "B" and k > 2 * ROW_BITS else HALVES
                    for h, part in enumerate(parts):
                        entries += 1
                        dve.wait_ge(s_right, entries)
                        pairs, lone = enter_pairs(k, part, NB) if side == "B" else ([(lambda v: inner(v, P // 2, part), 0)], None)
                        for pick, sign in pairs:
                            left, rite, (bl, bh) = pick(turned)[0], pick(right)[1], pick(b)
                            for o_, op in ((bl, ALU.min), (bh, ALU.max)):
                                if sign == 0:
                                    dve.tensor_tensor(o_, left, rite, op).then_inc(s_key, 1)
                                else:
                                    x0, x1 = (left, rite) if sign > 0 else (rite, left)
                                    dve.scalar_tensor_tensor(out=o_, in0=x0, scalar=-1.0, in1=x1, op0=ALU.mult, op1=op).then_inc(s_key, 1)
                                m += 1
                        if lone:
                            dve.tensor_scalar(b[:, lone[0]:lone[1], :], turned[:, lone[0]:lone[1], :], float(lone[2]), None, ALU.mult).then_inc(s_key, 1)
                            m += 1
                        done[h] = m
                    if len(parts) == 1:
                        done = [m, m]
                cur = 1 - cur
                if side == "A" and k > ROW_BITS:
                    attention(k - ROW_BITS - 1, ROW_BITS - 1 - j)
                at[(kind, side, k, j)] = (list(done), cur)

            dve.wait_ge(s_key, m)
            dve.wait_ge(s_cnt, T)
            for name, r in (("pair0", slice(0, FIRST)), ("pair", slice(FIRST, NB))):
                res, tmp = keys[cur][:, r, :], keys[1 - cur][:, r, :]
                step(dve.tensor_scalar(tmp.bitcast(I32), res.bitcast(I32), NODE_BITS, PAD_NODE, ALU.logical_shift_right, ALU.bitwise_and))
                step(dve.tensor_scalar(pair[:, r, :, 1].bitcast(I32), res.bitcast(I32), PAD_NODE, None, ALU.bitwise_and))
                step(dve.tensor_copy(pair[:, r, :, 0], tmp.bitcast(I32)), name)

            dve.wait_ge(s_row, 64)

            home = [None]

            def logit(g, u, part):
                par = u % 2
                zz = [zed[par][:, k_, :].rearrange("p (c h) -> p c h", c=GT) for k_ in range(3)]
                pz = ps[:, 2 + par, 0:GT * (HD + 1)].rearrange("p (c h) -> p c h", c=GT)
                if part == 0:
                    dve.wait_ge(s_el, g + 1)
                    dve.wait_ge(s_gat[u], gathered(g, u))
                    dve.tensor_tensor(zz[0], pz[:, :, 0:HD], gat[u][:, :, C:GW], ALU.add).then_inc(s_z, 1)
                if part == 1:
                    dve.wait_ge(s_z, g * 3 + 1)
                    dve.scalar_tensor_tensor(out=zz[1], in0=zz[0], scalar=0.2, in1=zz[0], op0=ALU.mult, op1=ALU.max).then_inc(s_z, 1)
                if part == 2:
                    dve.wait_ge(s_z, g * 3 + 2)
                    dve.tensor_tensor(zz[2], pz[:, :, HD:HD + 1].broadcast_to([P, GT, HD]), zz[1], ALU.min).then_inc(s_z, 1)

            def one_hot(g, u):
                dve.wait_ge(s_loc, g + 1)
                after(dve, s_agg, g, HOTS)
                dve.tensor_tensor(hot[u % HOTS][:, :, :], bcast(lane[:, :], 1, GT), bcast(loc[u % 2][:, :], 2, P), ALU.is_equal).then_inc(s_hot, 1)

            def weigh(g, u):
                par = u % 2
                dve.wait_ge(s_e, g + 1)
                e4 = bcast(wx[par][:, :, D:RW], 3, C)
                x4 = bcast(gat[u][:, :, 0:C], 2, HD)
                dve.tensor_tensor(wx[par][:, :, 0:D].rearrange("p c (h d) -> p c h d", h=HD), x4, e4, ALU.mult).then_inc(s_wx, 1)

            def add_up(g, par, b):
                dve.wait_ge(s_agg, g + 1)
                if isinstance(g, int) and g == 0:
                    dve.wait_ge(s_zero, 2)
                after(dve, s_acc, g, 1)
                dve.tensor_tensor(acc[:, bass.ds(b, 1), :], ps[:, 4 + par:5 + par, 0:RW], acc[:, bass.ds(b, 1), :], ALU.add).then_inc(s_acc, 1)

            def group(g, u):
                now = g if isinstance(g, int) else NG // 2
                thinks = 2 <= now < NG + 2
                if u == 0:
                    home[0] = blocks_of(dve, 1, g)
                if thinks:
                    logit(g - 2, (u - 2) % RING, 0)
                if now < NG:
                    one_hot(g, u)
                if thinks:
                    logit(g - 2, (u - 2) % RING, 1)
                if 5 <= now < NG + 5:
                    add_up(g - 5, (u - 5) % 2, home[0][u])
                if thinks:
                    logit(g - 2, (u - 2) % RING, 2)
                if 3 <= now < NG + 3:
                    weigh(g - 3, (u - 3) % RING)
            run(dve, NG, RING, RING, group)
            for g in range(NG, NG + 5):
                group(g, g % RING)
            dve.wait_ge(s_acc, NG)

            def did(ins, st, name, plain=False):
                ins.then_inc(s_pd, 1)
                dve.wait_ge(s_pd, count(PD, st, name))
                if plain:
                    dve.sem_inc(s_carry, 1)

            def prepare(st, par, e):
                accs = acc[:, sl(st * TS, TS), :]
                rows = base[:, sl(st * TS, TS), :]
                m4 = mid.rearrange("p t (h d) -> p t h d", h=HD)
                dn = [den[:, k_, :].rearrange("p (t h) -> p t h", t=TS) for k_ in range(2)]
                r = [rt[:, k_, :].rearrange("p (t e) -> p t e", t=TS) for k_ in range(6)]
                lg = ps[:, 6, 0:TS * NE].rearrange("p (t e) -> p t e", t=TS)
                if e == 0:
                    did(dve.tensor_scalar(dn[0], accs[:, :, D:RW], TINY, None, ALU.max), st, "den")
                    did(dve.reciprocal(dn[1], dn[0]), st, "rden")
                    after(dve, s_yin, st, 1)
                    did(dve.tensor_tensor(m4, accs[:, :, 0:D].rearrange("p t (h d) -> p t h d", h=HD), bcast(dn[1], 3, C), ALU.mult), st, "avg")
                if e == 1:
                    m3 = mid.rearrange("p t (h d) -> p (t h) d", h=HD)
                    did(dve.tensor_tensor(m3, m3, bcast(gnnb_t[:, :], 1, TS * HD), ALU.add), st, "bias")
                    did(dve.tensor_scalar(low, mid, 0.0, None, ALU.min), st, "neg")
                    dve.wait_ge(s_pa, count(PA, st, "eexp"))
                    did(dve.scalar_tensor_tensor(out=mid, in0=mid, scalar=0.0, in1=low, op0=ALU.max, op1=ALU.add), st, "elu")
                    did(dve.scalar_tensor_tensor(out=rows, in0=mid, scalar=-1.0, in1=rows, op0=ALU.add, op1=ALU.add), st, "x2")
                if e == 2:
                    for t in range(TS):
                        ins = dve.bn_stats(st2[:, t, :], base[:, sl(st * TS + t), :])
                    did(ins, st, "stats", True)
                    for t in range(TS):
                        ins = dve.bn_aggr(mv2[:, t, :], st2[:, t, :])
                    did(ins, st, "mv")
                    dve.wait_ge(s_pa, count(PA, st, "sd"))
                    did(dve.reciprocal(ln2[:, 1, :], ln2[:, 0, :]), st, "rstd")
                    did(dve.scalar_tensor_tensor(out=ln2[:, 2, :], in0=mv2[:, :, 0], scalar=-1.0, in1=ln2[:, 1, :], op0=ALU.mult, op1=ALU.mult), st, "nmr")
                if e == 5:
                    dve.wait_ge(s_pp, count(PP, st, "logits"))
                    did(dve.tensor_reduce(rs[:, 0, :], lg, AX.X, ALU.max), st, "lmax")
                    did(dve.tensor_tensor(r[0], lg, bcast(rs[:, 0, :], 2, NE), ALU.subtract), st, "lsub")
                if e == 6:
                    dve.wait_ge(s_pa, count(PA, st, "lexp"))
                    did(dve.tensor_reduce(rs[:, 1, :], r[1], AX.X, ALU.add), st, "lsum")
                    did(dve.reciprocal(rs[:, 2, :], rs[:, 1, :]), st, "lrec")
                    did(dve.tensor_tensor(r[2], r[1], bcast(rs[:, 2, :], 2, NE), ALU.mult), st, "prob", True)
                    for t in range(TS):
                        ins = dve.max(top[:, t, :], r[2][:, t, :])
                    did(ins, st, "top", True)
                    for t in range(TS):
                        ins = dve.max_index(topi[:, t, :], top[:, t, :], r[2][:, t, :])
                    did(ins, st, "topi")
                    did(dve.tensor_copy(topf[:, :, 0:2], topi[:, :, 0:2]), st, "topf")
                    did(dve.tensor_tensor(rs[:, 3, :], top[:, :, 0], top[:, :, 1], ALU.add), st, "psum")
                    did(dve.tensor_scalar(rs[:, 3, :], rs[:, 3, :], TINY, None, ALU.max), st, "pmax")
                    did(dve.reciprocal(rs[:, 0, :], rs[:, 3, :]), st, "prec")
                    did(dve.tensor_tensor(top[:, :, 2:4], top[:, :, 0:2], bcast(rs[:, 0, :], 2, 2), ALU.mult), st, "w")
                    for c, (q0, q1) in enumerate((("eq1", "c1"), ("eq2", "c2"))):
                        did(dve.tensor_tensor(r[3 + c], bcast(lane[:, 0:NE], 1, TS), topf[:, :, c:c + 1].broadcast_to([P, TS, NE]), ALU.is_equal), st, q0)
                        did(dve.tensor_tensor(r[3 + c], r[3 + c], top[:, :, 2 + c:3 + c].broadcast_to([P, TS, NE]), ALU.mult), st, q1)
                    did(dve.tensor_tensor(comb[par][:, :, :], r[3], r[4], ALU.add), st, "comb")
                if e == 7:
                    dve.wait_ge(s_yin, st + 1)
                    for u, (t0, t1) in enumerate(UNITS):
                        dve.wait_ge(s_pp, count(PP, st, f"b2p{u}"))
                        tok = base[:, sl(st * TS + t0, t1 - t0), :]
                        did(dve.tensor_tensor(tok, ps[:, 6 + u % 2, 0:(t1 - t0) * D].rearrange("p (t c) -> p t c", c=D),
                                              tok, ALU.add), st, f"b2{u}")

            def gather_in(st, par, e, u):
                unit = (st * NE + e) * NU + u
                dve.wait_ge(s_y, unit + 1)
                if not (isinstance(unit, int) and unit < NU):
                    dve.wait_ge(s_moe, unit - NU + 1)
                t0, t1 = UNITS[u]
                for t in range(t0, t1):
                    tok = base[:, sl(st * TS + t), :]
                    ins = dve.scalar_tensor_tensor(out=tok, in0=ps[:, 4 + u % 2:5 + u % 2, (t - t0) * D:(t - t0 + 1) * D],
                                                   scalar=comb[par][:, t, e:e + 1], in1=tok, op0=ALU.mult, op1=ALU.add)
                ins.then_inc(s_moe, 1)

            def supertile(st, par, last=False):
                for e in range(NE):
                    if not last:
                        prepare(st + 1, 1 - par, e)
                    for u in range(NU):
                        gather_in(st, par, e, u)
            for e in range(NE):
                prepare(0, 0, e)
            run(dve, NS - 1, 2, 2, lambda st, par: supertile(st, par))
            supertile(NS - 1, (NS - 1) % 2, True)

        @block.tensor
        def _(pe):
            pe.wait_ge(s_const, 4)
            pe.wait_ge(s_w, 16 * NW)
            small = ps[:, 4, :]
            for k in range(KC):
                pe.transpose(small[0:C, k * P:k * P + P], wcat[:, k, 0:C], ident[:, :])
            o = KC * P
            pe.transpose(small[0:C, o:o + 2 * HD], wlr[:, :], ident[0:2 * HD, 0:2 * HD])
            o += 2 * HD
            for k in range(KC):
                pe.transpose(small[:, o:o + NE], rw_s[:, k * P:k * P + P], ident[0:NE, 0:NE])
                o += NE
            pe.transpose(small[:, o:o + NE * KC], b1_r[:, :], ident[0:NE * KC, 0:NE * KC])
            o += NE * KC
            pe.transpose(small[:, o:o + KC], gpre_r[:, :], ident[0:KC, 0:KC]).then_inc(s_once, 1)
            pe.wait_ge(s_step, at["small"])
            for k in range(KC):
                ins = pe.matmul(ps[:, 5, k * 2 * HD:(k + 1) * 2 * HD], wT[:, k, :], wlrT[:, :], start=True, stop=True)
            ins.then_inc(s_once, 1)
            pe.wait_ge(s_step, at["wcat"])

            def turn_x(i, u):
                pe.wait_ge(s_xn, i + 1)
                after(pe, s_xT, i, 2)
                for k in range(KC):
                    ins = pe.transpose(ps[:, 4 + u, k * P:k * P + P], xn[u][:, k * P:k * P + P], ident[:, :])
                ins.then_inc(s_xTp, 1)

            def project(i, u):
                pe.wait_ge(s_xT, i + 1)
                after(pe, s_kv, i, 2)
                for k in range(KC):
                    ins = pe.matmul(ps[:, 6 + u, 0:CQ + 3 * HID], xnT[u][:, k, :], wcat[:, k, :], start=(k == 0), stop=(k == KC - 1))
                ins.then_inc(s_proj, 1)

            def tile(i, u):
                turn_x(i, u)
                if not (isinstance(i, int) and i == 0):
                    project(i - 1, 1 - u)
            run(pe, EARLY, 2, 4, tile)

            def turn_q(t):
                if t >= 2:
                    pe.wait_ge(s_qT, t - 1)
                pe.transpose(ps[:, 6 + t % 2, 0:P], q_all[:, t, :], ident[:, :]).then_inc(s_qTp, 1)

            def mix(t):
                pe.wait_ge(s_qT, t + 1)
                if t >= 2:
                    pe.wait_ge(s_arow, t - 1)
                pe.matmul(ps[:, 4 + t % 2, 0:D], qT[t % 2], mixw[:, :], start=True, stop=False)
                pe.matmul(ps[:, 4 + t % 2, 0:D], ones[0:1, :], rows_b[0:1, 0, :], start=False, stop=True).then_inc(s_mixp, 1)

            def attention(piece):
                if piece < len(LATE):
                    for t in range(*LATE[piece]):
                        tile(t, t % 2)
                    if LATE[piece][1] == T:
                        project(T - 1, (T - 1) % 2)
                if piece == 2:
                    pe.wait_ge(s_step, at["kmaxp"])
                    pe.transpose(ps[:, 4, 0:P], kmaxp[:, :], ident[:, :]).then_inc(s_once, 1)
                    pe.wait_ge(s_step, at["kdiag"])
                    pe.matmul(ps[:, 5, 0:P], ones[:, :], kdiag[:, :], start=True, stop=True).then_inc(s_once, 1)
                    pe.wait_ge(s_aonce, 3)
                    pe.transpose(ps[0:MEM, 6, 0:P], mexp[:, :], ident[:, :])
                    pe.transpose(ps[0:MEM, 6, P:2 * P], mk_t[:, 1, :], ident[:, :]).then_inc(s_once, 1)
                if piece in (3, 4):
                    for t in range(*CTX[piece - 3]):
                        if t % TS == 0:
                            pe.wait_ge(s_kexp, t // TS + 1)
                        r = slice(0, P if t < T - 1 else TAIL)
                        pe.matmul(ps[:, 7, 0:HID], kv[r, t, HID:2 * HID], kv[r, t, 0:HID], start=(t == 0), stop=False)
                        pe.matmul(ps[:, 4, 0:1], kv[r, t, 0:HID], ones[r, 0:1], start=(t == 0), stop=False)
                if piece == 4:
                    pe.wait_ge(s_step, at["memT"])
                    pe.matmul(ps[:, 7, 0:HID], memT[:, 1, :], memT[:, 0, :], start=False, stop=True)
                    pe.matmul(ps[:, 4, 0:1], memT[:, 0, :], ones[0:MEM, 0:1], start=False, stop=True).then_inc(s_once, 1)
                if piece == 5:
                    pe.wait_ge(s_step, at["ctxm"])
                    pe.matmul(ps[:, 5, 0:D], ctxm[:, :], wout_s[:, :], start=True, stop=True).then_inc(s_once, 1)
                if 0 <= piece - ROWS_AT < len(CHUNKS):
                    t0, t1 = CHUNKS[piece - ROWS_AT]
                    if t0 == 0:
                        pe.wait_ge(s_step, at["mixw"])
                        pe.wait_ge(s_cnt, T)
                        pe.matmul(ps[:, 5, 0:T], ones[:, :], cnt[:, :], start=True, stop=True).then_inc(s_once, 1)
                        pe.wait_ge(s_step, at["starts"])
                        pe.wait_ge(s_soft, 2)
                    for t in range(t0, t1):
                        turn_q(t)
                        if t > t0:
                            mix(t - 1)
                    mix(t1 - 1)

            for i, (_, side, k, j) in enters:
                done, cur = at[plan[i - 1]]
                for h, part in enumerate(HALVES):
                    pe.wait_ge(s_key, done[h])
                    for t in range(*part):
                        ins = pe.transpose(turned[:, t, :], keys[cur][:, t, :], ident[:, :])
                    ins.then_inc(s_turned, 1)
                if side == "A":
                    attention(k - ROW_BITS - 1)

            pe.wait_ge(s_row, 64)

            def turn_hot(g, u):
                par = u % 2
                pe.wait_ge(s_hot, g + 1)
                after(pe, s_hT, g, 2)
                for c in range(GT):
                    ins = pe.transpose(ps[:, par, c * P:c * P + P], hot[u % HOTS][:, c, :], ident[:, :])
                ins.then_inc(s_hTp, 1)

            def aggregate(g, u):
                par = u % 2
                pe.wait_ge(s_wx, g + 1)
                after(pe, s_acc, g, 2)
                for c in range(GT):
                    ins = pe.matmul(ps[:, 4 + par, 0:RW], hot[u % HOTS][:, c, :], wx[par][:, c, :], start=(c == 0), stop=(c == GT - 1))
                ins.then_inc(s_agg, 1)

            home = [None]

            def spread_el(g, u, b):
                par = u % 2
                pe.wait_ge(s_hT, g + 1)
                after(pe, s_z, g, 2, 3)
                for c in range(GT):
                    ins = pe.matmul(ps[:, 2 + par, c * (HD + 1):(c + 1) * (HD + 1)], hotT[par][:, c, :],
                                    el_all[:, bass.ds(b, 1), :].rearrange("p a h -> p (a h)"), start=True, stop=True)
                ins.then_inc(s_el, 1)

            def group(g, u):
                now = g if isinstance(g, int) else NG // 2
                if u == 0:
                    home[0] = blocks_of(pe, 2, g)
                if 4 <= now < NG + 4:
                    aggregate(g - 4, (u - 4) % RING)
                if 1 <= now < NG + 1:
                    spread_el(g - 1, (u - 1) % RING, home[0][u])
                if now < NG:
                    turn_hot(g, u)
            run(pe, NG, RING, RING, group)
            for g in range(NG, NG + 4):
                group(g, g % RING)

            def prepare(st, par, e):
                if e == 4:
                    pe.wait_ge(s_pa, count(PA, st, "y"))
                    after(pe, s_pd, st, 1, len(PD))
                    for t in range(TS):
                        if t >= 2:
                            pe.wait_ge(s_pa, count(PA, st, f"yT{t - 2}"))
                        for k in range(KC):
                            ins = pe.transpose(ps[:, 6 + t % 2, k * P:k * P + P], mid[:, t, k * P:k * P + P], ident[:, :])
                        ins.then_inc(s_pp, 1)
                if e == 5:
                    pe.wait_ge(s_pa, count(PA, st, f"yT{TS - 1}"))
                    for t in range(TS):
                        for k in range(KC):
                            ins = pe.matmul(ps[:, 6, t * NE:(t + 1) * NE], yT[par][:, k, t * P:t * P + P], rwT[:, k, :], start=(k == 0), stop=(k == KC - 1))
                    ins.then_inc(s_pp, 1)
                if e == 7:
                    pe.wait_ge(s_pd, count(PD, st, "comb"))
                    for t in range(4):
                        ins = pe.transpose(ps[0:NE, 7, t * P:t * P + P], comb[par][:, t, :], ident[:, :])
                    ins.then_inc(s_pp, 1)
                    for t in range(4, TS):
                        ins = pe.transpose(ps[0:NE, 6, (t - 4) * P:(t - 3) * P], comb[par][:, t, :], ident[:, :])
                    ins.then_inc(s_pp, 1)
                    for u, (t0, t1) in enumerate(UNITS):
                        if u == 0:
                            pe.wait_ge(s_pa, count(PA, st, "cTb"))
                        if u >= 2:
                            pe.wait_ge(s_pd, count(PD, st, f"b2{u - 2}"))
                        for t in range(t0, t1):
                            ins = pe.matmul(ps[:, 6 + u % 2, (t - t0) * D:(t - t0 + 1) * D], combT[:, t, :], b2_s[:, :], start=True, stop=True)
                        ins.then_inc(s_pp, 1)

            def hidden(st, par, e):
                for f in range(KC):
                    for c in range(2):
                        bank = (st * NE + e) * 4 + f * 2 + c
                        after(pe, s_g, bank, 4)
                        for k in range(KC):
                            ins = pe.matmul(ps[:, f * 2 + c, 0:HALFT], w1_s[:, e, k, f * P:f * P + P],
                                            yT[par][:, k, c * HALFT:(c + 1) * HALFT], start=(k == 0), stop=(k == KC - 1))
                        ins.then_inc(s_h, 1)

            def outward(st, par, e):
                pe.wait_ge(s_g, (st * NE + e) * 4 + 4)
                for u, (t0, t1) in enumerate(UNITS):
                    unit = (st * NE + e) * NU + u
                    after(pe, s_moe, unit, 2)
                    for t in range(t0, t1):
                        for k in range(KC):
                            ins = pe.matmul(ps[:, 4 + u % 2, (t - t0) * D:(t - t0 + 1) * D], hT[e % 2][:, k, t * P:t * P + P],
                                            w2_s[:, e, k, :], start=(k == 0), stop=(k == KC - 1))
                    ins.then_inc(s_y, 1)

            def supertile(st, par, last=False):
                for e in range(NE):
                    if not last:
                        prepare(st + 1, 1 - par, e)
                    if e < NE - 1:
                        hidden(st, par, e + 1)
                    elif not last:
                        hidden(st + 1, 1 - par, 0)
                    outward(st, par, e)
            for e in range(6):
                prepare(0, 0, e)
            pe.wait_ge(s_ew, 32 * NE)
            hidden(0, 0, 0)
            for e in range(6, NE):
                prepare(0, 0, e)
            run(pe, NS - 1, 2, 2, lambda st, par: supertile(st, par))
            supertile(NS - 1, (NS - 1) % 2, True)

        @block.scalar
        def _(act):
            act.wait_ge(s_step, at["mv"])
            act.activation(tmpT[:, :], mv[:, :, 1], ACT.Sqrt, bias=eps_t[:, 0:1]).then_inc(s_aonce, 1)
            act.wait_ge(s_step, at["norm2"])
            act.activation(tmpT[:, :], tmpT[:, :], ACT.Sqrt, scale=float(D)).then_inc(s_aonce, 1)
            act.wait_ge(s_step, at["rsc"])

            def normalise(i, u):
                after(act, s_xTp, i, 2)
                after(act, s_base, i, 2)
                act.activation(xn[u][:, :], base[:, i, :] if isinstance(i, int) else base[:, sl(i), :].rearrange("p a c -> p (a c)"),
                               ACT.Identity, bias=nmr[:, sl(i)], scale=rstd[:, sl(i)]).then_inc(s_xn, 1)

            def copy_xT(i, u):
                act.wait_ge(s_xTp, i + 1)
                after(act, s_proj, i, 2)
                act.activation(xnT[u][:, :, :], ps[:, 4 + u, 0:D].rearrange("p (k n) -> p k n", k=KC), ACT.Copy).then_inc(s_xT, 1)

            def store(i, u):
                act.wait_ge(s_proj, i + 1)
                proj = ps[:, 6 + u:7 + u, :]
                act.activation(tb[:, sl(i), :], proj[:, :, 0:GW], ACT.Copy)
                act.activation(el_all[:, sl(i), 0:HD], proj[:, :, GW:CQ], ACT.Copy)
                act.activation(q_all[:, sl(i), :], proj[:, :, CQ:CQ + HID], ACT.Copy, scale=rsc[:, sl(i)])
                act.activation(kv[:, sl(i), :], proj[:, :, CQ + HID:CQ + 3 * HID], ACT.Copy, scale=rsc[:, sl(i)]).then_inc(s_kv, 1)

            def tile(i, u):
                now = i if isinstance(i, int) else T // 2
                if now < T:
                    normalise(i, u)
                if 1 <= now < T + 1:
                    copy_xT(i - 1, 1 - u)
                if 2 <= now:
                    store(i - 2, u)
            run(act, EARLY, 2, 2, tile)

            def count_sources(blocks):
                for b in blocks:
                    if b:
                        act.wait_ge(s_cnt, b)
                    act.activation(junk, src_i, ACT.Sign, bias=nthr[:, b:b + 1], accum_out=cnt[:, b:b + 1]).then_inc(s_cnt, 1)

            def copy_qT(t):
                act.wait_ge(s_qTp, t + 1)
                if t >= 2:
                    act.wait_ge(s_mixp, t - 1)
                act.activation(qT[t % 2], ps[:, 6 + t % 2, 0:P], ACT.Copy).then_inc(s_qT, 1)

            def row(t):
                act.wait_ge(s_mixp, t + 1)
                act.activation(att[:, t, :], ps[:, 4 + t % 2, 0:D], ACT.Copy)
                if t:
                    act.wait_ge(s_arow, t)
                act.activation(sq[:, :], ps[:, 4 + t % 2, 0:D], ACT.Square, accum_out=ss[:, t:t + 1]).then_inc(s_arow, 1)

            def attention(piece):
                if piece < len(LATE):
                    t0, t1 = LATE[piece]
                    for t in range(t0, t1 + 2 * (t1 == T)):
                        tile(t, t % 2)
                if piece == 2:
                    act.wait_ge(s_step, at["nkmx"])
                    act.activation(mexp[:, :], mk_t[:, 0, :], ACT.Exp, bias=kmx[:, 2:3]).then_inc(s_aonce, 1)
                if piece == 3:
                    for c in range(NS):
                        act.wait_ge(s_ksub, c + 1)
                        kc = kv[:, TS * c:TS * c + TS, 0:HID]
                        act.activation(kc, kc, ACT.Exp).then_inc(s_kexp, 1)
                if piece == 4:
                    act.wait_ge(s_soft, 1)
                    act.activation(q_all[:, :, :], q_all[:, :, :], ACT.Exp).then_inc(s_aonce, 1)
                if 0 <= piece - ROWS_AT < len(CHUNKS):
                    t0, t1 = CHUNKS[piece - ROWS_AT]
                    for t in range(t0, t1):
                        copy_qT(t)
                        if t > t0:
                            row(t - 1)
                    row(t1 - 1)
                    act.wait_ge(s_arow, t1)
                    act.activation(ss[:, t0:t1], ss[:, t0:t1], ACT.Sqrt, scale=1.0 / D).then_inc(s_aonce, 1)

            act.wait_ge(s_edges, 96)
            turns = 0
            counted = 0
            for i, (_, side, k, j) in enters:
                parts = ((0, NB),) if side == "B" and k > 2 * ROW_BITS else HALVES
                for part in parts:
                    turns += 2 // len(parts)
                    act.wait_ge(s_turned, turns)
                    pairs = enter_pairs(k, part, NB)[0] if side == "B" else [(lambda v: inner(v, P // 2, part), 0)]
                    for pick, _ in pairs:
                        ins = act.activation(pick(right)[1], pick(turned)[1], ACT.Copy)
                    ins.then_inc(s_right, 1)
                if side == "A":
                    level = k - ROW_BITS - 1
                    attention(level)
                    if level < len(COUNTS):
                        count_sources(range(counted, counted + COUNTS[level]))
                        counted += COUNTS[level]

            kept = CHUNKS[-1][0] * D
            for n_, (c0, c1) in enumerate(((0, kept), (kept, T * RW))):
                act.wait_ge(s_scaled, 3 * (len(CHUNKS) - 1 + n_))
                act.activation(big[:, c0:c1], ones[:, 0:1].broadcast_to([P, c1 - c0]), ACT.Copy, scale=0.0).then_inc(s_zero, 1)
            def load_expert(e):
                if e == 0:
                    act.wait_ge(s_tab, 16)
                    act.wait_ge(s_qTp, T)
                act.dma_start(w1_s[:, e, :, :], w1[e].rearrange("(k p) f -> p k f", p=P)).then_inc(s_ew, 16)
                act.dma_start(w2_s[:, e, :, :], w2[e].rearrange("(k p) f -> p k f", p=P)).then_inc(s_ew, 16)

            def weights(g, u):
                par = u % 2
                act.wait_ge(s_z, g * 3 + 3)
                after(act, s_agg, g, 2)
                act.activation(wx[par][:, :, D:RW], zed[par][:, 2, :].rearrange("p (c h) -> p c h", c=GT), ACT.Exp).then_inc(s_e, 1)

            def copy_hot(g, u):
                par = u % 2
                act.wait_ge(s_hTp, g + 1)
                after(act, s_el, g, 2)
                act.activation(hotT[par][:, :, :], ps[:, par, 0:GT * P].rearrange("p (c n) -> p c n", c=GT), ACT.Copy).then_inc(s_hT, 1)

            def locate(g, u):
                act.wait_ge(s_kd[u], loaded(g, u))
                after(act, s_hot, g, 2)
                act.activation(loc[u % 2][:, :], kd[u][:, :, 0], ACT.Identity, bias=bases[:, sl(g)]).then_inc(s_loc, 1)

            def group(g, u):
                now = g if isinstance(g, int) else NG // 2
                if now < NG:
                    locate(g, u)
                if 1 <= now < NG + 1:
                    copy_hot(g - 1, (u - 1) % RING)
                if 3 <= now < NG + 3:
                    weights(g - 3, (u - 3) % RING)
                if isinstance(g, int) and g < NE:
                    load_expert(g)
            assert NE <= RING
            act.wait_ge(s_row, 64)
            run(act, NG, RING, RING, group)
            for g in range(NG, NG + 3):
                group(g, g % RING)

            def did(ins):
                ins.then_inc(s_pa, 1)

            def prepare(st, par, e):
                if e == 1:
                    act.wait_ge(s_pd, count(PD, st, "neg"))
                    did(act.activation(low, low, ACT.Exp))
                if e == 2:
                    act.wait_ge(s_pd, count(PD, st, "mv"))
                    did(act.activation(ln2[:, 0, :], mv2[:, :, 1], ACT.Sqrt, bias=eps_t[:, 0:1]))
                if e == 3:
                    act.wait_ge(s_pd, count(PD, st, "nmr"))
                    for t in range(TS):
                        ins = act.activation(mid[:, t:t + 1, :], base[:, sl(st * TS + t), :], ACT.Identity, bias=ln2[:, 2, t:t + 1], scale=ln2[:, 1, t:t + 1])
                    did(ins)
                if e == 4:
                    for t in range(TS):
                        act.wait_ge(s_pp, count(PP, st, f"yTp{t}"))
                        did(act.activation(yT[par][:, :, t * P:t * P + P], ps[:, 6 + t % 2, 0:D].rearrange("p (k n) -> p k n", k=KC), ACT.Copy))
                if e == 5:
                    act.wait_ge(s_pd, count(PD, st, "lsub"))
                    did(act.activation(rt[:, 1, :], rt[:, 0, :], ACT.Exp))
                if e == 7:
                    act.wait_ge(s_pp, count(PP, st, "cTpa"))
                    did(act.activation(combT[:, 0:4, :], ps[0:NE, 7, :].rearrange("p (t n) -> p t n", t=4), ACT.Copy))
                    act.wait_ge(s_pp, count(PP, st, "cTpb"))
                    did(act.activation(combT[:, 4:TS, :], ps[0:NE, 6, 0:(TS - 4) * P].rearrange("p (t n) -> p t n", t=TS - 4), ACT.Copy))

            def gelus(st, par, e):
                last_unit = (st * NE + e - 1) * NU
                if not (isinstance(last_unit, int) and last_unit <= 0):
                    act.wait_ge(s_y, last_unit)
                for f in range(KC):
                    for c in range(2):
                        act.wait_ge(s_h, (st * NE + e) * 4 + f * 2 + c + 1)
                        act.activation(hT[e % 2][:, f, c * HALFT:(c + 1) * HALFT], ps[:, f * 2 + c, 0:HALFT], ACT.Gelu,
                                       bias=b1_t[:, e, f:f + 1]).then_inc(s_g, 1)

            def supertile(st, par, last=False):
                for e in range(NE):
                    if not last:
                        prepare(st + 1, 1 - par, e)
                    if e < NE - 1:
                        gelus(st, par, e + 1)
                    elif not last:
                        gelus(st + 1, 1 - par, 0)
            for e in range(6):
                prepare(0, 0, e)
            gelus(0, 0, 0)
            for e in range(6, NE):
                prepare(0, 0, e)
            run(act, NS - 1, 2, 2, lambda st, par: supertile(st, par))
            supertile(NS - 1, (NS - 1) % 2, True)

        @block.gpsimd
        def _(pool):
            pool.memset(src_i[:, NB - 1, :], PAD_NODE).then_inc(s_pad, 1)
            pool.memset(dst_i[:, NB - 1, :], 0).then_inc(s_pad, 1)
            pool.memset(trow[:, :], 0).then_inc(s_pad, 1)
            pool.memset(base[:, T - 1, :], 0.0).then_inc(s_pad, 1)
            pool.memset(ident[:, :], 0.0).then_inc(s_pad, 1)
            pool.memset(ones[:, :], 1.0).then_inc(s_const, 1)
            pool.iota(lane_i[:, :], [[1, P]], base=0, channel_multiplier=0).then_inc(s_const, 1)
            pool.iota(row_i[:, :], [[1, 1]], base=0, channel_multiplier=GC).then_inc(s_const, 1)
            pool.wait_ge(s_pad, 5)
            pool.affine_select(out=ident[:, :], in_=ident[:, :], compare_op=ALU.not_equal, fill=1.0, base=0,
                               pattern=[[-1, P]], channel_multiplier=1).then_inc(s_const, 1)

            def add_x(i, u):
                pool.wait_ge(s_xn, i + 1)
                b = base[:, sl(i), :]
                pool.tensor_tensor(b, b, xn[u][:, :].unsqueeze(1), ALU.add).then_inc(s_base, 1)
            run(pool, T, 2, 2, add_x)

            pool.wait_ge(s_step, at["kmaxb"])
            for c in range(NS):
                kc = kv[:, TS * c:TS * c + TS, 0:HID]
                pool.tensor_tensor(kc, kc, bcast(kmaxb[:, :], 1, TS), ALU.subtract).then_inc(s_ksub, 1)
            q4 = q_all[:, :, :].rearrange("p t (h d) -> p (t h) d", h=MH)
            pool.wait_ge(s_step, at["qmax"])
            pool.tensor_tensor(q4, q4, bcast(qst[:, 0, :], 2, MD), ALU.subtract).then_inc(s_soft, 1)
            pool.wait_ge(s_step, at["qrec"])
            pool.tensor_tensor(q4, q4, bcast(qst[:, 1, :], 2, MD), ALU.mult).then_inc(s_soft, 1)
            for c, (t0, t1) in enumerate(CHUNKS):
                pool.wait_ge(s_step, at[f"scale{c}"])
                rows, n_ = att[:, t0:t1, :], t1 - t0
                pool.tensor_tensor(rows, rows, bcast(tmpT[:, t0:t1], 2, D), ALU.mult).then_inc(s_scaled, 1)
                pool.wait_ge(s_scaled, 3 * c + 1)
                pool.tensor_tensor(rows, rows, bcast(rows_b[:, 1, :], 1, n_), ALU.mult).then_inc(s_scaled, 1)
                pool.wait_ge(s_scaled, 3 * c + 2)
                pool.tensor_tensor(base[:, t0:t1, :], base[:, t0:t1, :], rows, ALU.add).then_inc(s_scaled, 1)
            pool.wait_ge(s_tab, 16)

            pool.wait_ge(s_step, at["pair"])
            def gather(g, u):
                pool.wait_ge(s_kd[u], loaded(g, u))
                after(pool, s_wx, g, RING)
                pool.sem_inc(s_carry_pool, 1)
                for c in range(GT):
                    pool.indirect_dma_start(gat[u][:, c, :], None, table_d,
                                            bass.IndirectOffsetOnAxis(ap=kd[u][:, c, 1:2].bitcast(I32), axis=0)).then_inc(s_gat[u], 16)
            run(pool, NG, RING, RING, gather)

            def seed(st, par):
                pool.wait_ge(s_pa, count(PA, st, "y"))
                tok = base[:, sl(st * TS, TS), :]
                pool.tensor_tensor(tok, tok, mid, ALU.add).then_inc(s_yin, 1)
            run(pool, NS, 2, 2, seed)

        @block.sync
        def _(sp):
            loads = [(wcat[:, k, 0:C], W[k * P:k * P + P, :]) for k in range(KC)]
            loads += [(wcat[:, k, CQ:], w_qkv[k * P:k * P + P, :]) for k in range(KC)]
            loads += [(wlr[0:HD, :], Wr), (wlr[HD:2 * HD, :], Wl), (rw_s[:, :], router_w), (wout_s[:, :], w_out), (b2_s[:, :], b2)]
            loads += [(b1_r[:, :], b1.rearrange("e (k p) -> (e k) p", p=P)), (gpre_r[:, :], g_pre.rearrange("(k p) -> k p", p=P))]
            loads += [(mk_t[:, a, :], mem_kv[a].rearrange("h d m -> (h d) m")) for a in range(2)]
            for dst_, src_ in loads:
                sp.dma_start(dst_, src_).then_inc(s_w, 16)
            sp.dma_start(rows_b[:, 0, :], b_out.partition_broadcast(P)).then_inc(s_w, 16)
            sp.dma_start(rows_b[:, 1, :], g_out.partition_broadcast(P)).then_inc(s_w, 16)
            sp.dma_start(gnnb_t[:, :], gnn_b.partition_broadcast(P)).then_inc(s_w, 16)
            sp.wait_ge(s_pad, 5)
            xm = x[0:(T - 1) * P, :].rearrange("(t p) c -> p t c", p=P)
            for c in range(4):
                sp.dma_start(base[:, 12 * c:12 * c + 12, :], xm[:, 12 * c:12 * c + 12, :]).then_inc(s_xl, 16)
            sp.dma_start(base[0:TAIL, T - 1, :], x[(T - 1) * P:N, :]).then_inc(s_xl, 16)
            for buf, d in ((src_i, src), (dst_i, dst)):
                sp.dma_start(buf[:, 0:NB - 1, :], d[0:FULL].rearrange("(t m l) -> m t l", m=P, l=P)).then_inc(s_edges, 16)
                sp.dma_start(buf[0:ROWS, NB - 1, :], d[FULL:FULL + ROWS * P].rearrange("(m l) -> m l", l=P)).then_inc(s_edges, 16)
                sp.dma_start(buf[ROWS:ROWS + 1, NB - 1, 0:REST], d[FULL + ROWS * P:E].rearrange("(m l) -> m l", m=1)).then_inc(s_edges, 16)
            sp.wait_ge(s_kv, T)
            sp.dma_start(table_d.rearrange("(t p) c -> p t c", p=P), tb).then_inc(s_tab, 16)
            sp.wait_ge(s_step, at["groups"])
            sp.dma_start(groups_d.rearrange("a (p c) -> p a c", c=GC), gout[:, :, :]).then_inc(s_gtd, 16)
            sp.dma_start(bases_d.rearrange("(p c) -> p c", c=GC), gsum[:, 3, :]).then_inc(s_gtd, 16)
            sp.wait_ge(s_gtd, 32)
            sp.dma_start(trow[0:1, 0:P * GC], groups_d[0:1, :]).then_inc(s_row, 16)
            sp.dma_start(trow[1:2, DLAG:DLAG + P * GC], groups_d[1:2, :]).then_inc(s_row, 16)
            sp.dma_start(trow[2:3, PLAG:PLAG + P * GC], groups_d[1:2, :]).then_inc(s_row, 16)
            sp.dma_start(bases[:, :], bases_d.partition_broadcast(P)).then_inc(s_row, 16)
            in_d, in_s = sorted_d.rearrange("(t m c) -> m t c", m=P, c=2 * P), pair.rearrange("p t l c -> p t (l c)")
            sp.wait_ge(s_step, at["pair0"])
            sp.dma_start(in_d[:, 0:FIRST, :], in_s[:, 0:FIRST, :]).then_inc(s_first, 16)
            sp.wait_ge(s_first, 16)
            sp.wait_ge(s_row, 64)

            def load_group(g, u):
                if isinstance(g, int) and g == RING // 2:
                    sp.wait_ge(s_step, at["pair"])
                    sp.dma_start(in_d[:, FIRST:NB, :], in_s[:, FIRST:NB, :]).then_inc(s_srt, 16)
                if isinstance(g, int) and g == RING - 1:
                    sp.wait_ge(s_srt, 16)
                if not (isinstance(g, int) and g < RING):
                    sp.wait_ge(s_loc, g - RING + 1)
                    sp.wait_ge(s_gat[u], gathered(g, u) - 16 * GT)
                    sp.sem_inc(s_carry_sp, 1)
                first = sp.value_load(trow[0:1, sl(g)], min_val=0, max_val=E * 2)
                sp.dma_start(kd[u][:, :, :].rearrange("p c a -> p (c a)"),
                             sorted_d[bass.ds(first, GE * 2)].rearrange("(p c) -> p c", p=P)).then_inc(s_kd[u], 16)
            run(sp, NG, RING, RING, load_group)

            def store(st, par):
                sp.wait_ge(s_moe, (st + 1) * (NE * NU))
                rows = out[0:(T - 1) * P, :].rearrange("(t p) c -> p t c", p=P)
                if isinstance(st, int) and st == NS - 1:
                    sp.dma_start(rows[:, TS * st:T - 1, :], base[:, TS * st:T - 1, :]).then_inc(s_out[par], 16)
                    sp.dma_start(out[(T - 1) * P:N, :], base[0:TAIL, T - 1, :]).then_inc(s_out[par], 16)
                else:
                    sp.dma_start(rows[:, sl(st * TS, TS), :], base[:, sl(st * TS, TS), :]).then_inc(s_out[par], 16)
            run(sp, NS - 1, 2, 2, store)
            store(NS - 1, (NS - 1) % 2)
            sp.wait_ge(s_out[0], 16 * ((NS + 1) // 2 + 1))
            sp.wait_ge(s_out[1], 16 * (NS // 2))


_INS = ["x", "src", "dst", "L0_gnn_W", "L0_gnn_Wl", "L0_gnn_Wr", "L0_gnn_b", "L0_mix_w_qkv", "L0_mix_mem_kv", "L0_mix_w_out",
        "L0_mix_b_out", "L0_mix_g_out", "L0_mix_g_pre", "L0_ffn_router_w", "L0_ffn_w1", "L0_ffn_b1", "L0_ffn_w2", "L0_ffn_b2"]
_OUTS = [((6250, 256), "float32")]


def kernel(**inputs):
    import numpy as _np
    import concourse.bacc as _bacc
    from concourse import mybir as _mybir
    from concourse.bass_utils import run_bass_kernel_spmd as _run

    nc = _bacc.Bacc("TRN2", target_bir_lowering=False, num_devices=1)
    arrays, args = {}, []
    for name in _INS:
        a = _np.ascontiguousarray(inputs[name])
        arrays[f"in_{name}_dram"] = a
        args.append(nc.dram_tensor(f"in_{name}_dram", a.shape, _mybir.dt.from_np(a.dtype), kind="ExternalInput").ap())
    for i, (shape, dtype) in enumerate(_OUTS):
        dt = _mybir.dt.from_np(_np.dtype(dtype))
        args.append(nc.dram_tensor(f"out_{i}_dram", shape, dt, kind="ExternalOutput").ap())
    gps_layer(nc, *args)
    r = _run(nc, [arrays], core_ids=[0])
    return r.results[0]["out_0_dram"]
```
